# Optimizing a Trainium2 kernel written in Bass

```python
import numpy as np
import jax
import jax.numpy as jnp

def _softmax(x, axis=-1):
    return jax.nn.softmax(x, axis=axis)

def _gelu(x):
    return jax.nn.gelu(x, approximate=True)

def _silu(x):
    return jax.nn.silu(x)

def _sigmoid(x):
    return jax.nn.sigmoid(x)

def _layernorm(x, axis=-1, eps=1e-05):
    m = jnp.mean(x, axis=axis, keepdims=True)
    v = jnp.var(x, axis=axis, keepdims=True)
    return (x - m) / jnp.sqrt(v + eps)

def _scatter_add(tgt, idx, src, axis=0):
    return tgt.at[idx].add(src)

def _segment_sum(src, seg, n):
    return jax.ops.segment_sum(src, seg, n)
kernel_name = 'mk_decoder_preln_d4_seqx_r8_fff657'

def setup_inputs(seed: int=0):
    np.random.seed(seed)
    _w = jnp.asarray

    def _rec_inputs():
        import jax
        import jax.numpy as jnp
        _rk = jax.random.key(seed)
        x = 7.22e-05 + 1 * jax.random.normal(jax.random.fold_in(_rk, 1), (16, 128, 128), jnp.float32)
        _lenS = 128 - jax.random.randint(jax.random.fold_in(_rk, 7), (16,), 0, max(1, 128 // 4) + 1, jnp.int32)
        _lenS2 = 128 - jax.random.randint(jax.random.fold_in(_rk, 8), (16,), 0, max(1, 128 // 4) + 1, jnp.int32)
        _ctx_768P = jax.random.normal(jax.random.fold_in(_rk, 11), (16, 16, 96), jnp.float32)
        _ctx_768c = jax.random.dirichlet(jax.random.fold_in(_rk, 511), 0.3 * jnp.ones((16,), jnp.float32), (16, 128))
        _ctx_768t = jnp.einsum('bsk,bkd->bsd', _ctx_768c, _ctx_768P)
        _ctx_768t = _ctx_768t * jax.lax.rsqrt(jnp.mean(jnp.square(_ctx_768t)) + 1e-12) * 0.953939
        ctx_768 = -0.000191848 + 0.999787 * (_ctx_768t + 0.3 * jax.random.normal(jax.random.fold_in(_rk, 611), (16, 128, 96), jnp.float32))
        return (x, ctx_768)
    x, ctx_768 = _rec_inputs()

    def _L0_attn_setup():
        import jax, jax.numpy as jnp
        import numpy as np
        B, T, E, H = (2, 256, 128, 4)
        Dk = E // H
        Dv = Dk * 2
        EPS = 1e-05
        ROPE_BASE = 10000.0

        def _rotary(q, k):
            d = q.shape[-1]
            inv_freq = 1.0 / ROPE_BASE ** (jnp.arange(0, d, 2, dtype=jnp.float32) / d)
            t = jnp.arange(q.shape[1], dtype=jnp.float32)
            freqs = jnp.einsum('t,f->tf', t, inv_freq)
            cos = jnp.cos(freqs)[None, :, None, :]
            sin = jnp.sin(freqs)[None, :, None, :]

            def rot(x):
                x1, x2 = (x[..., :d // 2], x[..., d // 2:])
                return jnp.concatenate([x1 * cos - x2 * sin, x2 * cos + x1 * sin], axis=-1)
            return (rot(q), rot(k))
        key = jax.random.key(seed)
        ks = jax.random.split(key, 7)
        s = 0.02
        return {'x': jax.random.normal(ks[0], (B, T, E), jnp.float32), 'Wq': jax.random.normal(ks[1], (E, E), jnp.float32) * s, 'Wk': jax.random.normal(ks[2], (E, E), jnp.float32) * s, 'Wv': jax.random.normal(ks[3], (E, 2 * E), jnp.float32) * s, 'Wg': jax.random.normal(ks[4], (E, 2 * E), jnp.float32) * s, 'Wo': jax.random.normal(ks[5], (2 * E, E), jnp.float32) * s, 'gn_weight': jnp.ones((Dv,), jnp.float32)}
    _L0_attn_all = _L0_attn_setup()
    _L0_attn_in = {k: v for k, v in _L0_attn_all.items() if k in ('Wq', 'Wk', 'Wv', 'Wg', 'Wo', 'gn_weight')}
    del _L0_attn_all

    def _L0_xattn_setup():
        import jax, jax.numpy as jnp
        import numpy as np
        N_HEADS = 16
        key = jax.random.key(seed)
        ks = jax.random.split(key, 8)
        b, l, m = (8, 128, 128)
        d_embed, d_cross = (128, 96)
        s_q = 1.0 / np.sqrt(d_embed)
        s_kv = 1.0 / np.sqrt(d_cross)
        return {'x': jax.random.normal(ks[0], (b, l, d_embed), jnp.float32), 'y': jax.random.normal(ks[1], (b, m, d_cross), jnp.float32), 'Wq': jax.random.normal(ks[2], (d_embed, d_embed), jnp.float32) * s_q, 'bq': jax.random.normal(ks[3], (d_embed,), jnp.float32) * 0.01, 'Wkv': jax.random.normal(ks[4], (2 * d_embed, d_cross), jnp.float32) * s_kv, 'bkv': jax.random.normal(ks[5], (2 * d_embed,), jnp.float32) * 0.01, 'Wo': jax.random.normal(ks[6], (d_embed, d_embed), jnp.float32) * s_q, 'bo': jax.random.normal(ks[7], (d_embed,), jnp.float32) * 0.01}
    _L0_xattn_all = _L0_xattn_setup()
    _L0_xattn_in = {k: v for k, v in _L0_xattn_all.items() if k in ('Wq', 'bq', 'Wkv', 'bkv', 'Wo', 'bo')}
    del _L0_xattn_all

    def _L0_ffn_setup():
        import jax, jax.numpy as jnp
        import numpy as np
        EPS = 1e-05

        def _layernorm(x, w, b):
            mu = jnp.mean(x, axis=-1, keepdims=True)
            var = jnp.mean((x - mu) ** 2, axis=-1, keepdims=True)
            return (x - mu) * jax.lax.rsqrt(var + EPS) * w + b

        def _rope_tables(T, D, base=10000.0):
            inv_freq = 1.0 / base ** (jnp.arange(0, D, 2, dtype=jnp.float32) / D)
            t = jnp.arange(T, dtype=jnp.float32)
            freqs = jnp.einsum('i,j->ij', t, inv_freq)
            emb = jnp.concatenate([freqs, freqs], axis=-1)
            return (jnp.cos(emb), jnp.sin(emb))

        def _rotate_half(x):
            x1, x2 = (x[..., :x.shape[-1] // 2], x[..., x.shape[-1] // 2:])
            return jnp.concatenate([-x2, x1], axis=-1)

        def _attn(x, ln_w, ln_b, conv_w, attn_w, proj_w, n_head):
            B, T, C = x.shape
            D = C // n_head
            h = _layernorm(x, ln_w, ln_b)
            hc = jnp.transpose(h, (0, 2, 1))
            hc = jnp.pad(hc, ((0, 0), (0, 0), (2, 0)))
            hc = jax.lax.conv_general_dilated(hc, conv_w, window_strides=(1,), padding='VALID', dimension_numbers=('NCH', 'OIH', 'NCH'), feature_group_count=C)
            h = jnp.transpose(hc, (0, 2, 1))
            qkv = h @ attn_w
            q, k, v = jnp.split(qkv, 3, axis=-1)
            q = q.reshape(B, T, n_head, D)
            k = k.reshape(B, T, n_head, D)
            v = v.reshape(B, T, n_head, D)
            cos, sin = _rope_tables(T, D)
            cos = cos[None, :, None, :]
            sin = sin[None, :, None, :]
            q = q * cos + _rotate_half(q) * sin
            k = k * cos + _rotate_half(k) * sin
            scores = jnp.einsum('bqhd,bkhd->bhqk', q, k) / jnp.sqrt(jnp.float32(D))
            causal = jnp.tril(jnp.ones((T, T), dtype=bool))
            scores = jnp.where(causal, scores, jnp.float32(-1e+30))
            p = jax.nn.softmax(scores, axis=-1)
            y = jnp.einsum('bhqk,bkhd->bqhd', p, v).reshape(B, T, C)
            return y @ proj_w

        def _moe(x, ln_w, ln_b, router_w, expert_wv, expert_proj):
            h = _layernorm(x, ln_w, ln_b)
            logits = h @ router_w
            expert_idx = jnp.argmax(logits, axis=-1)
            E = router_w.shape[-1]
            out = jnp.zeros_like(x)
            for e in range(E):
                gv = h @ expert_wv[e]
                gate_raw, value = jnp.split(gv, 2, axis=-1)
                y = gate_raw * jax.nn.sigmoid(gate_raw) * value @ expert_proj[e]
                out = out + jnp.where((expert_idx == e)[..., None], y, 0.0)
            return out
        C, H, E, B, T = (128, 16, 4, 4, 128)
        Dff = 4 * C
        key = jax.random.key(seed)
        ks = jax.random.split(key, 8)
        s = 0.02
        return {'x': jax.random.normal(ks[0], (B, T, C), dtype=jnp.float32), 'ln1_w': jnp.ones((C,), jnp.float32), 'ln1_b': jnp.zeros((C,), jnp.float32), 'ln2_w': jnp.ones((C,), jnp.float32), 'ln2_b': jnp.zeros((C,), jnp.float32), 'conv_w': jax.random.normal(ks[1], (C, 1, 3), dtype=jnp.float32) * 0.1, 'attn_w': jax.random.normal(ks[2], (C, 3 * C), dtype=jnp.float32) * s, 'proj_w': jax.random.normal(ks[3], (C, C), dtype=jnp.float32) * s, 'router_w': jax.random.normal(ks[4], (C, E), dtype=jnp.float32) * s, 'expert_wv': jax.random.normal(ks[5], (E, C, 2 * Dff), dtype=jnp.float32) * s, 'expert_proj': jax.random.normal(ks[6], (E, Dff, C), dtype=jnp.float32) * s}
    _L0_ffn_all = _L0_ffn_setup()
    _L0_ffn_in = {k: v for k, v in _L0_ffn_all.items() if k in ('ln1_w', 'ln1_b', 'ln2_w', 'ln2_b', 'conv_w', 'attn_w', 'proj_w', 'router_w', 'expert_wv', 'expert_proj')}
    del _L0_ffn_all

    def _L1_attn_setup():
        import jax, jax.numpy as jnp
        import numpy as np
        N_LAYER = 12
        N_HEAD = 16
        N_EMBD = 128
        key = jax.random.key(seed)
        k0, k1, k2 = jax.random.split(key, 3)
        B, T, C = (4, 256, N_EMBD)
        inputs_embeds = jax.random.normal(k0, (B, T, C), dtype=jnp.float32)
        Wqkv = jax.random.normal(k1, (N_LAYER, 3 * C, C), dtype=jnp.float32) * 0.0002
        bqkv = jnp.zeros((N_LAYER, 3 * C), dtype=jnp.float32)
        Wproj = jax.random.normal(k2, (N_LAYER, C, C), dtype=jnp.float32) * 0.0002
        bproj = jnp.zeros((N_LAYER, C), dtype=jnp.float32)
        return {'inputs_embeds': inputs_embeds, 'Wqkv': Wqkv, 'bqkv': bqkv, 'Wproj': Wproj, 'bproj': bproj}
    _L1_attn_all = _L1_attn_setup()
    _L1_attn_in = {k: v for k, v in _L1_attn_all.items() if k in ('Wqkv', 'bqkv', 'Wproj', 'bproj')}
    del _L1_attn_all

    def _L1_xattn_setup():
        import jax, jax.numpy as jnp
        import numpy as np
        Q_DIM = 128
        KV_DIM = 96
        HEADS = 16
        DK = Q_DIM // HEADS
        key = jax.random.key(seed)
        ks = jax.random.split(key, 6)
        B, T_q, T_kv = (4, 256, 256)
        s_q = 1.0 / np.sqrt(Q_DIM)
        s_kv = 1.0 / np.sqrt(KV_DIM)
        return {'q_tokens': jax.random.normal(ks[0], (B, T_q, Q_DIM), jnp.float32), 'kv_tokens': jax.random.normal(ks[1], (B, T_kv, KV_DIM), jnp.float32), 'Wq': jax.random.normal(ks[2], (Q_DIM, Q_DIM), jnp.float32) * s_q, 'Wk': jax.random.normal(ks[3], (Q_DIM, KV_DIM), jnp.float32) * s_kv, 'Wv': jax.random.normal(ks[4], (Q_DIM, KV_DIM), jnp.float32) * s_kv, 'Wo': jax.random.normal(ks[5], (Q_DIM, Q_DIM), jnp.float32) * s_q}
    _L1_xattn_all = _L1_xattn_setup()
    _L1_xattn_in = {k: v for k, v in _L1_xattn_all.items() if k in ('Wq', 'Wk', 'Wv', 'Wo')}
    del _L1_xattn_all

    def _L1_ffn_setup():
        import jax, jax.numpy as jnp
        import numpy as np
        TOP_K = 2
        key = jax.random.key(seed)
        ks = jax.random.split(key, 6)
        B, T, H, E, F = (2, 256, 128, 8, 512)
        s = 0.02
        return {'hidden_states': jax.random.normal(ks[0], (B, T, H), dtype=jnp.float32), 'router_w': jax.random.normal(ks[1], (E, H), dtype=jnp.float32) * s, 'w1': jax.random.normal(ks[2], (E, F, H), dtype=jnp.float32) * s, 'b1': jax.random.normal(ks[3], (E, F), dtype=jnp.float32) * s, 'w2': jax.random.normal(ks[4], (E, H, F), dtype=jnp.float32) * s, 'b2': jax.random.normal(ks[5], (E, H), dtype=jnp.float32) * s}
    _L1_ffn_all = _L1_ffn_setup()
    _L1_ffn_in = {k: v for k, v in _L1_ffn_all.items() if k in ('router_w', 'w1', 'b1', 'w2', 'b2')}
    del _L1_ffn_all

    def _L2_attn_setup():
        import jax, jax.numpy as jnp
        import numpy as np
        HEADS = 16
        D_MODEL = 128
        D_K = D_MODEL // HEADS
        SEQ = 256
        BSZ = 2

        def softmax_one(x, axis):
            x = x - jnp.max(x, axis=axis, keepdims=True)
            ex = jnp.exp(x)
            return ex / (1.0 + jnp.sum(ex, axis=axis, keepdims=True))
        key = jax.random.key(seed)
        ks = jax.random.split(key, 7)
        s = 1.0 / np.sqrt(D_MODEL)
        return {'x': jax.random.normal(ks[0], (SEQ, BSZ, D_MODEL), dtype=jnp.float32), 'Wq': jax.random.normal(ks[1], (D_MODEL, D_MODEL), dtype=jnp.float32) * s, 'bq': jnp.zeros((D_MODEL,), dtype=jnp.float32), 'Wk': jax.random.normal(ks[2], (D_MODEL, D_MODEL), dtype=jnp.float32) * s, 'bk': jnp.zeros((D_MODEL,), dtype=jnp.float32), 'Wv': jax.random.normal(ks[3], (D_MODEL, D_MODEL), dtype=jnp.float32) * s, 'bv': jnp.zeros((D_MODEL,), dtype=jnp.float32)}
    _L2_attn_all = _L2_attn_setup()
    _L2_attn_in = {k: v for k, v in _L2_attn_all.items() if k in ('Wq', 'bq', 'Wk', 'bk', 'Wv', 'bv')}
    del _L2_attn_all

    def _L2_xattn_setup():
        import jax, jax.numpy as jnp
        import numpy as np
        IN_DIM = 128
        CTX_DIM = 96
        NUM_HEADS = 16
        HEAD_DIM = IN_DIM // NUM_HEADS
        SCALE = 1.0 / float(np.sqrt(HEAD_DIM))
        key = jax.random.key(seed)
        ks = jax.random.split(key, 10)
        B, NQ, NKV = (8, 128, 64)
        s_in = 1.0 / float(np.sqrt(IN_DIM))
        s_ctx = 1.0 / float(np.sqrt(CTX_DIM))
        return {'x': jax.random.normal(ks[0], (B, NQ, IN_DIM), dtype=jnp.float32), 'context': jax.random.normal(ks[1], (B, NKV, CTX_DIM), dtype=jnp.float32), 'Wq': jax.random.normal(ks[2], (IN_DIM, IN_DIM), dtype=jnp.float32) * s_in, 'bq': jax.random.normal(ks[3], (IN_DIM,), dtype=jnp.float32) * 0.01, 'Wk': jax.random.normal(ks[4], (IN_DIM, CTX_DIM), dtype=jnp.float32) * s_ctx, 'bk': jax.random.normal(ks[5], (IN_DIM,), dtype=jnp.float32) * 0.01, 'Wv': jax.random.normal(ks[6], (IN_DIM, CTX_DIM), dtype=jnp.float32) * s_ctx, 'bv': jax.random.normal(ks[7], (IN_DIM,), dtype=jnp.float32) * 0.01, 'Wo': jax.random.normal(ks[8], (IN_DIM, IN_DIM), dtype=jnp.float32) * s_in, 'bo': jax.random.normal(ks[9], (IN_DIM,), dtype=jnp.float32) * 0.01}
    _L2_xattn_all = _L2_xattn_setup()
    _L2_xattn_in = {k: v for k, v in _L2_xattn_all.items() if k in ('Wq', 'bq', 'Wk', 'bk', 'Wv', 'bv', 'Wo', 'bo')}
    del _L2_xattn_all

    def _L2_ffn_setup():
        import jax, jax.numpy as jnp
        import numpy as np
        B, S, H, E, K = (2, 128, 128, 8, 2)
        F = 4 * H
        key = jax.random.key(seed)
        ks = jax.random.split(key, 8)
        std = 0.02
        return {'x': jax.random.normal(ks[0], (B, S, H), jnp.float32), 'gate_w': jax.random.normal(ks[1], (E, H), jnp.float32) * (std / np.sqrt(H)), 'gate_bias': jnp.zeros((E,), jnp.float32), 'Wu': jax.random.normal(ks[2], (E, F, H), jnp.float32) * std, 'bu': jnp.zeros((E, F), jnp.float32), 'Wd': jax.random.normal(ks[3], (E, H, F), jnp.float32) * std, 'bd': jnp.zeros((E, H), jnp.float32), 'sWu': jax.random.normal(ks[4], (F, H), jnp.float32) * std, 'sbu': jnp.zeros((F,), jnp.float32), 'sWd': jax.random.normal(ks[5], (H, F), jnp.float32) * std, 'sbd': jnp.zeros((H,), jnp.float32)}
    _L2_ffn_all = _L2_ffn_setup()
    _L2_ffn_in = {k: v for k, v in _L2_ffn_all.items() if k in ('gate_w', 'gate_bias', 'Wu', 'bu', 'Wd', 'bd', 'sWu', 'sbu', 'sWd', 'sbd')}
    del _L2_ffn_all

    def _L3_attn_setup():
        import jax, jax.numpy as jnp
        import numpy as np
        L = 2
        D = 128
        H = 8
        DK = D // H
        DV = D // H
        T = 256
        B = 4
        INTER = 352
        EPS = 1e-06

        def rmsnorm(x, w):
            return x * jax.lax.rsqrt(jnp.mean(x * x, axis=-1, keepdims=True) + EPS) * w

        def l2norm(x):
            return x * jax.lax.rsqrt(jnp.sum(x * x, axis=-1, keepdims=True) + EPS)

        def delta_attn(x, Wq, Wk, Wv, Wb, Wo, onorm_w):
            b, t, _ = x.shape
            q = jax.nn.silu((x @ Wq).reshape(b, t, H, DK))
            k = jax.nn.silu((x @ Wk).reshape(b, t, H, DK))
            q = l2norm(q)
            k = l2norm(k)
            v = jax.nn.silu((x @ Wv).reshape(b, t, H, DV))
            beta = jax.nn.sigmoid(x @ Wb) * 2.0
            qt = q.transpose(1, 0, 2, 3)
            kt = k.transpose(1, 0, 2, 3)
            vt = v.transpose(1, 0, 2, 3)
            bt = beta.transpose(1, 0, 2)

            def step(S, inps):
                qi, ki, vi, bi = inps
                pred = jnp.einsum('bhkv,bhk->bhv', S, ki)
                S = S + bi[..., None, None] * ki[..., :, None] * (vi - pred)[..., None, :]
                o = jnp.einsum('bhkv,bhk->bhv', S, qi)
                return (S, o)
            S0 = jnp.zeros((b, H, DK, DV), x.dtype)
            _, o = jax.lax.scan(step, S0, (qt, kt, vt, bt))
            o = rmsnorm(o, onorm_w)
            o = o.transpose(1, 0, 2, 3).reshape(b, t, H * DV)
            return o @ Wo
        key = jax.random.key(seed)
        ks = jax.random.split(key, 13)
        s = 0.02
        f32 = jnp.float32
        return {'input_embeds': jax.random.normal(ks[0], (T, B, D), f32), 'Wq': jax.random.normal(ks[1], (L, D, D), f32) * s, 'Wk': jax.random.normal(ks[2], (L, D, D), f32) * s, 'Wv': jax.random.normal(ks[3], (L, D, D), f32) * s, 'Wb': jax.random.normal(ks[4], (L, D, H), f32) * s, 'Wo': jax.random.normal(ks[5], (L, D, D), f32) * s, 'onorm_w': jnp.ones((L, DV), f32) + jax.random.normal(ks[6], (L, DV), f32) * 0.02, 'norm1_w': jnp.ones((L, D), f32) + jax.random.normal(ks[7], (L, D), f32) * 0.02, 'norm2_w': jnp.ones((L, D), f32) + jax.random.normal(ks[8], (L, D), f32) * 0.02, 'Wg': jax.random.normal(ks[9], (L, D, 2 * INTER), f32) * s, 'Wd': jax.random.normal(ks[10], (L, INTER, D), f32) * s, 'final_norm_w': jnp.ones((D,), f32) + jax.random.normal(ks[11], (D,), f32) * 0.02}
    _L3_attn_all = _L3_attn_setup()
    _L3_attn_in = {k: v for k, v in _L3_attn_all.items() if k in ('Wq', 'Wk', 'Wv', 'Wb', 'Wo', 'onorm_w', 'norm1_w', 'norm2_w', 'Wg', 'Wd', 'final_norm_w')}
    del _L3_attn_all

    def _L3_xattn_setup():
        import jax, jax.numpy as jnp
        import numpy as np
        IMG_DIM, TXT_DIM, HID = (128, 96, 128)
        B, LQ, LK = (8, 256, 256)
        key = jax.random.key(seed)
        ks = jax.random.split(key, 8)
        s_img = 1.0 / np.sqrt(IMG_DIM)
        s_txt = 1.0 / np.sqrt(TXT_DIM)
        return {'image_features': jax.random.normal(ks[0], (B, LQ, IMG_DIM), jnp.float32), 'text_features': jax.random.normal(ks[1], (B, LK, TXT_DIM), jnp.float32), 'Wq': jax.random.uniform(ks[2], (IMG_DIM, HID), jnp.float32, -s_img, s_img), 'bq': jax.random.uniform(ks[3], (HID,), jnp.float32, -s_img, s_img), 'Wk': jax.random.uniform(ks[4], (TXT_DIM, HID), jnp.float32, -s_txt, s_txt), 'bk': jax.random.uniform(ks[5], (HID,), jnp.float32, -s_txt, s_txt), 'Wv': jax.random.uniform(ks[6], (TXT_DIM, HID), jnp.float32, -s_txt, s_txt), 'bv': jax.random.uniform(ks[7], (HID,), jnp.float32, -s_txt, s_txt)}
    _L3_xattn_all = _L3_xattn_setup()
    _L3_xattn_in = {k: v for k, v in _L3_xattn_all.items() if k in ('Wq', 'bq', 'Wk', 'bk', 'Wv', 'bv')}
    del _L3_xattn_all

    def _L3_ffn_setup():
        import jax, jax.numpy as jnp
        import numpy as np
        EPS = 1e-12

        def rms_norm(t, gamma):
            n = jnp.maximum(jnp.linalg.norm(t, axis=-1, keepdims=True), EPS)
            scale = jnp.sqrt(jnp.asarray(t.shape[-1], t.dtype))
            return t / n * scale * gamma
        key = jax.random.key(seed)
        ks = jax.random.split(key, 4)
        b, s, d = (4, 512, 128)
        e, t = (8, 64)
        hidden = 4 * d
        return {'x': jax.random.normal(ks[0], (b, s, d), dtype=jnp.float32), 'gamma_x': jnp.ones((d,), dtype=jnp.float32), 'gamma_slot': jnp.ones((d,), dtype=jnp.float32), 'slot_embeds': jax.random.normal(ks[1], (e, t, d), dtype=jnp.float32), 'w1': jax.random.normal(ks[2], (d, hidden), dtype=jnp.float32) * (1.0 / np.sqrt(d)), 'w2': jax.random.normal(ks[3], (hidden, d), dtype=jnp.float32) * (1.0 / np.sqrt(hidden))}
    _L3_ffn_all = _L3_ffn_setup()
    _L3_ffn_in = {k: v for k, v in _L3_ffn_all.items() if k in ('gamma_x', 'gamma_slot', 'slot_embeds', 'w1', 'w2')}
    del _L3_ffn_all
    return {'x': x, 'ctx_768': ctx_768, 'L0_attn_Wq': _L0_attn_in['Wq'], 'L0_attn_Wk': _L0_attn_in['Wk'], 'L0_attn_Wv': _L0_attn_in['Wv'], 'L0_attn_Wg': _L0_attn_in['Wg'], 'L0_attn_Wo': _L0_attn_in['Wo'], 'L0_attn_gn_weight': _L0_attn_in['gn_weight'], 'L0_xattn_Wq': _L0_xattn_in['Wq'], 'L0_xattn_bq': _L0_xattn_in['bq'], 'L0_xattn_Wkv': _L0_xattn_in['Wkv'], 'L0_xattn_bkv': _L0_xattn_in['bkv'], 'L0_xattn_Wo': _L0_xattn_in['Wo'], 'L0_xattn_bo': _L0_xattn_in['bo'], 'L0_ffn_ln1_w': _L0_ffn_in['ln1_w'], 'L0_ffn_ln1_b': _L0_ffn_in['ln1_b'], 'L0_ffn_ln2_w': _L0_ffn_in['ln2_w'], 'L0_ffn_ln2_b': _L0_ffn_in['ln2_b'], 'L0_ffn_conv_w': _L0_ffn_in['conv_w'], 'L0_ffn_attn_w': _L0_ffn_in['attn_w'], 'L0_ffn_proj_w': _L0_ffn_in['proj_w'], 'L0_ffn_router_w': _L0_ffn_in['router_w'], 'L0_ffn_expert_wv': _L0_ffn_in['expert_wv'], 'L0_ffn_expert_proj': _L0_ffn_in['expert_proj'], 'L1_attn_Wqkv': _L1_attn_in['Wqkv'], 'L1_attn_bqkv': _L1_attn_in['bqkv'], 'L1_attn_Wproj': _L1_attn_in['Wproj'], 'L1_attn_bproj': _L1_attn_in['bproj'], 'L1_xattn_Wq': _L1_xattn_in['Wq'], 'L1_xattn_Wk': _L1_xattn_in['Wk'], 'L1_xattn_Wv': _L1_xattn_in['Wv'], 'L1_xattn_Wo': _L1_xattn_in['Wo'], 'L1_ffn_router_w': _L1_ffn_in['router_w'], 'L1_ffn_w1': _L1_ffn_in['w1'], 'L1_ffn_b1': _L1_ffn_in['b1'], 'L1_ffn_w2': _L1_ffn_in['w2'], 'L1_ffn_b2': _L1_ffn_in['b2'], 'L2_attn_Wq': _L2_attn_in['Wq'], 'L2_attn_bq': _L2_attn_in['bq'], 'L2_attn_Wk': _L2_attn_in['Wk'], 'L2_attn_bk': _L2_attn_in['bk'], 'L2_attn_Wv': _L2_attn_in['Wv'], 'L2_attn_bv': _L2_attn_in['bv'], 'L2_xattn_Wq': _L2_xattn_in['Wq'], 'L2_xattn_bq': _L2_xattn_in['bq'], 'L2_xattn_Wk': _L2_xattn_in['Wk'], 'L2_xattn_bk': _L2_xattn_in['bk'], 'L2_xattn_Wv': _L2_xattn_in['Wv'], 'L2_xattn_bv': _L2_xattn_in['bv'], 'L2_xattn_Wo': _L2_xattn_in['Wo'], 'L2_xattn_bo': _L2_xattn_in['bo'], 'L2_ffn_gate_w': _L2_ffn_in['gate_w'], 'L2_ffn_gate_bias': _L2_ffn_in['gate_bias'], 'L2_ffn_Wu': _L2_ffn_in['Wu'], 'L2_ffn_bu': _L2_ffn_in['bu'], 'L2_ffn_Wd': _L2_ffn_in['Wd'], 'L2_ffn_bd': _L2_ffn_in['bd'], 'L2_ffn_sWu': _L2_ffn_in['sWu'], 'L2_ffn_sbu': _L2_ffn_in['sbu'], 'L2_ffn_sWd': _L2_ffn_in['sWd'], 'L2_ffn_sbd': _L2_ffn_in['sbd'], 'L3_attn_Wq': _L3_attn_in['Wq'], 'L3_attn_Wk': _L3_attn_in['Wk'], 'L3_attn_Wv': _L3_attn_in['Wv'], 'L3_attn_Wb': _L3_attn_in['Wb'], 'L3_attn_Wo': _L3_attn_in['Wo'], 'L3_attn_onorm_w': _L3_attn_in['onorm_w'], 'L3_attn_norm1_w': _L3_attn_in['norm1_w'], 'L3_attn_norm2_w': _L3_attn_in['norm2_w'], 'L3_attn_Wg': _L3_attn_in['Wg'], 'L3_attn_Wd': _L3_attn_in['Wd'], 'L3_attn_final_norm_w': _L3_attn_in['final_norm_w'], 'L3_xattn_Wq': _L3_xattn_in['Wq'], 'L3_xattn_bq': _L3_xattn_in['bq'], 'L3_xattn_Wk': _L3_xattn_in['Wk'], 'L3_xattn_bk': _L3_xattn_in['bk'], 'L3_xattn_Wv': _L3_xattn_in['Wv'], 'L3_xattn_bv': _L3_xattn_in['bv'], 'L3_ffn_gamma_x': _L3_ffn_in['gamma_x'], 'L3_ffn_gamma_slot': _L3_ffn_in['gamma_slot'], 'L3_ffn_slot_embeds': _L3_ffn_in['slot_embeds'], 'L3_ffn_w1': _L3_ffn_in['w1'], 'L3_ffn_w2': _L3_ffn_in['w2']}

def reference(x, ctx_768, L0_attn_Wq, L0_attn_Wk, L0_attn_Wv, L0_attn_Wg, L0_attn_Wo, L0_attn_gn_weight, L0_xattn_Wq, L0_xattn_bq, L0_xattn_Wkv, L0_xattn_bkv, L0_xattn_Wo, L0_xattn_bo, L0_ffn_ln1_w, L0_ffn_ln1_b, L0_ffn_ln2_w, L0_ffn_ln2_b, L0_ffn_conv_w, L0_ffn_attn_w, L0_ffn_proj_w, L0_ffn_router_w, L0_ffn_expert_wv, L0_ffn_expert_proj, L1_attn_Wqkv, L1_attn_bqkv, L1_attn_Wproj, L1_attn_bproj, L1_xattn_Wq, L1_xattn_Wk, L1_xattn_Wv, L1_xattn_Wo, L1_ffn_router_w, L1_ffn_w1, L1_ffn_b1, L1_ffn_w2, L1_ffn_b2, L2_attn_Wq, L2_attn_bq, L2_attn_Wk, L2_attn_bk, L2_attn_Wv, L2_attn_bv, L2_xattn_Wq, L2_xattn_bq, L2_xattn_Wk, L2_xattn_bk, L2_xattn_Wv, L2_xattn_bv, L2_xattn_Wo, L2_xattn_bo, L2_ffn_gate_w, L2_ffn_gate_bias, L2_ffn_Wu, L2_ffn_bu, L2_ffn_Wd, L2_ffn_bd, L2_ffn_sWu, L2_ffn_sbu, L2_ffn_sWd, L2_ffn_sbd, L3_attn_Wq, L3_attn_Wk, L3_attn_Wv, L3_attn_Wb, L3_attn_Wo, L3_attn_onorm_w, L3_attn_norm1_w, L3_attn_norm2_w, L3_attn_Wg, L3_attn_Wd, L3_attn_final_norm_w, L3_xattn_Wq, L3_xattn_bq, L3_xattn_Wk, L3_xattn_bk, L3_xattn_Wv, L3_xattn_bv, L3_ffn_gamma_x, L3_ffn_gamma_slot, L3_ffn_slot_embeds, L3_ffn_w1, L3_ffn_w2):
    import jax
    import jax.numpy as jnp

    def _L0_attn_ref(x, Wq, Wk, Wv, Wg, Wo, gn_weight):
        import jax, jax.numpy as jnp
        import numpy as np
        B, T, E, H = (2, 256, 128, 4)
        Dk = E // H
        Dv = Dk * 2
        EPS = 1e-05
        ROPE_BASE = 10000.0

        def _rotary(q, k):
            d = q.shape[-1]
            inv_freq = 1.0 / ROPE_BASE ** (jnp.arange(0, d, 2, dtype=jnp.float32) / d)
            t = jnp.arange(q.shape[1], dtype=jnp.float32)
            freqs = jnp.einsum('t,f->tf', t, inv_freq)
            cos = jnp.cos(freqs)[None, :, None, :]
            sin = jnp.sin(freqs)[None, :, None, :]

            def rot(x):
                x1, x2 = (x[..., :d // 2], x[..., d // 2:])
                return jnp.concatenate([x1 * cos - x2 * sin, x2 * cos + x1 * sin], axis=-1)
            return (rot(q), rot(k))
        b, t, e = x.shape
        q = (x @ Wq).reshape(b, t, H, Dk)
        k = (x @ Wk).reshape(b, t, H, Dk)
        q, k = _rotary(q, k)
        q = q.transpose(0, 2, 1, 3) * Dk ** (-0.5)
        k = k.transpose(0, 2, 1, 3)
        v = (x @ Wv).reshape(b, t, H, Dv).transpose(0, 2, 1, 3)
        gamma = 1.0 - jnp.exp2(-5.0 - jnp.arange(H, dtype=jnp.float32))
        ti = jnp.arange(t)
        n = ti[:, None] - ti[None, :]
        decay = jnp.where(n >= 0, gamma[:, None, None] ** jnp.maximum(n, 0).astype(jnp.float32), 0.0)
        scores = jnp.einsum('bhtd,bhsd->bhts', q, k) * decay[None]
        o = jnp.einsum('bhts,bhsd->bhtd', scores, v)
        o = o.transpose(0, 2, 1, 3)
        rms = jnp.sqrt(jnp.mean(o * o, axis=-1, keepdims=True) + EPS)
        o = o / rms * gn_weight
        g = x @ Wg
        return o.reshape(b, t, H * Dv) * g @ Wo

    def _L0_xattn_ref(x, y, Wq, bq, Wkv, bkv, Wo, bo):
        import jax, jax.numpy as jnp
        import numpy as np
        N_HEADS = 16
        b, l, d = x.shape
        m = y.shape[1]
        h = N_HEADS
        dh = d // h
        q = (jnp.einsum('bld,ed->ble', x, Wq) + bq).reshape(b, l, h, dh)
        kv = (jnp.einsum('bmc,ec->bme', y, Wkv) + bkv).reshape(b, m, h, 2 * dh)
        k, v = (kv[..., :dh], kv[..., dh:])
        scale = 1.0 / jnp.sqrt(jnp.asarray(dh, x.dtype))
        att = jax.nn.softmax(jnp.einsum('blhd,bmhd->blmh', q, k) * scale, axis=2)
        out = jnp.einsum('blmh,bmhd->blhd', att, v).reshape(b, l, d)
        return jnp.einsum('bld,ed->ble', out, Wo) + bo

    def _L0_ffn_ref(x, ln1_w, ln1_b, ln2_w, ln2_b, conv_w, attn_w, proj_w, router_w, expert_wv, expert_proj):
        import jax, jax.numpy as jnp
        import numpy as np
        EPS = 1e-05

        def _layernorm(x, w, b):
            mu = jnp.mean(x, axis=-1, keepdims=True)
            var = jnp.mean((x - mu) ** 2, axis=-1, keepdims=True)
            return (x - mu) * jax.lax.rsqrt(var + EPS) * w + b

        def _rope_tables(T, D, base=10000.0):
            inv_freq = 1.0 / base ** (jnp.arange(0, D, 2, dtype=jnp.float32) / D)
            t = jnp.arange(T, dtype=jnp.float32)
            freqs = jnp.einsum('i,j->ij', t, inv_freq)
            emb = jnp.concatenate([freqs, freqs], axis=-1)
            return (jnp.cos(emb), jnp.sin(emb))

        def _rotate_half(x):
            x1, x2 = (x[..., :x.shape[-1] // 2], x[..., x.shape[-1] // 2:])
            return jnp.concatenate([-x2, x1], axis=-1)

        def _attn(x, ln_w, ln_b, conv_w, attn_w, proj_w, n_head):
            B, T, C = x.shape
            D = C // n_head
            h = _layernorm(x, ln_w, ln_b)
            hc = jnp.transpose(h, (0, 2, 1))
            hc = jnp.pad(hc, ((0, 0), (0, 0), (2, 0)))
            hc = jax.lax.conv_general_dilated(hc, conv_w, window_strides=(1,), padding='VALID', dimension_numbers=('NCH', 'OIH', 'NCH'), feature_group_count=C)
            h = jnp.transpose(hc, (0, 2, 1))
            qkv = h @ attn_w
            q, k, v = jnp.split(qkv, 3, axis=-1)
            q = q.reshape(B, T, n_head, D)
            k = k.reshape(B, T, n_head, D)
            v = v.reshape(B, T, n_head, D)
            cos, sin = _rope_tables(T, D)
            cos = cos[None, :, None, :]
            sin = sin[None, :, None, :]
            q = q * cos + _rotate_half(q) * sin
            k = k * cos + _rotate_half(k) * sin
            scores = jnp.einsum('bqhd,bkhd->bhqk', q, k) / jnp.sqrt(jnp.float32(D))
            causal = jnp.tril(jnp.ones((T, T), dtype=bool))
            scores = jnp.where(causal, scores, jnp.float32(-1e+30))
            p = jax.nn.softmax(scores, axis=-1)
            y = jnp.einsum('bhqk,bkhd->bqhd', p, v).reshape(B, T, C)
            return y @ proj_w

        def _moe(x, ln_w, ln_b, router_w, expert_wv, expert_proj):
            h = _layernorm(x, ln_w, ln_b)
            logits = h @ router_w
            expert_idx = jnp.argmax(logits, axis=-1)
            E = router_w.shape[-1]
            out = jnp.zeros_like(x)
            for e in range(E):
                gv = h @ expert_wv[e]
                gate_raw, value = jnp.split(gv, 2, axis=-1)
                y = gate_raw * jax.nn.sigmoid(gate_raw) * value @ expert_proj[e]
                out = out + jnp.where((expert_idx == e)[..., None], y, 0.0)
            return out
        n_head = 16
        x = x + _attn(x, ln1_w, ln1_b, conv_w, attn_w, proj_w, n_head)
        x = x + _moe(x, ln2_w, ln2_b, router_w, expert_wv, expert_proj)
        return x

    def _L1_attn_ref(inputs_embeds, Wqkv, bqkv, Wproj, bproj):
        import jax, jax.numpy as jnp
        import numpy as np
        N_LAYER = 12
        N_HEAD = 16
        N_EMBD = 128
        B, T, C = inputs_embeds.shape
        H = N_HEAD
        D = C // H
        scale = 1.0 / np.sqrt(D).astype(np.float32)
        x = inputs_embeds
        for i in range(N_LAYER):
            qkv = x @ Wqkv[i].T + bqkv[i]
            q, k, v = jnp.split(qkv, 3, axis=-1)
            q = q.reshape(B, T, H, D).transpose(0, 2, 1, 3)
            k = k.reshape(B, T, H, D).transpose(0, 2, 1, 3)
            v = v.reshape(B, T, H, D).transpose(0, 2, 1, 3)
            att = jnp.einsum('bhqd,bhkd->bhqk', q, k) * scale
            y = jnp.einsum('bhqk,bhkd->bhqd', att, v)
            y = y.transpose(0, 2, 1, 3).reshape(B, T, C)
            x = y @ Wproj[i].T + bproj[i] + x
        return x

    def _L1_xattn_ref(q_tokens, kv_tokens, Wq, Wk, Wv, Wo):
        import jax, jax.numpy as jnp
        import numpy as np
        Q_DIM = 128
        KV_DIM = 96
        HEADS = 16
        DK = Q_DIM // HEADS
        B, T_q, _ = q_tokens.shape
        T_kv = kv_tokens.shape[1]
        q = q_tokens @ Wq.T
        k = kv_tokens @ Wk.T
        v = kv_tokens @ Wv.T
        q = q.reshape(B, T_q, HEADS, DK).transpose(0, 2, 1, 3)
        k = k.reshape(B, T_kv, HEADS, DK).transpose(0, 2, 1, 3)
        v = v.reshape(B, T_kv, HEADS, DK).transpose(0, 2, 1, 3)
        scale = 1.0 / jnp.sqrt(jnp.asarray(DK, q.dtype))
        attn = jnp.einsum('bhqd,bhkd->bhqk', q, k) * scale
        attn = jax.nn.softmax(attn, axis=-1)
        out = jnp.einsum('bhqk,bhkd->bhqd', attn, v)
        out = out.transpose(0, 2, 1, 3).reshape(B, T_q, Q_DIM)
        return out @ Wo.T

    def _L1_ffn_ref(hidden_states, router_w, w1, b1, w2, b2):
        import jax, jax.numpy as jnp
        import numpy as np
        TOP_K = 2
        x = hidden_states
        router_logits = jnp.einsum('bth,eh->bte', x, router_w)
        topk_values, topk_indices = jax.lax.top_k(router_logits, TOP_K)
        topk_weights = jax.nn.softmax(topk_values.astype(jnp.float32), axis=-1).astype(x.dtype)
        h1 = jnp.einsum('bth,efh->btef', x, w1) + b1
        h1 = jax.nn.gelu(h1, approximate=False)
        expert_outputs = jnp.einsum('btef,ehf->bteh', h1, w2) + b2
        gather_idx = topk_indices[..., None]
        topk_expert_outputs = jnp.take_along_axis(expert_outputs, gather_idx, axis=2)
        mixed_output = jnp.sum(topk_expert_outputs * topk_weights[..., None], axis=2)
        return mixed_output

    def _L2_attn_ref(x, Wq, bq, Wk, bk, Wv, bv):
        import jax, jax.numpy as jnp
        import numpy as np
        HEADS = 16
        D_MODEL = 128
        D_K = D_MODEL // HEADS
        SEQ = 256
        BSZ = 2

        def softmax_one(x, axis):
            x = x - jnp.max(x, axis=axis, keepdims=True)
            ex = jnp.exp(x)
            return ex / (1.0 + jnp.sum(ex, axis=axis, keepdims=True))
        S, B, D = x.shape
        q = (x @ Wq.T + bq).reshape(S, B, HEADS, D_K)
        k = (x @ Wk.T + bk).reshape(S, B, HEADS, D_K)
        v = (x @ Wv.T + bv).reshape(S, B, HEADS, D_K)
        scores = jnp.einsum('ibhd,jbhd->ijbh', q, k) / np.sqrt(D_K).astype(np.float32)
        causal = jnp.tril(jnp.ones((S, S), dtype=bool))[:, :, None, None]
        scores = jnp.where(causal, scores, -jnp.inf)
        attn = softmax_one(scores, axis=1)
        out = jnp.einsum('ijbh,jbhd->ibhd', attn, v)
        return out.reshape(S, B, D)

    def _L2_xattn_ref(x, context, Wq, bq, Wk, bk, Wv, bv, Wo, bo):
        import jax, jax.numpy as jnp
        import numpy as np
        IN_DIM = 128
        CTX_DIM = 96
        NUM_HEADS = 16
        HEAD_DIM = IN_DIM // NUM_HEADS
        SCALE = 1.0 / float(np.sqrt(HEAD_DIM))
        q = x @ Wq.T + bq
        k = context @ Wk.T + bk
        v = context @ Wv.T + bv
        B, NQ, _ = q.shape
        NKV = k.shape[1]
        q = q.reshape(B, NQ, NUM_HEADS, HEAD_DIM)
        k = k.reshape(B, NKV, NUM_HEADS, HEAD_DIM)
        v = v.reshape(B, NKV, NUM_HEADS, HEAD_DIM)
        attn = jnp.einsum('bihd,bjhd->bhij', q, k) * SCALE
        attn = jax.nn.softmax(attn, axis=-1)
        out = jnp.einsum('bhij,bjhd->bihd', attn, v)
        out = out.reshape(B, NQ, IN_DIM)
        return out @ Wo.T + bo

    def _L2_ffn_ref(x, gate_w, gate_bias, Wu, bu, Wd, bd, sWu, sbu, sWd, sbd):
        import jax, jax.numpy as jnp
        import numpy as np
        B, S, H, E, K = (2, 128, 128, 8, 2)
        F = 4 * H
        b, s, h = x.shape
        x_flat = x.reshape(-1, h)
        T = x_flat.shape[0]
        scores = jax.nn.sigmoid(x_flat @ gate_w.T + gate_bias)
        top_scores, top_idx = jax.lax.top_k(scores, K)
        top_scores = top_scores / (top_scores.sum(-1, keepdims=True) + 1e-06)
        w = jnp.zeros((T, E), x.dtype).at[jnp.arange(T)[:, None], top_idx].add(top_scores)
        h1 = jnp.einsum('th,efh->etf', x_flat, Wu) + bu[:, None, :]
        a1 = jax.nn.gelu(h1, approximate=False)
        y = jnp.einsum('etf,ehf->eth', a1, Wd) + bd[:, None, :]
        combined = jnp.einsum('te,eth->th', w, y)
        sh = jax.nn.gelu(x_flat @ sWu.T + sbu, approximate=False)
        shared = (sh @ sWd.T + sbd) * 0.1
        return (combined + shared).reshape(b, s, h)

    def _L3_attn_ref(input_embeds, Wq, Wk, Wv, Wb, Wo, onorm_w, norm1_w, norm2_w, Wg, Wd, final_norm_w):
        import jax, jax.numpy as jnp
        import numpy as np
        L = 2
        D = 128
        H = 8
        DK = D // H
        DV = D // H
        T = 256
        B = 4
        INTER = 352
        EPS = 1e-06

        def rmsnorm(x, w):
            return x * jax.lax.rsqrt(jnp.mean(x * x, axis=-1, keepdims=True) + EPS) * w

        def l2norm(x):
            return x * jax.lax.rsqrt(jnp.sum(x * x, axis=-1, keepdims=True) + EPS)

        def delta_attn(x, Wq, Wk, Wv, Wb, Wo, onorm_w):
            b, t, _ = x.shape
            q = jax.nn.silu((x @ Wq).reshape(b, t, H, DK))
            k = jax.nn.silu((x @ Wk).reshape(b, t, H, DK))
            q = l2norm(q)
            k = l2norm(k)
            v = jax.nn.silu((x @ Wv).reshape(b, t, H, DV))
            beta = jax.nn.sigmoid(x @ Wb) * 2.0
            qt = q.transpose(1, 0, 2, 3)
            kt = k.transpose(1, 0, 2, 3)
            vt = v.transpose(1, 0, 2, 3)
            bt = beta.transpose(1, 0, 2)

            def step(S, inps):
                qi, ki, vi, bi = inps
                pred = jnp.einsum('bhkv,bhk->bhv', S, ki)
                S = S + bi[..., None, None] * ki[..., :, None] * (vi - pred)[..., None, :]
                o = jnp.einsum('bhkv,bhk->bhv', S, qi)
                return (S, o)
            S0 = jnp.zeros((b, H, DK, DV), x.dtype)
            _, o = jax.lax.scan(step, S0, (qt, kt, vt, bt))
            o = rmsnorm(o, onorm_w)
            o = o.transpose(1, 0, 2, 3).reshape(b, t, H * DV)
            return o @ Wo
        x = input_embeds.transpose(1, 0, 2)
        for l in range(L):
            h = rmsnorm(x, norm1_w[l])
            x = x + delta_attn(h, Wq[l], Wk[l], Wv[l], Wb[l], Wo[l], onorm_w[l])
            h = rmsnorm(x, norm2_w[l])
            gy = h @ Wg[l]
            g, y = jnp.split(gy, 2, axis=-1)
            x = x + jax.nn.silu(g) * y @ Wd[l]
        x = rmsnorm(x, final_norm_w)
        return x.transpose(1, 0, 2)

    def _L3_xattn_ref(image_features, text_features, Wq, bq, Wk, bk, Wv, bv):
        import jax, jax.numpy as jnp
        import numpy as np
        IMG_DIM, TXT_DIM, HID = (128, 96, 128)
        B, LQ, LK = (8, 256, 256)
        query = jnp.einsum('bqi,ih->bqh', image_features, Wq) + bq
        key = jnp.einsum('bkt,th->bkh', text_features, Wk) + bk
        value = jnp.einsum('bkt,th->bkh', text_features, Wv) + bv
        scale = 1.0 / jnp.sqrt(jnp.asarray(HID, query.dtype))
        scores = jnp.einsum('bqh,bkh->bqk', query, key) * scale
        weights = jax.nn.softmax(scores, axis=-1)
        attended = jnp.einsum('bqk,bkh->bqh', weights, value)
        return attended

    def _L3_ffn_ref(x, gamma_x, gamma_slot, slot_embeds, w1, w2):
        import jax, jax.numpy as jnp
        import numpy as np
        EPS = 1e-12

        def rms_norm(t, gamma):
            n = jnp.maximum(jnp.linalg.norm(t, axis=-1, keepdims=True), EPS)
            scale = jnp.sqrt(jnp.asarray(t.shape[-1], t.dtype))
            return t / n * scale * gamma
        b, s, d = x.shape
        e, t, _ = slot_embeds.shape
        xn = rms_norm(x, gamma_x)
        se = rms_norm(slot_embeds, gamma_slot)
        logits = jnp.einsum('bsd,etd->bset', xn, se)
        dispatch = jax.nn.softmax(logits, axis=1)
        slots = jnp.einsum('bsd,bset->betd', xn, dispatch)
        h = jax.nn.gelu(slots @ w1, approximate=False)
        processed = h @ w2
        combine = jax.nn.softmax(logits.reshape(b, s, e * t), axis=-1)
        out = jnp.einsum('bnd,bsn->bsd', processed.reshape(b, e * t, d), combine)
        return out
    x = x + _L0_attn_ref(_layernorm(x, axis=-1), L0_attn_Wq, L0_attn_Wk, L0_attn_Wv, L0_attn_Wg, L0_attn_Wo, L0_attn_gn_weight)
    x = x + _L0_xattn_ref(_layernorm(x, axis=-1), ctx_768, L0_xattn_Wq, L0_xattn_bq, L0_xattn_Wkv, L0_xattn_bkv, L0_xattn_Wo, L0_xattn_bo)
    x = x + _L0_ffn_ref(_layernorm(x, axis=-1), L0_ffn_ln1_w, L0_ffn_ln1_b, L0_ffn_ln2_w, L0_ffn_ln2_b, L0_ffn_conv_w, L0_ffn_attn_w, L0_ffn_proj_w, L0_ffn_router_w, L0_ffn_expert_wv, L0_ffn_expert_proj)
    x = x + _L1_attn_ref(_layernorm(x, axis=-1), L1_attn_Wqkv, L1_attn_bqkv, L1_attn_Wproj, L1_attn_bproj)
    x = x + _L1_xattn_ref(_layernorm(x, axis=-1), ctx_768, L1_xattn_Wq, L1_xattn_Wk, L1_xattn_Wv, L1_xattn_Wo)
    x = x + _L1_ffn_ref(_layernorm(x, axis=-1), L1_ffn_router_w, L1_ffn_w1, L1_ffn_b1, L1_ffn_w2, L1_ffn_b2)
    x = x + _L2_attn_ref(_layernorm(x, axis=-1), L2_attn_Wq, L2_attn_bq, L2_attn_Wk, L2_attn_bk, L2_attn_Wv, L2_attn_bv)
    x = x + _L2_xattn_ref(_layernorm(x, axis=-1), ctx_768, L2_xattn_Wq, L2_xattn_bq, L2_xattn_Wk, L2_xattn_bk, L2_xattn_Wv, L2_xattn_bv, L2_xattn_Wo, L2_xattn_bo)
    x = x + _L2_ffn_ref(_layernorm(x, axis=-1), L2_ffn_gate_w, L2_ffn_gate_bias, L2_ffn_Wu, L2_ffn_bu, L2_ffn_Wd, L2_ffn_bd, L2_ffn_sWu, L2_ffn_sbu, L2_ffn_sWd, L2_ffn_sbd)
    x = x + _L3_attn_ref(_layernorm(x, axis=-1), L3_attn_Wq, L3_attn_Wk, L3_attn_Wv, L3_attn_Wb, L3_attn_Wo, L3_attn_onorm_w, L3_attn_norm1_w, L3_attn_norm2_w, L3_attn_Wg, L3_attn_Wd, L3_attn_final_norm_w)
    x = x + _L3_xattn_ref(_layernorm(x, axis=-1), ctx_768, L3_xattn_Wq, L3_xattn_bq, L3_xattn_Wk, L3_xattn_bk, L3_xattn_Wv, L3_xattn_bv)
    x = x + _L3_ffn_ref(_layernorm(x, axis=-1), L3_ffn_gamma_x, L3_ffn_gamma_slot, L3_ffn_slot_embeds, L3_ffn_w1, L3_ffn_w2)
    return x

_drawn_inputs = setup_inputs


def setup_inputs(seed=0):
    import zlib

    import numpy as np

    out = dict(_drawn_inputs(seed))
    spreads = {'L0_attn_gn_weight': (1.0, 0.6),
     'L0_ffn_ln1_w': (1.0, 0.6),
     'L0_ffn_ln1_b': (0.0, 0.8),
     'L0_ffn_ln2_w': (1.0, 0.6),
     'L0_ffn_ln2_b': (0.0, 0.8),
     'L1_attn_bqkv': (0.0, 0.8),
     'L1_attn_bproj': (0.0, 0.1),
     'L2_attn_bq': (0.0, 2.0),
     'L2_attn_bk': (0.0, 2.0),
     'L2_attn_bv': (0.0, 1.428),
     'L2_ffn_gate_bias': (0.0, 0.1),
     'L2_ffn_bu': (0.0, 0.8),
     'L2_ffn_bd': (0.0, 1.238),
     'L2_ffn_sbu': (0.0, 2.0),
     'L2_ffn_sbd': (0.0, 2.0),
     'L3_ffn_gamma_x': (1.0, 0.6),
     'L3_ffn_gamma_slot': (1.0, 0.6)}
    factors = {'L0_xattn_bq': 8.0,
     'L0_xattn_bkv': 5.389,
     'L0_xattn_bo': 5.694,
     'L0_ffn_conv_w': 8.0,
     'L0_ffn_attn_w': 8.0,
     'L0_ffn_proj_w': 8.0,
     'L0_ffn_router_w': 8.0,
     'L0_ffn_expert_wv': 8.0,
     'L0_ffn_expert_proj': 8.0,
     'L1_attn_Wqkv': 8.0,
     'L1_attn_Wproj': 8.0,
     'L1_ffn_router_w': 4.742,
     'L1_ffn_w1': 4.546,
     'L1_ffn_b1': 29.589,
     'L1_ffn_w2': 4.491,
     'L1_ffn_b2': 32.798,
     'L2_xattn_bq': 64.0,
     'L2_xattn_bk': 200.0,
     'L2_xattn_bv': 51.684,
     'L2_xattn_bo': 36.441,
     'L2_ffn_gate_w': 8.0,
     'L2_ffn_Wu': 4.573,
     'L2_ffn_Wd': 4.131,
     'L2_ffn_sWu': 8.0,
     'L2_ffn_sWd': 8.0,
     'L3_attn_Wb': 7.095,
     'L3_attn_onorm_w': 47.773,
     'L3_attn_norm1_w': 8.0,
     'L3_attn_norm2_w': 40.404,
     'L3_attn_Wg': 8.0,
     'L3_attn_Wd': 8.0,
     'L3_attn_final_norm_w': 64.0,
     'L3_xattn_Wq': 99.176,
     'L3_xattn_bq': 200.0,
     'L3_xattn_Wk': 97.89,
     'L3_xattn_bk': 200.0,
     'L3_xattn_bv': 26.245,
     'L2_attn_Wq': 3.304,
     'L2_attn_Wk': 2.889,
     'L2_xattn_Wq': 2.691,
     'L3_ffn_slot_embeds': 5.012,
     'L3_ffn_w1': 3.059,
     'L3_ffn_w2': 2.75,
     'L3_xattn_Wv': 5.098}
    for name, (base, spread) in spreads.items():
        noise = np.random.default_rng([zlib.crc32(name.encode()), seed]).standard_normal(out[name].shape)
        drawn = base * np.exp(spread * noise) if base else spread * noise
        out[name] = jnp.asarray(drawn.astype(out[name].dtype))
    for name, factor in factors.items():
        out[name] = (out[name] * factor).astype(out[name].dtype)
    return out
```

```python
from contextlib import ExitStack

import numpy as np

import concourse.bass as bass
from concourse import mybir

F32 = mybir.dt.float32
BF16 = mybir.dt.bfloat16
U32 = mybir.dt.uint32
ALU = mybir.AluOpType
ACT = mybir.ActivationFunctionType
AX = mybir.AxisListType

P = 128
NB = 16
T = 128
D = 128
C = 96
GI = 4
NG = NB // GI
GT = GI * T
LN_EPS = 1e-5
BASE_LOADS = 64
PHASES = list(range(12))
ARENA = 0
NAMES = []
PACKS = {}



class Shared:

    def __init__(self, nc, ctx, dram):
        self.nc, self.dram = nc, dram
        self.X = ctx.enter_context(nc.sbuf_tensor("X", [P, NB, D], F32))
        self.cT = ctx.enter_context(nc.sbuf_tensor("cT", [C + 1, NB, T], F32))
        self.Z = ctx.enter_context(nc.sbuf_tensor("Z", [P, NB, D], F32))
        self.ident = ctx.enter_context(nc.sbuf_tensor("ident", [P, P], F32))
        self.half = ctx.enter_context(nc.sbuf_tensor("half", [P, 2 * GI], F32))
        self.plus = ctx.enter_context(nc.sbuf_tensor("plus", [P, 2 * GI], F32))
        self.iota = ctx.enter_context(nc.sbuf_tensor("iota", [P, 8], F32))
        self.arena = [ctx.enter_context(nc.sbuf_tensor(f"arena{i}", [P, ARENA], F32)) for i in range(2)]
        self.loaded = [ctx.enter_context(nc.semaphore(f"weights_loaded{i}")) for i in range(2)]
        self.base_loaded = ctx.enter_context(nc.semaphore("base_loaded"))
        self.loads = [0, 0]
        self.tick = ctx.enter_context(nc.semaphore("tick"))

    def wait_alone(self, eng, sem, value):
        eng.wait_ge(sem, value)
        eng.sem_inc(self.tick, 1)

    def load(self, eng, n):
        if n < len(UNITS):
            name = UNITS[n]
            cols = PACKS[name].cols
            if cols:
                eng.dma_start(self.arena[n % 2][:, 0:cols], self.dram["w_" + name][:, :]).then_inc(self.loaded[n % 2], 16)
                self.loads[n % 2] += 1

    def weights(self, n):
        pack = PACKS[UNITS[n]]
        return ({k: self.arena[n % 2][0:r, o:o + c] for k, (o, r, c) in pack.at.items()},
                self.loaded[n % 2], 16 * self.loads[n % 2])


class Pack:

    def __init__(self, *parts):
        self.at, self.cols = {}, 0
        for name, rows, cols in parts:
            self.at[name] = (self.cols, rows, cols)
            self.cols += cols

    def fill(self, parts):
        out = np.zeros((P, self.cols), np.float32)
        for name, (o, r, c) in self.at.items():
            out[0:r, o:o + c] = parts[name].reshape(r, c)
        return out


class Norm:

    def __init__(self, k, sb, sem, tag):
        self.k = k
        self.st = sb(f"{tag}_st", [P, GI, 6], F32)
        self.mv = sb(f"{tag}_mv", [P, GI, 2], F32)
        self.ve = sb(f"{tag}_ve", [P, GI], F32)
        self.rs = sb(f"{tag}_rs", [P, GI], F32)
        self.xn = sb(f"{tag}_xn", [P, GI, D], F32)
        self.bn = sem(f"{tag}_bn")
        self.stats = sem(f"{tag}_stats")
        self.eps = sem(f"{tag}_eps")
        self.rstd = sem(f"{tag}_rstd")
        self.ready = sem(f"{tag}_ready")
        self.turned = sem(f"{tag}_turned")

    def on_vector_stats(self, dve, g, src):
        for i in range(GI):
            ins = dve.bn_stats(self.st[:, i, :], src(i))
        ins.then_inc(self.bn, 1)
        self.k.wait_alone(dve, self.bn, g + 1)
        for i in range(GI):
            ins = dve.bn_aggr(self.mv[:, i, :], self.st[:, i, :])
        ins.then_inc(self.stats, 1)

    def on_pool(self, pool, g, eps=LN_EPS):
        self.k.wait_alone(pool, self.stats, g + 1)
        pool.tensor_scalar(self.ve[:, :], self.mv[:, :, 1], eps, None, ALU.add).then_inc(self.eps, 1)
        pool.wait_ge(self.eps, g + 1)
        pool.tensor_tensor(self.rs[:, :], self.ve[:, :], self.k.half[:, 0:GI], ALU.pow).then_inc(self.rstd, 1)

    def on_vector_apply(self, dve, g, src):
        dve.wait_ge(self.rstd, g + 1)
        for i in range(GI):
            ins = dve.tensor_scalar(self.xn[:, i, :], src(i), self.mv[:, i, 0:1], self.rs[:, i:i + 1],
                                    ALU.subtract, ALU.mult)
        ins.then_inc(self.ready, 1)

    def on_tensor(self, pe, g, bank):
        pe.wait_ge(self.ready, g + 1)
        for i in range(GI):
            ins = pe.transpose(bank[:, i * T:(i + 1) * T], self.xn[:, i, :], self.k.ident[:, :])
        ins.then_inc(self.turned, 1)


class Scope:

    def __init__(self, k, ctx, tag):
        self.k, self.ctx, self.tag, self.sems = k, ctx, tag, []

    def sb(self, name, shape, dt=F32):
        return self.ctx.enter_context(self.k.nc.sbuf_tensor(f"{self.tag}_{name}", shape, dt))

    def banks(self, n=8):
        return [self.ctx.enter_context(self.k.nc.psum_tensor(f"{self.tag}_bank{i}", [P, 512], F32)) for i in range(n)]

    def sem(self, name):
        s = self.ctx.enter_context(self.k.nc.semaphore(f"{self.tag}_{name}"))
        self.sems.append(s)
        return s



H = 16
DH = D // H
R = 4
TILES = H // R
HW = 1 + DH
VW = DH + 1
SPREAD = TILES * P
PACKS["l0x"] = PACKS["l1x"] = PACKS["l2x"] = Pack(
    ("wq", D, SPREAD), ("bq", P, TILES), ("wk", C + 1, SPREAD), ("wv", C + 1, H * VW), ("wo", D, D), ("bo", 1, D),
    ("one", 1, T))
PACKS["l0g"] = Pack(
    ("wq", D, SPREAD), ("wqp", D, SPREAD), ("wk", D, SPREAD), ("wkp", D, SPREAD), ("wv", D, H * VW), ("wo", D, D),
    ("ln1_w", D, 1), ("ln1_b", D, 1), ("conv", D, 3), ("cq", P, T), ("sq", P, T), ("ck", P, T), ("sk", P, T),
    ("aug", 1, P), ("vaug", 1, H * VW), ("one", 1, GT), ("mask", T, T), ("maskT", T, T))


def spread(w, bias=None, aug=0.0, perm=False):
    rows = w.shape[0] + (bias is not None)
    out = np.zeros((rows, TILES, R, 32), np.float32)
    order = [(d + DH // 2) % DH for d in range(DH)] if perm else list(range(DH))
    out[:w.shape[0], :, :, 1:HW] = w.reshape(-1, TILES, R, DH)[..., order]
    if bias is not None:
        out[-1, :, :, 1:HW] = bias.reshape(TILES, R, DH)
        out[-1, :, :, 0] = aug
    return out.reshape(rows, SPREAD)


def value_columns(w, bias):
    out = np.zeros((w.shape[0] + 1, H, VW), np.float32)
    out[:-1, :, :DH] = w.reshape(-1, H, DH)
    out[-1, :, :DH] = bias.reshape(H, DH)
    out[-1, :, DH] = 1.0
    return out.reshape(-1, H * VW)


class SoftAttention:

    def __init__(self, k, s, n, kind):
        self.k, self.kind = k, kind
        self.w, self.loaded, self.count = k.weights(n)
        self.cross = kind != "l0g"
        self.SCALE = float(DH) ** -0.5
        sb = s.sb
        self.norm = Norm(k, sb, s.sem, "ln")
        self.xT = sb("xT", [D, GT])
        self.qs, self.ks = sb("qs", [P, TILES, GT]), sb("ks", [P, TILES, GT])
        self.v = sb("v", [T, GI, H * VW])
        self.nm = [sb(f"nm{i}", [T, TILES, P]) for i in range(2)]
        self.qa = [sb(f"qa{i}", [P, TILES, T]) for i in range(2)]
        self.PT = [sb(f"PT{i}", [T, R, TILES * T]) for i in range(2)]
        self.rs = sb("rs", [T, H])
        self.at = sb("at", [T, H, DH])
        self.aT = sb("aT", [D, T])
        if self.cross:
            self.cG = sb("cG", [C + 1, GI, T])
            self.dst = k.X
        else:
            self.norm2 = Norm(k, sb, s.sem, "ln1")
            self.hT = sb("hT", [D, GT])
            self.t1, self.t2 = [sb(f"t1{i}", [P, GT]) for i in range(2)], [sb(f"t2{i}", [P, GT]) for i in range(2)]
            self.identb = sb("identb", [P, P], BF16)
            self.maskb = sb("maskb", [T, TILES, T], BF16)
            self.maskTb = sb("maskTb", [T, TILES, T], BF16)
            self.dst = k.Z
        self.b = s.banks(8)
        names = ("cG_ready k_made k_ready v_made v_ready xT_ready q_made q_ready zeroed scored maxed nm_turned qa_ready "
                 "scored2 expd pv inverted at_ready at_turned aT_ready out_made added "
                 "h_ready conv1 conv2 masks roped summed t_made")
        self.q = {x: s.sem(x) for x in names.split()}


    def project_tensor(self, pe, g):
        q, b, w = self.q, self.b, self.w
        pe.wait_ge(q["cG_ready"], g + 1)
        for j in range(TILES):
            ins = pe.matmul(b[j][:, :], w["wk"][:, j * P:(j + 1) * P], self.cG[:, :, :], start=True, stop=True)
        ins.then_inc(q["k_made"], 1)
        for i in range(GI):
            ins = pe.matmul(b[5 + i // 3][:, (i % 3) * H * VW:(i % 3 + 1) * H * VW], self.cG[:, i, :], w["wv"],
                            start=True, stop=True)
        ins.then_inc(q["v_made"], 1)
        pe.wait_ge(q["added"], g * GI + 1)
        self.norm.on_tensor(pe, g, b[7])
        pe.wait_ge(q["xT_ready"], g + 1)
        pe.wait_ge(q["k_ready"], g + 1)
        for j in range(TILES):
            ins = pe.matmul(b[j][:, :], w["wq"][:, j * P:(j + 1) * P], self.xT[:, :], start=True, stop=True)
        ins.then_inc(q["q_made"], 1)
        pe.wait_ge(q["q_ready"], g + 1)
        pe.wait_ge(q["v_ready"], g + 1)

    def project_scalar(self, act, g):
        q, b = self.q, self.b
        act.wait_ge(q["k_made"], g + 1)
        for j in range(TILES):
            ins = act.copy(self.ks[:, j, :], b[j][:, :])
        ins.then_inc(q["k_ready"], 1)
        act.wait_ge(q["v_made"], g + 2)
        act.copy(self.v[:, 0:3, :], b[5][:, 0:3 * H * VW])
        act.copy(self.v[:, 3, :], b[6][:, 0:H * VW]).then_inc(q["v_ready"], 1)
        act.wait_ge(self.norm.turned, g + 1)
        act.copy(self.xT[:, :], b[7][:, :]).then_inc(q["xT_ready"], 1)

    def project_vector(self, dve, g):
        q, b = self.q, self.b
        k_src = lambda i: self.k.X[:, g * GI + i, :]
        self.norm.on_vector_stats(dve, g, k_src)
        self.norm.on_vector_apply(dve, g, k_src)
        dve.wait_ge(q["q_made"], g + 1)
        for j in range(TILES):
            ins = dve.tensor_scalar(self.qs[:, j, :], b[j][:, :], self.w["bq"][:, j:j + 1], self.SCALE, ALU.add, ALU.mult)
        ins.then_inc(q["q_ready"], 1)


    def own_tensor(self, pe, g):
        q, b, w = self.q, self.b, self.w
        pe.wait_ge(q["added"], g * GI + 1)
        self.norm2.on_tensor(pe, g, b[7])
        pe.wait_ge(q["conv2"], g * 2 + 2)
        for m in range(2 * TILES):
            j, name = m % TILES, "k" if m < TILES else "q"
            lo = b[2 * (m % 2)]
            hi = b[2 * (m % 2) + 1]
            pe.wait_ge(q["roped"], g * 2 * TILES + m + 1)
            pe.matmul(lo[:, :], w["w" + name][:, j * P:(j + 1) * P], self.xT[:, :], start=True, stop=(name == "q"))
            if name == "k":
                pe.matmul(lo[:, :], w["aug"], w["one"], start=False, stop=True)
            pe.matmul(hi[:, :], w["w" + name + "p"][:, j * P:(j + 1) * P], self.xT[:, :], start=True, stop=True)\
              .then_inc(q["t_made"], 1)
        for i in range(GI):
            o = b[5 + i // 3][:, (i % 3) * H * VW:(i % 3 + 1) * H * VW]
            pe.matmul(o, self.xT[:, i * T:(i + 1) * T], w["wv"], start=True, stop=False)
            ins = pe.matmul(o, w["one"][:, 0:T], w["vaug"], start=False, stop=True)
        ins.then_inc(q["v_made"], 1)
        pe.wait_ge(q["roped"], g * 2 * TILES + 2 * TILES + 2)
        pe.wait_ge(q["summed"], g * 2 * TILES + 2 * TILES + 2)
        pe.wait_ge(q["v_ready"], g + 1)

    def own_scalar(self, act, g):
        q, b = self.q, self.b
        act.wait_ge(self.norm2.turned, g + 1)
        act.activation(self.hT[:, :], b[7][:, :], ACT.Identity, scale=self.w["ln1_w"], bias=self.w["ln1_b"])\
           .then_inc(q["h_ready"], 1)
        act.wait_ge(q["v_made"], g + 2)
        act.copy(self.v[:, 0:3, :], b[5][:, 0:3 * H * VW])
        act.copy(self.v[:, 3, :], b[6][:, 0:H * VW]).then_inc(q["v_ready"], 1)

    def own_vector(self, dve, g):
        q, b, w = self.q, self.b, self.w
        x_src = lambda i: self.k.X[:, g * GI + i, :]
        self.norm.on_vector_stats(dve, g, x_src)
        self.norm.on_vector_apply(dve, g, x_src)
        dve.wait_ge(self.norm.ready, g + 1)
        dve.tensor_copy(self.k.Z[:, bass.ds(g * GI, GI), :], self.norm.xn[:, :, :])
        y_src = lambda i: self.norm.xn[:, i, :]
        self.norm2.on_vector_stats(dve, g, y_src)
        self.norm2.on_vector_apply(dve, g, y_src)
        h = self.hT[:, :].rearrange("p (i t) -> p i t", i=GI)
        x = self.xT[:, :].rearrange("p (i t) -> p i t", i=GI)
        dve.wait_ge(q["h_ready"], g + 1)
        dve.tensor_scalar(x, h, w["conv"][:, 2:3], None, ALU.mult).then_inc(q["conv1"], 1)
        dve.wait_ge(q["conv1"], g + 1)
        for shift in (1, 2):
            dve.scalar_tensor_tensor(out=x[:, :, shift:T], in0=h[:, :, 0:T - shift], scalar=w["conv"][:, 2 - shift:3 - shift],
                                     in1=x[:, :, shift:T], op0=ALU.mult, op1=ALU.add).then_inc(q["conv2"], 1)
            dve.wait_ge(q["conv2"], g * 2 + shift)
        for m in range(2 * TILES):
            name = "k" if m < TILES else "q"
            dve.wait_ge(q["summed"], g * 2 * TILES + m + 1)
            dve.wait_ge(q["t_made"], g * 2 * TILES + m + 1)
            for t, bank, table in ((self.t1, b[2 * (m % 2)], w["c" + name]), (self.t2, b[2 * (m % 2) + 1], w["s" + name])):
                ins = dve.tensor_tensor(t[m % 2][:, :].rearrange("p (i t) -> p i t", i=GI),
                                        bank[:, :].rearrange("p (i t) -> p i t", i=GI),
                                        table.unsqueeze(1).to_broadcast([P, GI, T]), ALU.mult)
            ins.then_inc(q["roped"], 1)

    def own_pool(self, pool, g):
        q = self.q
        self.norm.on_pool(pool, g)
        self.norm2.on_pool(pool, g)
        for m in range(2 * TILES):
            pool.wait_ge(q["roped"], g * 2 * TILES + m + 3)
            dst = (self.ks if m < TILES else self.qs)[:, m % TILES, :]
            pool.tensor_tensor(dst, self.t1[m % 2][:, :], self.t2[m % 2][:, :], ALU.add).then_inc(q["summed"], 1)


    def first_scores(self, pe, g, i, groups):
        q = self.q
        for r in groups:
            u = g * GI + i
            pe.wait_ge(q["maxed"], u * R + r + 1)
            bank = self.b[r % 2]
            if not self.cross:
                pe.matmul(bank[:, :], self.identb[:, :], self.maskb[:, :, :], start=True, stop=False, skip_group_check=True)
            for j in range(TILES):
                ins = pe.matmul(bank[:, j * T:(j + 1) * T], self.qs[32 * r:32 * r + HW, j, i * T:(i + 1) * T],
                                self.ks[32 * r:32 * r + HW, j, i * T:(i + 1) * T], start=self.cross, stop=True,
                                skip_group_check=True)
            ins.then_inc(q["scored"], 1)

    def second_scores(self, pe, g, i):
        q = self.q
        u = g * GI + i
        pe.wait_ge(q["qa_ready"], u + 1)
        for r in range(R):
            pe.wait_ge(q["expd"], u * R + r + 1)
            bank = self.b[2 + r % 2]
            if not self.cross:
                pe.matmul(bank[:, :], self.identb[:, :], self.maskTb[:, :, :], start=True, stop=False, skip_group_check=True)
            for j in range(TILES):
                ins = pe.matmul(bank[:, j * T:(j + 1) * T], self.ks[32 * r:32 * r + HW, j, i * T:(i + 1) * T],
                                self.qa[i % 2][32 * r:32 * r + HW, j, :], start=self.cross, stop=True, skip_group_check=True)
            ins.then_inc(q["scored2"], 1)

    def attend_tensor(self, pe, g):
        q, b, w = self.q, self.b, self.w
        for t in range(GI + 3):
            if t < GI:
                self.first_scores(pe, g, t, (0, 1))
            if 0 <= t - 1 < GI:
                u = g * GI + t - 1
                pe.wait_ge(q["maxed"], u * R + R + 2)
                for j in range(TILES):
                    ins = pe.transpose(b[4][:, j * T:(j + 1) * T], self.nm[(t - 1) % 2][:, j, :], self.k.ident[:, :])
                ins.then_inc(q["nm_turned"], 1)
            if 0 <= t - 3 < GI:
                u = g * GI + t - 3
                pe.wait_ge(q["at_ready"], u + 1)
                pe.transpose(b[6][:, 0:T], self.at[:, :, :].rearrange("p h d -> p (h d)"), self.k.ident[:, :])\
                  .then_inc(q["at_turned"], 1)
            if t < GI:
                self.first_scores(pe, g, t, (2, 3))
            if 0 <= t - 1 < GI:
                self.second_scores(pe, g, t - 1)
            if 0 <= t - 2 < GI:
                u = g * GI + t - 2
                pe.wait_ge(q["expd"], u * R + R + 2)
                for h in range(H):
                    j, r = h // R, h % R
                    ins = pe.matmul(b[5][:, h * VW:(h + 1) * VW], self.PT[(t - 2) % 2][:, r, j * T:(j + 1) * T],
                                    self.v[:, t - 2, h * VW:(h + 1) * VW], start=True, stop=True)
                ins.then_inc(q["pv"], 1)
            if 0 <= t - 3 < GI:
                u = g * GI + t - 3
                pe.wait_ge(q["aT_ready"], u + 1)
                pe.wait_ge(q["added"], u + 1)
                ins = pe.matmul(b[7][:, 0:D], self.aT[:, :], w["wo"], start=True, stop=not self.cross)
                if self.cross:
                    ins = pe.matmul(b[7][:, 0:D], w["one"], w["bo"], start=False, stop=True)
                ins.then_inc(q["out_made"], 1)

    def attend_scalar(self, act, g):
        q, b = self.q, self.b
        for t in range(1, GI + 3):
            if 0 <= t - 3 < GI:
                u = g * GI + t - 3
                act.wait_ge(q["at_turned"], u + 1)
                act.copy(self.aT[:, :], b[6][:, 0:T]).then_inc(q["aT_ready"], 1)
            if 0 <= t - 1 < GI:
                u = g * GI + t - 1
                act.wait_ge(q["pv"], u + 1)
                for r in range(R):
                    act.wait_ge(q["scored2"], u * R + r + 1)
                    act.activation(self.PT[(t - 1) % 2][:, r, :], b[2 + r % 2][:, :], ACT.Exp).then_inc(q["expd"], 1)

    def attend_vector(self, dve, g):
        q, b = self.q, self.b

        def maxima(i, groups):
            for r in groups:
                dve.wait_ge(q["scored"], (g * GI + i) * R + r + 1)
                dve.tensor_reduce(self.nm[i % 2][:, :, 32 * r], b[r % 2][:, :].rearrange("p (j t) -> p j t", j=TILES),
                                  AX.X, ALU.max, negate=True).then_inc(q["maxed"], 1)

        for t in range(GI + 3):
            if t < GI:
                maxima(t, (0, 1))
            if 0 <= t - 1 < GI:
                i, u = t - 1, g * GI + t - 1
                dve.wait_ge(q["nm_turned"], u + 1)
                dve.tensor_tensor(self.qa[i % 2][:, :, :], b[4][:, :].rearrange("p (j t) -> p j t", j=TILES),
                                  self.qs[:, :, i * T:(i + 1) * T], ALU.add).then_inc(q["qa_ready"], 1)
            if t < GI:
                maxima(t, (2, 3))
            if 0 <= t - 2 < GI:
                u = g * GI + t - 2
                o = b[5][:, 0:H * VW].rearrange("p (h c) -> p h c", h=H)
                self.k.wait_alone(dve, q["pv"], u + 3)
                dve.reciprocal(self.rs[:, :], o[:, :, DH]).then_inc(q["inverted"], 1)
                dve.wait_ge(q["inverted"], u + 1)
                dve.tensor_tensor(self.at[:, :, :], o[:, :, 0:DH], self.rs[:, :].unsqueeze(2).to_broadcast([T, H, DH]),
                                  ALU.mult).then_inc(q["at_ready"], 1)
            if 0 <= t - 3 < GI:
                u = g * GI + t - 3
                x = self.dst[:, u, :]
                dve.wait_ge(q["out_made"], u + 1)
                dve.tensor_tensor(x, b[7][:, 0:D], x, ALU.add).then_inc(q["added"], 1)


def sublayer_soft_attention(k, s, n):
    a = SoftAttention(k, s, n, UNITS[n])
    q, w = a.q, a.w
    with k.nc.Block() as block:
        @block.sync
        def _(sp):
            k.load(sp, n + 1)

        @block.gpsimd
        def _(pool):
            for nm in a.nm:
                ins = pool.memset(nm[:, :, :], 0.0)
            ins.then_inc(q["zeroed"], 1)
            if not a.cross:
                pool.sem_inc(q["summed"], 2)
            with pool.Fori(0, NG) as g:
                if a.cross:
                    k.wait_alone(pool, q["v_made"], g + 1)
                    pool.tensor_copy(a.cG[:, :, :], k.cT[:, bass.ds(g * GI, GI), :]).then_inc(q["cG_ready"], 1)
                    a.norm.on_pool(pool, g)
                else:
                    a.own_pool(pool, g)

        @block.tensor
        def _(pe):
            pe.wait_ge(a.loaded, a.count)
            pe.sem_inc(q["pv"], 2)
            pe.sem_inc(q["v_made"], 1)
            if not a.cross:
                pe.wait_ge(q["masks"], 3)
            with pe.Fori(0, NG) as g:
                (a.project_tensor if a.cross else a.own_tensor)(pe, g)
                a.attend_tensor(pe, g)

        @block.scalar
        def _(act):
            act.wait_ge(a.loaded, a.count)
            act.sem_inc(q["expd"], 2)
            if not a.cross:
                act.copy(a.identb[:, :], k.ident[:, :]).then_inc(q["masks"], 1)
                act.copy(a.maskb[:, :, :], w["mask"].unsqueeze(1).to_broadcast([T, TILES, T])).then_inc(q["masks"], 1)
                act.copy(a.maskTb[:, :, :], w["maskT"].unsqueeze(1).to_broadcast([T, TILES, T])).then_inc(q["masks"], 1)
            with act.Fori(0, NG) as g:
                (a.project_scalar if a.cross else a.own_scalar)(act, g)
                a.attend_scalar(act, g)

        @block.vector
        def _(dve):
            dve.wait_ge(a.loaded, a.count)
            dve.wait_ge(q["zeroed"], 1)
            dve.sem_inc(q["maxed"], 2)
            dve.sem_inc(q["added"], 1)
            if not a.cross:
                dve.sem_inc(q["roped"], 2)
            with dve.Fori(0, NG) as g:
                (a.project_vector if a.cross else a.own_vector)(dve, g)
                a.attend_vector(dve, g)


def cross_pack(wq, bq, wk, bk, wv, bv, wo, bo):
    return {"wq": spread(wq), "bq": spread(bq[None]).reshape(TILES, P).T, "wk": spread(wk, bk, 1.0),
            "wv": value_columns(wv, bv), "wo": wo, "bo": bo, "one": np.ones((1, T), np.float32)}


def pack_l0x(a):
    wkv = a["L0_xattn_Wkv"].reshape(H, 2, DH, C)
    bkv = a["L0_xattn_bkv"].reshape(H, 2, DH)
    return cross_pack(a["L0_xattn_Wq"].T, a["L0_xattn_bq"], wkv[:, 0].reshape(D, C).T, bkv[:, 0].reshape(D),
                      wkv[:, 1].reshape(D, C).T, bkv[:, 1].reshape(D), a["L0_xattn_Wo"].T, a["L0_xattn_bo"])


def pack_l1x(a):
    z = np.zeros(D, np.float32)
    return cross_pack(a["L1_xattn_Wq"].T, z, a["L1_xattn_Wk"].T, z, a["L1_xattn_Wv"].T, z, a["L1_xattn_Wo"].T, z)


def pack_l2x(a):
    return cross_pack(*(a["L2_xattn_" + x].T for x in ("Wq", "bq", "Wk", "bk", "Wv", "bv", "Wo", "bo")))


def rotary(width, copies_at, scale):
    f = 1.0 / (10000.0 ** (np.arange(0, width, 2, dtype=np.float32) / np.float32(width)))
    angle = np.arange(T, dtype=np.float32)[:, None] * f.astype(np.float32)[None]
    cos, sin = np.zeros((P, T), np.float32), np.zeros((P, T), np.float32)
    for d in range(width):
        for row in copies_at(d):
            cos[row] = np.cos(angle[:, d % (width // 2)]) * scale
            sin[row] = np.sin(angle[:, d % (width // 2)]) * (-scale if d < width // 2 else scale)
    return cos, sin


def pack_l0g(a):
    wq, wk, wv = (a["L0_ffn_attn_w"][:, i * D:(i + 1) * D] for i in range(3))
    rows = lambda d: [32 * r + 1 + d for r in range(R)]
    cq, sq = rotary(DH, rows, float(DH) ** -0.5)
    ck, sk = rotary(DH, rows, 1.0)
    ck[0::32] = 1.0
    aug = np.zeros((1, P), np.float32)
    aug[0, 0::32] = 1.0
    v = value_columns(wv, np.zeros(D, np.float32))
    allowed = np.tril(np.ones((T, T), bool))
    mask = np.where(allowed, 0.0, -1e30).astype(np.float32)
    return {"wq": spread(wq), "wqp": spread(wq, perm=True), "wk": spread(wk), "wkp": spread(wk, perm=True),
            "wv": v[:-1], "vaug": v[-1:], "wo": a["L0_ffn_proj_w"], "ln1_w": a["L0_ffn_ln1_w"], "ln1_b": a["L0_ffn_ln1_b"],
            "conv": a["L0_ffn_conv_w"], "cq": cq, "sq": sq, "ck": ck, "sk": sk, "aug": aug,
            "one": np.ones((1, GT), np.float32), "mask": mask, "maskT": mask.T}



RH, RK, RV = 4, 32, 64
PACKS["l0a"] = Pack(("wq", D, D), ("wqp", D, D), ("wk", D, D), ("wkp", D, D), ("wvg", D, 4 * D), ("wo", P, 2 * D),
                    ("gn", P, 1), ("cq", P, T), ("sq", P, T), ("ck", P, T), ("sk", P, T), ("decay", T, RH * T))


def sublayer_retention(k, s, n):
    nc, X, ident = k.nc, k.X, k.ident
    w, loaded, count = k.weights(n)
    norm = Norm(k, s.sb, s.sem, "ln")
    wo = s.sb("wo", [P, 2, D])
    xT = s.sb("xT", [D, GT])
    part = [s.sb(f"part{i}", [D, GT]) for i in range(4)]
    qT, kT = s.sb("qT", [D, GT]), s.sb("kT", [D, GT])
    vg = s.sb("vg", [T, GI, 2, RH * RV])
    PT = s.sb("PT", [T, RH, GT])
    osq = [s.sb(f"osq{i}", [T, RH, RV]) for i in range(2)]
    ss, sse, rr = s.sb("ss", [T, RH]), s.sb("sse", [T, RH]), s.sb("rr", [T, RH])
    on = s.sb("on", [T, RH, RV])
    og = [s.sb(f"og{i}", [T, RH * RV]) for i in range(2)]
    ogT = s.sb("ogT", [P, 2, T])
    b = s.banks(8)
    q = {x: s.sem(x) for x in ("gained xT_ready qk_made parts qk_ready vg_made vg_ready scored decayed o_made squared summed "
                               "meaned rooted on_ready og_ready og_turned ogT_ready out_made added").split()}

    with nc.Block() as block:
        @block.sync
        def _(sp):
            k.load(sp, n + 1)

        @block.gpsimd
        def _(pool):
            with pool.Fori(0, NG) as g:
                norm.on_pool(pool, g)
                pool.wait_ge(q["parts"], g + 1)
                pool.tensor_tensor(qT[:, :], part[0][:, :], part[1][:, :], ALU.add)
                pool.tensor_tensor(kT[:, :], part[2][:, :], part[3][:, :], ALU.add).then_inc(q["qk_ready"], 1)
                for i in range(GI):
                    u = g * GI + i
                    k.wait_alone(pool, q["summed"], u + 1)
                    pool.tensor_scalar(sse[:, :], ss[:, :], 1.0 / RV, LN_EPS, ALU.mult, ALU.add).then_inc(q["meaned"], 1)
                    pool.wait_ge(q["meaned"], u + 1)
                    pool.tensor_tensor(rr[:, :], sse[:, :], k.half[:, 0:RH], ALU.pow).then_inc(q["rooted"], 1)

        @block.tensor
        def _(pe):
            pe.wait_ge(loaded, count)
            with pe.Fori(0, NG) as g:
                norm.on_tensor(pe, g, b[6])
                pe.wait_ge(q["xT_ready"], g + 1)
                pe.wait_ge(q["added"], g * GI + 1)
                for j, name in enumerate(("wq", "wqp", "wk", "wkp")):
                    ins = pe.matmul(b[j][:, :], w[name], xT[:, :], start=True, stop=True)
                ins.then_inc(q["qk_made"], 1)
                for i in range(GI):
                    u = g * GI + i
                    pe.wait_ge(q["vg_ready"], u + 1)
                    pe.matmul(b[4 + i % 2][:, :], xT[:, i * T:(i + 1) * T], w["wvg"], start=True, stop=True)\
                      .then_inc(q["vg_made"], 1)
                pe.wait_ge(q["qk_ready"], g + 1)
                for h in range(RH):
                    for i in range(GI):
                        ins = pe.matmul(b[h][:, i * T:(i + 1) * T], kT[RK * h:RK * (h + 1), i * T:(i + 1) * T],
                                        qT[RK * h:RK * (h + 1), i * T:(i + 1) * T], start=True, stop=True)
                    ins.then_inc(q["scored"], 1)
                pe.wait_ge(q["decayed"], g * RH + RH)
                pe.wait_ge(q["vg_ready"], g * GI + GI + 2)
                for t in range(GI + 2):
                    if t < GI:
                        for h in range(RH):
                            ins = pe.matmul(b[6 + t % 2][:, h * RV:(h + 1) * RV], PT[:, h, t * T:(t + 1) * T],
                                            vg[:, t, 0, h * RV:(h + 1) * RV], start=True, stop=True)
                        ins.then_inc(q["o_made"], 1)
                    if 0 <= t - 2 < GI:
                        u = g * GI + t - 2
                        pe.wait_ge(q["ogT_ready"], u + 1)
                        pe.wait_ge(q["added"], u + 1)
                        for c in range(2):
                            ins = pe.matmul(b[0][:, 0:D], ogT[:, c, :], wo[:, c, :], start=(c == 0), stop=(c == 1))
                        ins.then_inc(q["out_made"], 1)
                    if 0 <= t - 1 < GI:
                        u = g * GI + t - 1
                        pe.wait_ge(q["og_ready"], u + 1)
                        for c in range(2):
                            ins = pe.transpose(b[4][:, c * T:(c + 1) * T], og[(t - 1) % 2][:, c * P:(c + 1) * P], ident[:, :])
                        ins.then_inc(q["og_turned"], 1)

        @block.scalar
        def _(act):
            act.sem_inc(q["vg_ready"], 2)
            with act.Fori(0, NG) as g:
                act.wait_ge(norm.turned, g + 1)
                act.copy(xT[:, :], b[6][:, :]).then_inc(q["xT_ready"], 1)
                for i in range(GI):
                    u = g * GI + i
                    act.wait_ge(q["vg_made"], u + 1)
                    act.copy(vg[:, i, :, :], b[4 + i % 2][:, :].rearrange("p (c x) -> p c x", c=2)).then_inc(q["vg_ready"], 1)
                for t in range(GI + 1):
                    if t < GI:
                        act.wait_ge(q["o_made"], g * GI + t + 1)
                        act.activation(osq[t % 2][:, :, :], b[6 + t % 2][:, 0:RH * RV].rearrange("p (h d) -> p h d", h=RH), ACT.Square)\
                           .then_inc(q["squared"], 1)
                    if t >= 1:
                        act.wait_ge(q["og_turned"], g * GI + t)
                        act.copy(ogT[:, :, :], b[4][:, 0:2 * T].rearrange("p (c t) -> p c t", c=2)).then_inc(q["ogT_ready"], 1)

        @block.vector
        def _(dve):
            dve.wait_ge(loaded, count)
            dve.tensor_scalar(wo[:, :, :], w["wo"].rearrange("p (c d) -> p c d", c=2), w["gn"], None, ALU.mult)\
               .then_inc(q["gained"], 1)
            dve.wait_ge(q["gained"], 1)
            dve.sem_inc(q["added"], 1)
            with dve.Fori(0, NG) as g:
                def src(i):
                    return X[:, g * GI + i, :]
                norm.on_vector_stats(dve, g, src)
                norm.on_vector_apply(dve, g, src)
                dve.wait_ge(q["qk_made"], g + 1)
                for j, name in enumerate(("cq", "sq", "ck", "sk")):
                    ins = dve.tensor_tensor(part[j][:, :].rearrange("p (i t) -> p i t", i=GI),
                                            b[j][:, :].rearrange("p (i t) -> p i t", i=GI),
                                            w[name].unsqueeze(1).to_broadcast([P, GI, T]), ALU.mult)
                ins.then_inc(q["parts"], 1)
                decay = w["decay"].rearrange("p (h t) -> p h t", h=RH)
                for h in range(RH):
                    dve.wait_ge(q["scored"], g * RH + h + 1)
                    dve.tensor_tensor(PT[:, h, :].rearrange("p (i t) -> p i t", i=GI),
                                      b[h][:, :].rearrange("p (i t) -> p i t", i=GI),
                                      decay[:, h, :].unsqueeze(1).to_broadcast([T, GI, T]), ALU.mult).then_inc(q["decayed"], 1)
                for t in range(GI + 2):
                    if 0 <= t - 2 < GI:
                        u = g * GI + t - 2
                        dve.wait_ge(q["out_made"], u + 1)
                        dve.tensor_tensor(src(t - 2), b[0][:, 0:D], src(t - 2), ALU.add).then_inc(q["added"], 1)
                    if t < GI:
                        u = g * GI + t
                        o = b[6 + t % 2][:, 0:RH * RV].rearrange("p (h d) -> p h d", h=RH)
                        dve.wait_ge(q["squared"], u + 1)
                        dve.tensor_reduce(ss[:, :], osq[t % 2][:, :, :], AX.X, ALU.add).then_inc(q["summed"], 1)
                        dve.wait_ge(q["rooted"], u + 1)
                        dve.tensor_tensor(on[:, :, :], o, rr[:, :].unsqueeze(2).to_broadcast([T, RH, RV]), ALU.mult)\
                           .then_inc(q["on_ready"], 1)
                        dve.wait_ge(q["on_ready"], u + 1)
                        dve.tensor_tensor(og[t % 2][:, :], on[:, :, :].rearrange("p h d -> p (h d)"), vg[:, t, 1, :], ALU.mult)\
                           .then_inc(q["og_ready"], 1)


def pack_l0a(a):
    partner = [(c // RK) * RK + (c % RK + RK // 2) % RK for c in range(D)]
    rows = lambda d: [RK * h + d for h in range(RH)]
    cq, sq = rotary(RK, rows, float(RK) ** -0.5)
    ck, sk = rotary(RK, rows, 1.0)
    gamma = 1.0 - np.exp2(-5.0 - np.arange(RH, dtype=np.float32))
    steps = (np.arange(T)[None, :] - np.arange(T)[:, None]).astype(np.float32)
    decay = np.where(steps >= 0, gamma[:, None, None] ** np.maximum(steps, 0), 0.0).astype(np.float32)
    return {"wq": a["L0_attn_Wq"], "wqp": a["L0_attn_Wq"][:, partner], "wk": a["L0_attn_Wk"], "wkp": a["L0_attn_Wk"][:, partner],
            "wvg": np.concatenate([a["L0_attn_Wv"], a["L0_attn_Wg"]], 1),
            "wo": a["L0_attn_Wo"].reshape(2, P, D).transpose(1, 0, 2),
            "gn": np.concatenate([a["L0_attn_gn_weight"], a["L0_attn_gn_weight"]]),
            "cq": cq, "sq": sq, "ck": ck, "sk": sk, "decay": decay.transpose(1, 0, 2)}



LAYERS = 12
LAYER_COLS = D + 2 * D + D + 2 + 2 * D
PACKS["l1a"] = Pack(("blocks", D, D),)


def sublayer_linear(k, s, n):
    nc, X, ident = k.nc, k.X, k.ident
    w, loaded, count = k.weights(n)
    norm = Norm(k, s.sb, s.sem, "ln")
    RT = s.sb("RT", [D, NB * T])
    buf = [s.sb(f"layer{i}", [P, LAYER_COLS]) for i in range(2)]
    qT = [s.sb(f"qT{i}", [D, GT]) for i in range(4)]
    kv = [s.sb(f"kv{i}", [T, GI, 2 * D]) for i in range(2)]
    M = [s.sb(f"M{i}", [D, GT]) for i in range(2)]
    yT = [s.sb(f"yT{i}", [D, GT]) for i in range(2)]
    bQ, bK0, bK1, bM, bY, bR, bX0, bX1 = s.banks(8)
    bK = (bK0, bK1)
    q = {x: s.sem(x) for x in ("RT_set streamed0 streamed1 layer_done q_made q_ready kv_made kv_ready m_made m_ready y_made "
                               "y_ready r_made r_ready back added").split()}
    STEPS = 2 * NG

    with nc.Block() as block:
        @block.sync
        def _(sp):
            k.load(sp, n + 1)
            sp.sem_inc(q["layer_done"], 2)
            with sp.Fori(0, LAYERS // 2) as pair:
                for l in range(2):
                    sp.wait_ge(q["layer_done"], pair * 2 + l + 1)
                    sp.dma_start(buf[l][:, :], k.dram["layers_l1a"][bass.ds(pair * 2 + l, 1), :, :]
                                 .rearrange("o p c -> (o p) c")).then_inc(q[f"streamed{l}"], 16)

        @block.gpsimd
        def _(pool):
            with pool.Fori(0, NG) as g:
                norm.on_pool(pool, g)

        @block.tensor
        def _(pe):
            pe.wait_ge(loaded, count)
            pe.sem_inc(norm.turned, 1)
            with pe.Fori(0, NG) as g:
                pe.wait_ge(q["RT_set"], g + 1)
                norm.on_tensor(pe, g, bX0)
            pe.wait_ge(q["RT_set"], NG + 1)
            with pe.Fori(0, LAYERS // 2) as pair:
                for t in range(STEPS + 3):
                    if 0 <= t - 2 < STEPS:
                        x = t - 2
                        u = pair * STEPS + x
                        pe.wait_ge(q["m_ready"], u + 1)
                        pe.wait_ge(q["q_ready"], u + 2)
                        pe.wait_ge(q["y_ready"], u + 1)
                        for i in range(GI):
                            ins = pe.matmul(bY[:, i * T:(i + 1) * T], M[x % 2][:, i * D:(i + 1) * D],
                                            qT[x % 4][:, i * T:(i + 1) * T], start=True, stop=True)
                        ins.then_inc(q["y_made"], 1)
                    if 0 <= t - 3 < STEPS:
                        x = t - 3
                        u = pair * STEPS + x
                        pe.wait_ge(q["y_ready"], u + 2)
                        pe.wait_ge(q["r_ready"], u + 4)
                        pe.matmul(bR[:, :], buf[x // NG][:, 3 * D:4 * D], yT[x % 2][:, :], start=True, stop=True)\
                          .then_inc(q["r_made"], 1)
                    if 0 <= t - 1 < STEPS:
                        x = t - 1
                        u = pair * STEPS + x
                        pe.wait_ge(q["kv_ready"], u + 1)
                        for i in range(GI):
                            ins = pe.matmul(bM[:, i * D:(i + 1) * D], kv[x % 2][:, i, 0:D], kv[x % 2][:, i, D:2 * D],
                                            start=True, stop=True)
                        ins.then_inc(q["m_made"], 1)
                    if t < STEPS:
                        l, g = t // NG, t % NG
                        u = pair * STEPS + t
                        if g == 0:
                            pe.wait_ge(q[f"streamed{l}"], pair * 16 + 16)
                        pe.wait_ge(q["r_ready"], u + 1)
                        pe.wait_ge(q["q_ready"], u + 1)
                        pe.matmul(bQ[:, :], buf[l][:, 0:D], RT[:, g * GT:(g + 1) * GT], start=True, stop=True)\
                          .then_inc(q["q_made"], 1)
                        for i in range(GI):
                            ins = pe.matmul(bK[i // 2][:, (i % 2) * 2 * D:(i % 2 + 1) * 2 * D],
                                            RT[:, (g * GI + i) * T:(g * GI + i + 1) * T], buf[l][:, D:3 * D],
                                            start=True, stop=True)
                        ins.then_inc(q["kv_made"], 1)
            for g in range(NG):
                bank = (bX0, bX1)[g % 2]
                pe.wait_ge(q["r_ready"], LAYERS * NG + 4)
                if g >= 2:
                    pe.wait_ge(q["added"], g - 1)
                for i in range(GI):
                    ins = pe.transpose(bank[:, i * D:(i + 1) * D], RT[:, (g * GI + i) * T:(g * GI + i + 1) * T], ident[:, :])
                ins.then_inc(q["back"], 1)

        @block.scalar
        def _(act):
            act.sem_inc(q["RT_set"], 1)
            act.sem_inc(q["q_ready"], 1)
            act.sem_inc(q["y_ready"], 1)
            with act.Fori(0, NG) as g:
                act.wait_ge(norm.turned, g + 2)
                act.copy(RT[:, bass.ds(g * GT, GT)], bX0[:, :]).then_inc(q["RT_set"], 1)
            with act.Fori(0, LAYERS // 2) as pair:
                for t in range(STEPS + 2):
                    if 0 <= t - 2 < STEPS:
                        x = t - 2
                        act.wait_ge(q["y_made"], pair * STEPS + x + 1)
                        act.copy(yT[x % 2][:, :], bY[:, :]).then_inc(q["y_ready"], 1)
                    if t < STEPS:
                        if t % NG == 0:
                            act.wait_ge(q[f"streamed{t // NG}"], pair * 16 + 16)
                        act.wait_ge(q["q_made"], pair * STEPS + t + 1)
                        act.activation(qT[t % 4][:, :], bQ[:, :], ACT.Identity, bias=buf[t // NG][:, 4 * D:4 * D + 1])\
                           .then_inc(q["q_ready"], 1)

        @block.vector
        def _(dve):
            dve.wait_ge(loaded, count)
            dve.sem_inc(q["r_ready"], 4)
            with dve.Fori(0, NG) as g:
                def src(i):
                    return X[:, g * GI + i, :]
                norm.on_vector_stats(dve, g, src)
                dve.wait_ge(norm.turned, g + 1)
                norm.on_vector_apply(dve, g, src)
            dve.wait_ge(q["RT_set"], NG + 1)
            with dve.Fori(0, LAYERS // 2) as pair:
                for t in range(STEPS + 3):
                    if 0 <= t - 3 < STEPS:
                        x = t - 3
                        u = pair * STEPS + x
                        state = RT[:, (x % NG) * GT:(x % NG + 1) * GT]
                        dve.wait_ge(q["r_made"], u + 1)
                        dve.wait_ge(q["r_ready"], u + 1)
                        dve.scalar_tensor_tensor(out=state, in0=bR[:, :], scalar=buf[x // NG][:, 4 * D + 1:4 * D + 2],
                                                 in1=state, op0=ALU.add, op1=ALU.add).then_inc(q["r_ready"], 1)
                        if x % NG == NG - 1:
                            dve.wait_ge(q["r_ready"], u + 5)
                            dve.sem_inc(q["layer_done"], 1)
                    if 0 <= t - 1 < STEPS:
                        x = t - 1
                        dve.wait_ge(q["m_made"], pair * STEPS + x + 1)
                        dve.tensor_tensor(M[x % 2][:, :].rearrange("p (i d) -> p i d", i=GI),
                                          bM[:, :].rearrange("p (i d) -> p i d", i=GI),
                                          w["blocks"].unsqueeze(1).to_broadcast([D, GI, D]), ALU.mult).then_inc(q["m_ready"], 1)
                    if t < STEPS:
                        bias = buf[t // NG][:, 4 * D + 2:6 * D + 2].unsqueeze(1).to_broadcast([T, 2, 2 * D])
                        if t % NG == 0:
                            dve.wait_ge(q[f"streamed{t // NG}"], pair * 16 + 16)
                        dve.wait_ge(q["kv_made"], pair * STEPS + t + 1)
                        for c in range(2):
                            ins = dve.tensor_tensor(kv[t % 2][:, 2 * c:2 * c + 2, :],
                                                    bK[c][:, :].rearrange("p (i d) -> p i d", i=2), bias, ALU.add)
                        ins.then_inc(q["kv_ready"], 1)
            for g in range(NG):
                x = X[:, g * GI:(g + 1) * GI, :]
                dve.wait_ge(q["back"], g + 1)
                dve.tensor_tensor(x, (bX0, bX1)[g % 2][:, :].rearrange("p (i d) -> p i d", i=GI), x, ALU.add)\
                   .then_inc(q["added"], 1)


def pack_l1a(a):
    head = np.arange(D) // 8
    return {"blocks": (head[:, None] == head[None, :]).astype(np.float32) * np.float32(8.0 ** -0.5)}


def stream_l1a(a):
    wqkv, bqkv = a["L1_attn_Wqkv"].transpose(0, 2, 1), a["L1_attn_bqkv"]
    return {"layers_l1a": np.concatenate([
        wqkv, a["L1_attn_Wproj"].transpose(0, 2, 1), bqkv[:, 0:D, None], a["L1_attn_bproj"][:, :, None],
        np.broadcast_to(bqkv[:, None, D:], (LAYERS, P, 2 * D))], 2)}



PACKS["l2a"] = Pack(("wqkv", D, 3 * D), ("bias", P, 3 * D))


def sublayer_over_sequences(k, s, n):
    nc, X, ident = k.nc, k.X, k.ident
    w, loaded, count = k.weights(n)
    SCALE = float(DH) ** -0.5
    norm = Norm(k, s.sb, s.sem, "ln")
    xT = s.sb("xT", [D, GT])
    qkv = s.sb("qkv", [P, NB, 3 * D])
    S = s.sb("S", [P, NB, H, NB])
    prod = [s.sb(f"prod{i}", [P, NB * D]) for i in range(2)]
    nmax, den, inv = s.sb("nmax", [P, NB * H]), s.sb("den", [P, NB * H]), s.sb("inv", [P, NB * H])
    o = s.sb("o", [P, NB, D])
    b = s.banks(8)
    q = {x: s.sem(x) for x in ("xT_ready qkv_made qkv_ready filled mult reduced maxed shifted expd summed plus_one inverted "
                               "o_mult o_reduced o_scaled").split()}

    with nc.Block() as block:
        @block.sync
        def _(sp):
            k.load(sp, n + 1)

        @block.gpsimd
        def _(pool):
            pool.memset(S[:, :, :, :], -1e30).then_inc(q["filled"], 1)
            with pool.Fori(0, NG) as g:
                norm.on_pool(pool, g)

        @block.tensor
        def _(pe):
            pe.wait_ge(loaded, count)
            with pe.Fori(0, NG) as g:
                pe.wait_ge(q["xT_ready"], g + 1)
                norm.on_tensor(pe, g, b[4])
                pe.wait_ge(q["xT_ready"], g + 2)
                for i in range(GI):
                    pe.wait_ge(q["qkv_ready"], g * GI + i + 1)
                    pe.matmul(b[i][:, 0:3 * D], xT[:, i * T:(i + 1) * T], w["wqkv"], start=True, stop=True)\
                      .then_inc(q["qkv_made"], 1)

        @block.scalar
        def _(act):
            act.sem_inc(q["xT_ready"], 1)
            with act.Fori(0, NG) as g:
                act.wait_ge(norm.turned, g + 1)
                act.copy(xT[:, :], b[4][:, :]).then_inc(q["xT_ready"], 1)
            for i in range(NB):
                act.wait_ge(q["shifted"], i + 1)
                act.activation(S[:, i, :, :], S[:, i, :, :], ACT.Exp, scale=SCALE).then_inc(q["expd"], 1)

        @block.vector
        def _(dve):
            dve.wait_ge(loaded, count)
            dve.sem_inc(q["qkv_ready"], 4)
            with dve.Fori(0, NG) as g:
                def src(i):
                    return X[:, g * GI + i, :]
                norm.on_vector_stats(dve, g, src)
                norm.on_vector_apply(dve, g, src)
                for i in range(GI):
                    dve.wait_ge(q["qkv_made"], g * GI + i + 1)
                    dve.tensor_tensor(qkv[:, bass.ds(g * GI + i, 1), :].rearrange("p o c -> p (o c)"), b[i][:, 0:3 * D],
                                      w["bias"], ALU.add).then_inc(q["qkv_ready"], 1)
            dve.wait_ge(q["qkv_ready"], NB + 4)
            dve.wait_ge(q["filled"], 1)
            for i in range(NB + 1):
                if i < NB:
                    if i >= 2:
                        dve.wait_ge(q["reduced"], i - 1)
                    dve.tensor_tensor(prod[i % 2][:, 0:(i + 1) * D].rearrange("p (j c) -> p j c", c=D),
                                      qkv[:, 0:i + 1, D:2 * D],
                                      qkv[:, i:i + 1, 0:D].to_broadcast([P, i + 1, D]), ALU.mult).then_inc(q["mult"], 1)
                if i >= 1:
                    m = i - 1
                    dve.wait_ge(q["mult"], m + 1)
                    dve.tensor_reduce(S[:, m, :, 0:m + 1].rearrange("p h j -> p j h"),
                                      prod[m % 2][:, 0:(m + 1) * D].rearrange("p (j h d) -> p j h d", h=H, d=DH),
                                      AX.X, ALU.add).then_inc(q["reduced"], 1)
            dve.wait_ge(q["reduced"], NB)
            rows = S[:, :, :, :].rearrange("p i h j -> p (i h) j")
            dve.tensor_reduce(nmax[:, :], rows, AX.X, ALU.max).then_inc(q["maxed"], 1)
            dve.wait_ge(q["maxed"], 1)
            for i in range(NB):
                dve.tensor_tensor(S[:, i, :, :], S[:, i, :, :], nmax[:, i * H:(i + 1) * H].unsqueeze(2).to_broadcast([P, H, NB]),
                                  ALU.subtract).then_inc(q["shifted"], 1)
            dve.wait_ge(q["expd"], NB)
            dve.tensor_reduce(den[:, :], rows, AX.X, ALU.add).then_inc(q["summed"], 1)
            dve.wait_ge(q["summed"], 1)
            dve.tensor_scalar(inv[:, :], den[:, :], 1.0, None, ALU.add).then_inc(q["plus_one"], 1)
            dve.wait_ge(q["plus_one"], 1)
            dve.reciprocal(den[:, :], inv[:, :]).then_inc(q["inverted"], 1)
            dve.wait_ge(q["inverted"], 1)
            for i in range(NB + 1):
                if i < NB:
                    if i >= 2:
                        dve.wait_ge(q["o_reduced"], i - 1)
                    dve.tensor_tensor(prod[i % 2][:, 0:(i + 1) * D].rearrange("p (j h d) -> p j h d", h=H, d=DH),
                                      qkv[:, 0:i + 1, 2 * D:3 * D].rearrange("p j (h d) -> p j h d", h=H),
                                      S[:, i, :, 0:i + 1].rearrange("p h j -> p j h").unsqueeze(3)
                                      .to_broadcast([P, i + 1, H, DH]), ALU.mult).then_inc(q["o_mult"], 1)
                if i >= 1:
                    m = i - 1
                    dve.wait_ge(q["o_mult"], m + 1)
                    dve.tensor_reduce(o[:, m, :], prod[m % 2][:, 0:(m + 1) * D].rearrange("p (j c) -> p c j", c=D),
                                      AX.X, ALU.add).then_inc(q["o_reduced"], 1)
            dve.wait_ge(q["o_reduced"], NB)
            oh = o[:, :, :].rearrange("p i (h d) -> p (i h) d", h=H)
            dve.tensor_tensor(oh, oh, den[:, :].unsqueeze(2).to_broadcast([P, NB * H, DH]), ALU.mult).then_inc(q["o_scaled"], 1)
            dve.wait_ge(q["o_scaled"], 1)
            dve.tensor_tensor(X[:, :, :], X[:, :, :], o[:, :, :], ALU.add)


def pack_l2a(a):
    bias = np.concatenate([a["L2_attn_bq"], a["L2_attn_bk"], a["L2_attn_bv"]])
    return {"wqkv": np.concatenate([a["L2_attn_Wq"].T, a["L2_attn_Wk"].T, a["L2_attn_Wv"].T], 1),
            "bias": np.broadcast_to(bias[None], (P, 3 * D))}



FF = 4 * D
FC = FF // P
PACKS["l1f"] = Pack(("router", D, 8), ("b2", 8, D))
PACKS["l0f"] = Pack(("router", D, 4), ("ln2_w", D, 1), ("ln2_b", D, 1))
PACKS["l2f"] = Pack(("router", D, 8), ("b2", 9, D), ("gate_bias", P, 8))
EXPERT_COLS = {"l0f": 3 * FF, "l1f": 2 * FF + FC, "l2f": 2 * FF + FC}


class Moe:

    def __init__(self, k, s, n, kind):
        self.k, self.s, self.n, self.kind = k, s, n, kind
        self.w, self.loaded, self.count = k.weights(n)
        self.gated = kind == "l0f"
        self.shared = kind == "l2f"
        self.NR = 4 if self.gated else 8
        self.NE = self.NR + self.shared
        self.stream = k.dram["experts_" + kind]
        sb = s.sb
        self.xg = sb("xg", [D, GT])
        self.xT = sb("xT", [D, NB * T])
        self.W = sb("W", [T, NB, self.NE])
        self.Wg = sb("Wg", [T, GI, self.NE])
        self.sc = sb("sc", [T, GI, 8])
        self.mx = sb("mx", [T, GI, 8])
        self.ix = sb("ix", [T, GI, 8], U32)
        self.idf = sb("idf", [T, GI, 2])
        self.den = sb("den", [T, GI])
        self.inv = sb("inv", [T, GI])
        self.w2top = sb("w2top", [T, GI, 2])
        self.oh = sb("oh", [T, GI * 2, 8])
        self.ohw = sb("ohw", [T, GI * 2, 8])
        self.wT = sb("wT", [self.NE, GT])
        self.buf = [sb(f"expert{i}", [P, EXPERT_COLS[kind]]) for i in range(2)]
        self.a = sb("a", [P, 2, FC, GT])
        self.sg = sb("sg", [P, 2, GT]) if self.gated else None
        self.banks = s.banks(8)
        names = ("logits_made lg_ready sc_ready best indexed idf_ready den_ready den2_ready inv_ready w_ready oh_ready "
                 "ohw_ready Wg_ready W_turned wT_ready bias_made xg_ready xg_used xT_ready diff_ready e_ready X_set "
                 "streamed0 streamed1 expert_done up gated silud downed added moved")
        self.q = {x: s.sem(x) for x in names.split()}
        self.norm = Norm(k, sb, s.sem, "ln2")


    def setup_pool(self, pool, g):
        q = self.q
        self.norm.on_pool(pool, g)
        pool.wait_ge(q["xg_ready"], g + 1)
        pool.tensor_copy(self.xT[:, bass.ds(g * GT, GT)], self.xg[:, :]).then_inc(q["xT_ready"], 1)

    def setup_tensor(self, pe, g):
        q, b = self.q, self.banks
        self.norm.on_tensor(pe, g, b[0])
        pe.wait_ge(q["xg_ready"], g + 1)
        for i in range(GI):
            ins = pe.matmul(b[1][:, i * 8:i * 8 + self.NR], self.xg[:, i * T:(i + 1) * T], self.w["router"],
                            start=True, stop=True)
        ins.then_inc(q["logits_made"], 1)
        if self.gated:
            return
        pe.wait_ge(q["Wg_ready"], g + 1)
        for i in range(GI):
            ins = pe.transpose(b[2][0:self.NE, i * T:(i + 1) * T], self.Wg[:, i, :], self.k.ident[:, :])
        ins.then_inc(q["W_turned"], 1)
        pe.wait_ge(q["wT_ready"], g + 1)
        for i in range(GI):
            ins = pe.matmul(b[3][:, i * D:(i + 1) * D], self.wT[:, i * T:(i + 1) * T], self.w["b2"], start=True, stop=True)
        ins.then_inc(q["bias_made"], 1)

    def setup_scalar(self, act, g):
        q, b = self.q, self.banks
        act.wait_ge(self.norm.turned, g + 1)
        act.wait_ge(q["xT_ready"], g + 1)
        if self.gated:
            act.activation(self.xg[:, :], b[0][:, :], ACT.Identity, scale=self.w["ln2_w"], bias=self.w["ln2_b"])\
               .then_inc(q["xg_ready"], 1)
            return
        act.copy(self.xg[:, :], b[0][:, :]).then_inc(q["xg_ready"], 1)
        if self.shared:
            act.wait_ge(q["lg_ready"], g + 1)
            act.activation(self.sc[:, :, :], self.oh[:, 0:GI, :], ACT.Sigmoid).then_inc(q["sc_ready"], 1)
        else:
            act.wait_ge(q["diff_ready"], g + 1)
            act.activation(self.inv[:, :], self.den[:, :], ACT.Exp).then_inc(q["e_ready"], 1)
        act.wait_ge(q["W_turned"], g + 1)
        act.copy(self.wT[:, :], b[2][0:self.NE, :]).then_inc(q["wT_ready"], 1)

    def route_vector(self, dve, g):
        q, k, b = self.q, self.k, self.banks
        lg = b[1][:, 0:GI * 8].rearrange("p (i e) -> p i e", i=GI)
        NR = self.NR
        dve.wait_ge(q["logits_made"], g + 1)
        if self.shared:
            dve.tensor_tensor(self.oh[:, 0:GI, :], lg, self.w["gate_bias"].unsqueeze(1).to_broadcast([P, GI, 8]), ALU.add)\
               .then_inc(q["lg_ready"], 1)
            k.wait_alone(dve, q["sc_ready"], g + 1)
        else:
            dve.tensor_copy(self.sc[:, :, 0:NR], lg[:, :, 0:NR]).then_inc(q["lg_ready"], 1)
            k.wait_alone(dve, q["lg_ready"], g + 1)
        for i in range(GI):
            ins = dve.max(self.mx[:, i, :], self.sc[:, i, :])
        ins.then_inc(q["best"], 1)
        k.wait_alone(dve, q["best"], g + 1)
        for i in range(GI):
            ins = dve.max_index(self.ix[:, i, :], self.mx[:, i, :], self.sc[:, i, :])
        ins.then_inc(q["indexed"], 1)
        k.wait_alone(dve, q["indexed"], g + 1)
        dve.tensor_copy(self.idf[:, :, :], self.ix[:, :, 0:2]).then_inc(q["idf_ready"], 1)
        iota8 = self.k.iota[:, 0:8]
        if self.gated:
            dve.wait_ge(q["idf_ready"], g + 1)
            dve.tensor_tensor(self.W[:, bass.ds(g * GI, GI), :], iota8[:, 0:NR].unsqueeze(1).to_broadcast([P, GI, NR]),
                              self.idf[:, :, 0:1].to_broadcast([P, GI, NR]), ALU.is_equal).then_inc(q["moved"], 1)
            rows = bass.ds(g * GI, GI)
            dve.tensor_tensor(self.k.X[:, rows, :], self.k.X[:, rows, :], self.k.Z[:, rows, :], ALU.add)\
               .then_inc(q["X_set"], 1)
            return
        best, second = self.mx[:, :, 0], self.mx[:, :, 1]
        if self.shared:
            dve.tensor_tensor(self.den[:, :], best, second, ALU.add).then_inc(q["den_ready"], 1)
            k.wait_alone(dve, q["den_ready"], g + 1)
            dve.tensor_scalar(self.den[:, :], self.den[:, :], 1e-6, None, ALU.add).then_inc(q["den2_ready"], 1)
            k.wait_alone(dve, q["den2_ready"], g + 1)
            dve.reciprocal(self.inv[:, :], self.den[:, :]).then_inc(q["inv_ready"], 1)
            dve.wait_ge(q["inv_ready"], g + 1)
            dve.tensor_tensor(self.w2top[:, :, :], self.mx[:, :, 0:2], self.inv[:, :].unsqueeze(2).to_broadcast([P, GI, 2]),
                              ALU.mult).then_inc(q["w_ready"], 1)
        else:
            dve.tensor_tensor(self.den[:, :], second, best, ALU.subtract).then_inc(q["diff_ready"], 1)
            k.wait_alone(dve, q["e_ready"], g + 1)
            dve.tensor_scalar(self.den[:, :], self.inv[:, :], 1.0, None, ALU.add).then_inc(q["den2_ready"], 1)
            k.wait_alone(dve, q["den2_ready"], g + 1)
            dve.reciprocal(self.w2top[:, :, 0], self.den[:, :]).then_inc(q["inv_ready"], 1)
            dve.wait_ge(q["inv_ready"], g + 1)
            dve.tensor_tensor(self.w2top[:, :, 1], self.w2top[:, :, 0], self.inv[:, :], ALU.mult).then_inc(q["w_ready"], 1)
        top = self.w2top[:, :, :].rearrange("p i r -> p (i r)").unsqueeze(2).to_broadcast([P, GI * 2, 8])
        idx = self.idf[:, :, :].rearrange("p i r -> p (i r)").unsqueeze(2).to_broadcast([P, GI * 2, 8])
        dve.wait_ge(q["idf_ready"], g + 1)
        if self.shared:
            dve.wait_ge(q["sc_ready"], g + 1)
        dve.tensor_tensor(self.oh[:, :, :], iota8.unsqueeze(1).to_broadcast([P, GI * 2, 8]), idx, ALU.is_equal)\
           .then_inc(q["oh_ready"], 1)
        dve.wait_ge(q["oh_ready"], g + 1)
        dve.wait_ge(q["w_ready"], g + 1)
        dve.tensor_tensor(self.ohw[:, :, :], self.oh[:, :, :], top, ALU.mult).then_inc(q["ohw_ready"], 1)
        dve.wait_ge(q["ohw_ready"], g + 1)
        pair = self.ohw[:, :, :].rearrange("p (i r) e -> p i r e", r=2)
        dve.tensor_tensor(self.Wg[:, :, 0:NR], pair[:, :, 0, :], pair[:, :, 1, :], ALU.add).then_inc(q["Wg_ready"], 1)
        dve.wait_ge(q["Wg_ready"], g + 1)
        dve.tensor_copy(self.W[:, bass.ds(g * GI, GI), :], self.Wg[:, :, :]).then_inc(q["moved"], 1)
        dve.wait_ge(q["bias_made"], g + 1)
        dve.tensor_tensor(self.k.X[:, bass.ds(g * GI, GI), :], b[3][:, :].rearrange("p (i d) -> p i d", i=GI),
                          self.k.X[:, bass.ds(g * GI, GI), :], ALU.add).then_inc(q["X_set"], 1)

    def prime_vector(self, dve):
        q = self.q
        if self.gated:
            dve.memset(self.sc[:, :, :], -3e38).then_inc(q["moved"], 1)
        if self.shared:
            dve.memset(self.Wg[:, :, 8:9], 0.1).then_inc(q["moved"], 1)
        if self.gated or self.shared:
            dve.wait_ge(q["moved"], 1)


    def expert_sync(self, sp, e, b, pair):
        q = self.q
        sp.wait_ge(q["expert_done"], e + 1)
        sp.dma_start(self.buf[b][:, :], self.stream[bass.ds(e, 1), :, :].rearrange("o p c -> (o p) c"))\
          .then_inc(q[f"streamed{b}"], 16)

    def up_tensor(self, pe, u, g, b):
        q = self.q
        for c in range(FC):
            x = self.xT[:, g * GT:(g + 1) * GT]
            if self.gated:
                pe.wait_ge(q["gated"], u * FC + c + 1)
                j = 2 * (c % 2)
                pe.matmul(self.banks[j][:, :], self.buf[b][:, c * P:(c + 1) * P], x, start=True, stop=True)
                pe.matmul(self.banks[j + 1][:, :], self.buf[b][:, FF + c * P:FF + (c + 1) * P], x, start=True, stop=True)\
                  .then_inc(q["up"], 1)
            else:
                pe.wait_ge(q["gated"], u * FC + c + 1)
                pe.matmul(self.banks[c][:, :], self.buf[b][:, c * P:(c + 1) * P], x, start=True, stop=True)\
                  .then_inc(q["up"], 1)

    def down_tensor(self, pe, u, g, b, last):
        q, par = self.q, g % 2
        w2 = self.buf[b][:, (2 * FF if self.gated else FF):(3 * FF if self.gated else 2 * FF)].rearrange("p (c d) -> p c d", c=FC)
        out = self.banks[4 + par]
        pe.wait_ge(q["gated"], u * FC + FC + (2 if self.gated else 4))
        pe.wait_ge(q["added"], u + 3)
        for i in range(GI):
            for c in range(FC):
                ins = pe.matmul(out[:, i * D:(i + 1) * D], self.a[:, par, c, i * T:(i + 1) * T], w2[:, c, :],
                                start=(c == 0), stop=(c == FC - 1))
        ins.then_inc(q["downed"], 1)
        if last:
            pe.wait_ge(q["downed"], u + 3)
            pe.sem_inc(q["expert_done"], 1)

    def expert_tensor(self, pe, e, b, pair):
        pe.wait_ge(self.q[f"streamed{b}"], pair * 16 + 16)
        self.up_tensor(pe, e * NG, 0, b)
        for g in range(1, NG):
            self.up_tensor(pe, e * NG + g, g, b)
            self.down_tensor(pe, e * NG + g - 1, g - 1, b, False)
        self.down_tensor(pe, e * NG + NG - 1, NG - 1, b, True)

    def expert_scalar(self, act, e, b, pair):
        q = self.q
        for g in range(NG):
            u, par = e * NG + g, g % 2
            act.wait_ge(q["downed"], u + 1)
            for c in range(FC):
                act.wait_ge(q["up"], u * FC + c + 1)
                if self.gated:
                    act.wait_ge(q["gated"], u * FC + c + 1)
                    act.activation(self.sg[:, c % 2, :], self.banks[2 * (c % 2)][:, :], ACT.Silu).then_inc(q["silud"], 1)
                else:
                    act.activation(self.a[:, par, c, :], self.banks[c][:, :], ACT.Gelu,
                                   bias=self.buf[b][:, 2 * FF + c:2 * FF + c + 1]).then_inc(q["gated"], 1)

    def expert_vector(self, dve, e, b, pair):
        q, X = self.q, self.k.X
        for g in range(NG + 1):
            u = e * NG + g
            if g < NG and self.gated:
                dve.wait_ge(q["downed"], u + 1)
                for c in range(FC):
                    dve.wait_ge(q["silud"], u * FC + c + 1)
                    dve.tensor_tensor(self.a[:, g % 2, c, :], self.sg[:, c % 2, :], self.banks[2 * (c % 2) + 1][:, :],
                                      ALU.mult).then_inc(q["gated"], 1)
            if g >= 1:
                u, h = u - 1, g - 1
                dve.wait_ge(q["added"], u + 1)
                dve.wait_ge(q["downed"], u + 3)
                for i in range(GI):
                    x = X[:, h * GI + i, :]
                    ins = dve.scalar_tensor_tensor(out=x, in0=self.banks[4 + h % 2][:, i * D:(i + 1) * D],
                                                   scalar=self.W[:, h * GI + i, bass.ds(e, 1)], in1=x,
                                                   op0=ALU.mult, op1=ALU.add)
                ins.then_inc(q["added"], 1)


    def experts(self, eng, one):
        with eng.Fori(0, self.NR // 2) as pair:
            for b in range(2):
                one(eng, pair * 2 + b, b, pair)
        if self.shared:
            one(eng, self.NR, 0, self.NR // 2)


def sublayer_moe(k, s, n):
    m = Moe(k, s, n, UNITS[n])
    q, X = m.q, k.X
    with k.nc.Block() as block:
        @block.sync
        def _(sp):
            k.load(sp, n + 1)
            sp.sem_inc(q["expert_done"], 2)
            m.experts(sp, m.expert_sync)

        @block.gpsimd
        def _(pool):
            pool.sem_inc(q["xT_ready"], 1)
            with pool.Fori(0, NG) as g:
                m.setup_pool(pool, g)

        @block.tensor
        def _(pe):
            pe.wait_ge(m.loaded, m.count)
            pe.sem_inc(q["downed"], 2)
            with pe.Fori(0, NG) as g:
                m.setup_tensor(pe, g)
            pe.wait_ge(q["X_set"], NG)
            pe.wait_ge(q["xT_ready"], NG + 1)
            m.experts(pe, m.expert_tensor)

        @block.scalar
        def _(act):
            act.wait_ge(m.loaded, m.count)
            if not m.gated:
                act.sem_inc(q["gated"], 4)
            with act.Fori(0, NG) as g:
                m.setup_scalar(act, g)
            m.experts(act, m.expert_scalar)

        @block.vector
        def _(dve):
            dve.wait_ge(m.loaded, m.count)
            m.prime_vector(dve)
            dve.sem_inc(q["added"], 4)
            if m.gated:
                dve.sem_inc(q["gated"], 2)
            with dve.Fori(0, NG) as g:
                def src(i):
                    return (k.Z if m.gated else X)[:, g * GI + i, :]
                m.norm.on_vector_stats(dve, g, src)
                m.norm.on_vector_apply(dve, g, src)
                m.route_vector(dve, g)
            dve.wait_ge(q["X_set"], NG)
            dve.wait_ge(q["moved"], NG + (m.shared or m.gated))
            m.experts(dve, m.expert_vector)


def expert_arrays(w1, b1, w2):
    e = w1.shape[0]
    return np.concatenate([w1.transpose(0, 2, 1), w2.transpose(0, 2, 1).reshape(e, FC, P, D).transpose(0, 2, 1, 3).reshape(e, P, FF),
                           b1.reshape(e, FC, P).transpose(0, 2, 1)], 2)


def pack_l1f(a):
    return {"router": a["L1_ffn_router_w"].T, "b2": a["L1_ffn_b2"]}


def stream_l1f(a):
    return {"experts_l1f": expert_arrays(a["L1_ffn_w1"], a["L1_ffn_b1"], a["L1_ffn_w2"])}


def pack_l2f(a):
    return {"router": a["L2_ffn_gate_w"].T, "b2": np.concatenate([a["L2_ffn_bd"], a["L2_ffn_sbd"][None]], 0),
            "gate_bias": np.broadcast_to(a["L2_ffn_gate_bias"][None], (P, 8))}


def stream_l2f(a):
    return {"experts_l2f": expert_arrays(np.concatenate([a["L2_ffn_Wu"], a["L2_ffn_sWu"][None]], 0),
                                         np.concatenate([a["L2_ffn_bu"], a["L2_ffn_sbu"][None]], 0),
                                         np.concatenate([a["L2_ffn_Wd"], a["L2_ffn_sWd"][None]], 0))}
def pack_l0f(a):
    return {"router": a["L0_ffn_router_w"], "ln2_w": a["L0_ffn_ln2_w"], "ln2_b": a["L0_ffn_ln2_b"]}


def stream_l0f(a):
    proj = a["L0_ffn_expert_proj"].reshape(4, FC, P, D).transpose(0, 2, 1, 3).reshape(4, P, FF)
    return {"experts_l0f": np.concatenate([a["L0_ffn_expert_wv"], proj], 2)}



L3 = 2
EH, ED = 8, 16
INTER = 352
IC = -(-INTER // P)
RMS_EPS = 1e-6
QKVB = 3 * D + EH
MIX_COLS = QKVB + D + 2
FFN_COLS = 2 * INTER + IC * D + 1
PACKS["l3a"] = Pack(("final", P, D))


class RmsNorm:

    def __init__(self, k, sb, sem, tag):
        self.k = k
        self.sq = sb(f"{tag}_sq", [P, GI, D])
        self.ss, self.me, self.rs = sb(f"{tag}_ss", [P, GI]), sb(f"{tag}_me", [P, GI]), sb(f"{tag}_rs", [P, GI])
        self.xn = sb(f"{tag}_xn", [P, GI, D])
        self.squared, self.mean, self.root = sem(f"{tag}_squared"), sem(f"{tag}_mean"), sem(f"{tag}_root")
        self.ready, self.turned = sem(f"{tag}_ready"), sem(f"{tag}_turned")

    def on_scalar(self, act, src):
        for i in range(GI):
            ins = act.activation(self.sq[:, i, :], src(i), ACT.Square, accum_out=self.ss[:, i:i + 1])
        ins.then_inc(self.squared, 1)

    def on_pool(self, pool, n):
        self.k.wait_alone(pool, self.squared, n + 1)
        pool.tensor_scalar(self.me[:, :], self.ss[:, :], 1.0 / D, RMS_EPS, ALU.mult, ALU.add).then_inc(self.mean, 1)
        pool.wait_ge(self.mean, n + 1)
        pool.tensor_tensor(self.rs[:, :], self.me[:, :], self.k.half[:, 0:GI], ALU.pow).then_inc(self.root, 1)

    def on_vector(self, dve, n, src):
        dve.wait_ge(self.root, n + 1)
        for i in range(GI):
            ins = dve.tensor_scalar(self.xn[:, i, :], src(i), self.rs[:, i:i + 1], None, ALU.mult)
        ins.then_inc(self.ready, 1)

    def on_tensor(self, pe, n, bank):
        pe.wait_ge(self.ready, n + 1)
        for i in range(GI):
            ins = pe.transpose(bank[:, i * T:(i + 1) * T], self.xn[:, i, :], self.k.ident[:, :])
        ins.then_inc(self.turned, 1)


def sublayer_delta(k, s, n):
    nc, X, ident, Y = k.nc, k.X, k.ident, k.Z
    w, loaded, count = k.weights(n)
    sb = s.sb
    ln = Norm(k, sb, s.sem, "ln")
    n1, n2, nf = (RmsNorm(k, sb, s.sem, x) for x in ("n1", "n2", "nf"))
    mix, ffn = sb("mix", [P, MIX_COLS]), sb("ffn", [P, FFN_COLS])
    wqkvb, wo = mix[:, 0:QKVB], mix[:, QKVB:QKVB + D]
    gain1, gaino = mix[:, QKVB + D:QKVB + D + 1], mix[:, QKVB + D + 1:QKVB + D + 2]
    wd = ffn[:, 2 * INTER:2 * INTER + IC * D].rearrange("p (c d) -> p c d", c=IC)
    gain2 = ffn[:, FFN_COLS - 1:FFN_COLS]
    hT = sb("hT", [D, GT])
    qkv = sb("qkv", [P, NB, 3 * D])
    bl, beta = sb("bl", [P, NB, EH]), sb("beta", [P, NB, EH])
    sqk = sb("sqk", [P, NB, 2 * D])
    ss2, me2, rs2 = (sb(x, [P, NB * 2 * EH]) for x in ("ss2", "me2", "rs2"))
    kprod = [sb(f"kprod{i}", [P, NB * D]) for i in range(2)]
    qprod = [sb(f"qprod{i}", [P, NB * D]) for i in range(2)]
    GK, GQ = sb("GK", [P, NB, NB, EH]), sb("GQ", [P, NB, NB, EH])
    U, pred, o = sb("U", [P, NB, D]), sb("pred", [P, D]), sb("o", [P, NB, D])
    sso, meo, rso = (sb(x, [P, NB * EH]) for x in ("sso", "meo", "rso"))
    on = sb("on", [P, GI, D])
    oT = sb("oT", [D, GT])
    sg = sb("sg", [P, 2, GT])
    a = sb("a", [P, IC, GT])
    b = s.banks(8)
    q = {x: s.sem(x) for x in (
        "Y_ready mix_loaded ffn_loaded mix_done ffn_done hT_ready qkv_made silud beta_half beta_ready sq_ready ss_ready me_ready "
        "rs_ready unit kk_mult kk_ready qk_mult qk_ready p_mult p_ready diff u_ready o_mult o_ready osq oss ome ors onormed "
        "o_turned oT_ready out_made hT2_ready up gsilu gated down final_w added").split()}

    def heads(x):
        return x.rearrange("p n (h d) -> p n h d", h=EH)

    with nc.Block() as block:
        @block.sync
        def _(sp):
            k.load(sp, n + 1)
            with sp.Fori(0, L3) as l:
                sp.wait_ge(q["mix_done"], l + 1)
                sp.dma_start(mix[:, :], k.dram["mix_l3a"][bass.ds(l, 1), :, :].rearrange("o p c -> (o p) c"))\
                  .then_inc(q["mix_loaded"], 16)
                sp.wait_ge(q["ffn_done"], l + 1)
                sp.dma_start(ffn[:, :], k.dram["ffn_l3a"][bass.ds(l, 1), :, :].rearrange("o p c -> (o p) c"))\
                  .then_inc(q["ffn_loaded"], 16)

        @block.gpsimd
        def _(pool):
            pool.sem_inc(q["qk_mult"], 1)
            pool.sem_inc(q["o_mult"], 1)
            with pool.Fori(0, NG) as g:
                ln.on_pool(pool, g)
            with pool.Fori(0, L3) as l:
                with pool.Fori(0, NG) as g:
                    n1.on_pool(pool, l * NG + g)
                k.wait_alone(pool, q["ss_ready"], l + 1)
                pool.tensor_scalar(me2[:, :], ss2[:, :], RMS_EPS, None, ALU.add).then_inc(q["me_ready"], 1)
                pool.wait_ge(q["me_ready"], l + 1)
                pool.tensor_tensor(rs2[:, :], me2[:, :], k.half[:, 0:1].to_broadcast([P, NB * 2 * EH]), ALU.pow)\
                    .then_inc(q["rs_ready"], 1)
                pool.wait_ge(q["unit"], l + 1)
                for i in range(NB):
                    pool.wait_ge(q["qk_ready"], l * NB + i + 1)
                    pool.tensor_tensor(qprod[i % 2][:, 0:(i + 1) * D].rearrange("p (j c) -> p j c", c=D),
                                       qkv[:, 0:i + 1, D:2 * D], qkv[:, i:i + 1, 0:D].to_broadcast([P, i + 1, D]), ALU.mult)\
                        .then_inc(q["qk_mult"], 1)
                for i in range(NB):
                    pool.wait_ge(q["o_ready"], l * NB + i + 1)
                    if i < 2:
                        pool.wait_ge(q["qk_ready"], l * NB + NB + 2)
                    pool.wait_ge(q["u_ready"], l * NB + i + 1)
                    pool.tensor_tensor(heads(qprod[i % 2][:, 0:(i + 1) * D].rearrange("p (j c) -> p j c", c=D)),
                                       heads(U[:, 0:i + 1, :]),
                                       GQ[:, i, 0:i + 1, :].unsqueeze(3).to_broadcast([P, i + 1, EH, ED]), ALU.mult)\
                        .then_inc(q["o_mult"], 1)
                k.wait_alone(pool, q["oss"], l + 1)
                pool.tensor_scalar(meo[:, :], sso[:, :], 1.0 / ED, RMS_EPS, ALU.mult, ALU.add).then_inc(q["ome"], 1)
                pool.wait_ge(q["ome"], l + 1)
                pool.tensor_tensor(rso[:, :], meo[:, :], k.half[:, 0:1].to_broadcast([P, NB * EH]), ALU.pow).then_inc(q["ors"], 1)
                with pool.Fori(0, NG) as g:
                    n2.on_pool(pool, l * NG + g)
            with pool.Fori(0, NG) as g:
                nf.on_pool(pool, g)

        @block.tensor
        def _(pe):
            pe.sem_inc(q["mix_done"], 1)
            pe.sem_inc(q["ffn_done"], 1)
            pe.sem_inc(q["down"], 1)
            pe.sem_inc(q["o_turned"], 1)
            with pe.Fori(0, L3) as l:
                k.wait_alone(pe, q["mix_loaded"], l * 16 + 16)
                with pe.Fori(0, NG) as g:
                    m = l * NG + g
                    n1.on_tensor(pe, m, b[4])
                    pe.wait_ge(q["hT_ready"], m + 1)
                    for i in range(GI):
                        pe.wait_ge(q["silud"], m * GI + i + 1)
                        pe.matmul(b[i][:, 0:QKVB], hT[:, i * T:(i + 1) * T], wqkvb, start=True, stop=True)\
                          .then_inc(q["qkv_made"], 1)
                with pe.Fori(0, NG) as g:
                    m = l * NG + g
                    pe.wait_ge(q["onormed"], m + 1)
                    pe.wait_ge(q["oT_ready"], m + 1)
                    for i in range(GI):
                        ins = pe.transpose(b[4][:, i * T:(i + 1) * T], on[:, i, :], ident[:, :])
                    ins.then_inc(q["o_turned"], 1)
                    pe.wait_ge(q["oT_ready"], m + 2)
                    pe.wait_ge(q["Y_ready"], NG + l * 2 * NG + g)
                    for i in range(GI):
                        ins = pe.matmul(b[5][:, i * D:(i + 1) * D], oT[:, i * T:(i + 1) * T], wo, start=True, stop=True)
                    ins.then_inc(q["out_made"], 1)
                pe.wait_ge(q["Y_ready"], NG + l * 2 * NG + NG)
                pe.sem_inc(q["mix_done"], 1)
                k.wait_alone(pe, q["ffn_loaded"], l * 16 + 16)
                with pe.Fori(0, NG) as g:
                    m = l * NG + g
                    n2.on_tensor(pe, m, b[4])
                    pe.wait_ge(q["hT2_ready"], m + 1)
                    for c in range(IC):
                        f = min(P, INTER - c * P)
                        pe.wait_ge(q["gated"], m * IC + c + 1)
                        pe.matmul(b[2 * (c % 2)][0:f, :], ffn[:, c * P:c * P + f], hT[:, :], start=True, stop=True)
                        pe.matmul(b[2 * (c % 2) + 1][0:f, :], ffn[:, INTER + c * P:INTER + c * P + f], hT[:, :],
                                  start=True, stop=True).then_inc(q["up"], 1)
                    pe.wait_ge(q["gated"], m * IC + IC + 2)
                    pe.wait_ge(q["Y_ready"], 2 * NG + l * 2 * NG + g)
                    for i in range(GI):
                        for c in range(IC):
                            f = min(P, INTER - c * P)
                            ins = pe.matmul(b[5][:, i * D:(i + 1) * D], a[0:f, c, i * T:(i + 1) * T], wd[0:f, c, :],
                                            start=(c == 0), stop=(c == IC - 1))
                    ins.then_inc(q["down"], 1)
                pe.wait_ge(q["Y_ready"], 3 * NG + l * 2 * NG)
                pe.sem_inc(q["ffn_done"], 1)

        @block.scalar
        def _(act):
            act.sem_inc(q["silud"], 4)
            act.sem_inc(q["oT_ready"], 1)
            with act.Fori(0, L3) as l:
                with act.Fori(0, NG) as g:
                    m = l * NG + g
                    act.wait_ge(q["Y_ready"], l * 2 * NG + g + 1)
                    n1.on_scalar(act, lambda i: Y[:, g * GI + i, :])
                    act.wait_ge(q["mix_loaded"], l * 16 + 16)
                    act.wait_ge(n1.turned, m + 1)
                    act.activation(hT[:, :], b[4][:, :], ACT.Copy, scale=gain1).then_inc(q["hT_ready"], 1)
                    for i in range(GI):
                        act.wait_ge(q["qkv_made"], m * GI + i + 1)
                        act.activation(qkv[:, bass.ds(g * GI + i, 1), :].rearrange("p o c -> p (o c)"), b[i][:, 0:3 * D], ACT.Silu)
                        act.copy(bl[:, bass.ds(g * GI + i, 1), :].rearrange("p o c -> p (o c)"), b[i][:, 3 * D:QKVB])\
                           .then_inc(q["silud"], 1)
                act.wait_ge(q["silud"], l * NB + NB + 4)
                act.activation(sqk[:, :, :], qkv[:, :, 0:2 * D], ACT.Square).then_inc(q["sq_ready"], 1)
                act.activation(beta[:, :, :], bl[:, :, :], ACT.Sigmoid).then_inc(q["beta_half"], 1)
                act.wait_ge(q["o_ready"], l * NB + NB + 2)
                act.activation(sqk[:, :, 0:D], o[:, :, :], ACT.Square).then_inc(q["osq"], 1)
                with act.Fori(0, NG) as g:
                    m = l * NG + g
                    act.wait_ge(q["o_turned"], m + 2)
                    act.activation(oT[:, :], b[4][:, :], ACT.Copy, scale=gaino).then_inc(q["oT_ready"], 1)
                act.wait_ge(q["ffn_loaded"], l * 16 + 16)
                with act.Fori(0, NG) as g:
                    m = l * NG + g
                    act.wait_ge(q["Y_ready"], NG + l * 2 * NG + g + 1)
                    n2.on_scalar(act, lambda i: Y[:, g * GI + i, :])
                    act.wait_ge(n2.turned, m + 1)
                    act.activation(hT[:, :], b[4][:, :], ACT.Copy, scale=gain2).then_inc(q["hT2_ready"], 1)
                    for c in range(IC):
                        f = min(P, INTER - c * P)
                        act.wait_ge(q["up"], m * IC + c + 1)
                        act.wait_ge(q["gated"], m * IC + c + 1)
                        act.activation(sg[0:f, c % 2, :], b[2 * (c % 2)][0:f, :], ACT.Silu).then_inc(q["gsilu"], 1)
            with act.Fori(0, NG) as g:
                act.wait_ge(q["Y_ready"], NG + L3 * 2 * NG)
                act.wait_ge(nf.ready, g + 1)
                nf.on_scalar(act, lambda i: Y[:, g * GI + i, :])

        @block.vector
        def _(dve):
            dve.wait_ge(loaded, count)
            dve.sem_inc(q["gated"], 2)
            dve.sem_inc(q["qk_ready"], 2)
            dve.sem_inc(q["o_ready"], 2)
            dve.sem_inc(nf.ready, 1)
            with dve.Fori(0, NG) as g:
                def src(i):
                    return X[:, g * GI + i, :]
                ln.on_vector_stats(dve, g, src)
                ln.on_vector_apply(dve, g, src)
                dve.wait_ge(ln.ready, g + 1)
                dve.tensor_copy(Y[:, bass.ds(g * GI, GI), :], ln.xn[:, :, :]).then_inc(q["Y_ready"], 1)
            with dve.Fori(0, L3) as l:
                with dve.Fori(0, NG) as g:
                    n1.on_vector(dve, l * NG + g, lambda i: Y[:, g * GI + i, :])
                dve.wait_ge(q["sq_ready"], l + 1)
                dve.tensor_reduce(ss2[:, :], sqk[:, :, :].rearrange("p n (h d) -> p (n h) d", d=ED), AX.X, ALU.add)\
                   .then_inc(q["ss_ready"], 1)
                k.wait_alone(dve, q["beta_half"], l + 1)
                dve.tensor_scalar(beta[:, :, :], beta[:, :, :], 2.0, None, ALU.mult).then_inc(q["beta_ready"], 1)
                dve.wait_ge(q["rs_ready"], l + 1)
                qk = qkv[:, :, 0:2 * D].rearrange("p n (h d) -> p n h d", d=ED)
                dve.tensor_tensor(qk, qk, rs2[:, :].rearrange("p (n h) -> p n h", n=NB).unsqueeze(3)
                                  .to_broadcast([P, NB, 2 * EH, ED]), ALU.mult).then_inc(q["unit"], 1)
                dve.wait_ge(q["unit"], l + 1)
                for i in range(NB + 1):
                    if 1 <= i < NB:
                        if i >= 3:
                            dve.wait_ge(q["kk_ready"], l * (NB - 1) + i - 2)
                        dve.tensor_tensor(kprod[i % 2][:, 0:i * D].rearrange("p (j c) -> p j c", c=D),
                                          qkv[:, 0:i, D:2 * D], qkv[:, i:i + 1, D:2 * D].to_broadcast([P, i, D]), ALU.mult)\
                           .then_inc(q["kk_mult"], 1)
                    if i >= 2:
                        j = i - 1
                        dve.wait_ge(q["kk_mult"], l * (NB - 1) + j)
                        dve.tensor_reduce(GK[:, j, 0:j, :], kprod[j % 2][:, 0:j * D].rearrange("p (j h d) -> p j h d", h=EH, d=ED),
                                          AX.X, ALU.add).then_inc(q["kk_ready"], 1)
                    if i >= 1:
                        j = i - 1
                        dve.wait_ge(q["qk_mult"], l * NB + j + 2)
                        dve.tensor_reduce(GQ[:, j, 0:j + 1, :],
                                          qprod[j % 2][:, 0:(j + 1) * D].rearrange("p (j h d) -> p j h d", h=EH, d=ED),
                                          AX.X, ALU.add).then_inc(q["qk_ready"], 1)

                def output(i):
                    dve.wait_ge(q["o_mult"], l * NB + i + 2)
                    dve.tensor_reduce(o[:, i, :], qprod[i % 2][:, 0:(i + 1) * D].rearrange("p (j c) -> p c j", c=D),
                                      AX.X, ALU.add).then_inc(q["o_ready"], 1)

                dve.wait_ge(q["kk_ready"], l * (NB - 1) + NB - 1)
                dve.wait_ge(q["beta_ready"], l + 1)
                for i in range(NB):
                    v, bi = qkv[:, i, 2 * D:3 * D], beta[:, i, :].unsqueeze(2).to_broadcast([P, EH, ED])
                    u = U[:, i, :].rearrange("p (h d) -> p h d", h=EH)
                    if i == 0:
                        dve.tensor_tensor(u, v.rearrange("p (h d) -> p h d", h=EH), bi, ALU.mult).then_inc(q["u_ready"], 1)
                        continue
                    dve.wait_ge(q["u_ready"], l * NB + i)
                    dve.tensor_tensor(heads(kprod[0][:, 0:i * D].rearrange("p (j c) -> p j c", c=D)), heads(U[:, 0:i, :]),
                                      GK[:, i, 0:i, :].unsqueeze(3).to_broadcast([P, i, EH, ED]), ALU.mult).then_inc(q["p_mult"], 1)
                    dve.wait_ge(q["p_mult"], l * (NB - 1) + i)
                    dve.tensor_reduce(pred[:, :], kprod[0][:, 0:i * D].rearrange("p (j c) -> p c j", c=D), AX.X, ALU.add)\
                       .then_inc(q["p_ready"], 1)
                    dve.wait_ge(q["p_ready"], l * (NB - 1) + i)
                    dve.tensor_tensor(pred[:, :], v, pred[:, :], ALU.subtract).then_inc(q["diff"], 1)
                    dve.wait_ge(q["diff"], l * (NB - 1) + i)
                    dve.tensor_tensor(u, pred[:, :].rearrange("p (h d) -> p h d", h=EH), bi, ALU.mult).then_inc(q["u_ready"], 1)
                    if i >= 2:
                        output(i - 2)
                output(NB - 2)
                output(NB - 1)
                dve.wait_ge(q["osq"], l + 1)
                dve.tensor_reduce(sso[:, :], sqk[:, :, 0:D].rearrange("p n (h d) -> p n h d", h=EH), AX.X, ALU.add)\
                   .then_inc(q["oss"], 1)
                k.wait_alone(dve, q["ors"], l + 1)
                with dve.Fori(0, NG) as g:
                    m = l * NG + g
                    dve.wait_ge(q["o_turned"], m + 1)
                    dve.tensor_tensor(on[:, :, :].rearrange("p i (h d) -> p (i h) d", h=EH),
                                      o[:, bass.ds(g * GI, GI), :].rearrange("p i (h d) -> p (i h) d", h=EH),
                                      rso[:, bass.ds(g * GI * EH, GI * EH)].unsqueeze(2).to_broadcast([P, GI * EH, ED]),
                                      ALU.mult).then_inc(q["onormed"], 1)
                    y = Y[:, bass.ds(g * GI, GI), :]
                    dve.wait_ge(q["Y_ready"], l * 2 * NG + g + 1)
                    dve.wait_ge(q["out_made"], m + 1)
                    dve.tensor_tensor(y, b[5][:, :].rearrange("p (i d) -> p i d", i=GI), y, ALU.add).then_inc(q["Y_ready"], 1)
                with dve.Fori(0, NG) as g:
                    m = l * NG + g
                    dve.wait_ge(q["Y_ready"], NG + l * 2 * NG + g + 1)
                    n2.on_vector(dve, m, lambda i: Y[:, g * GI + i, :])
                    for c in range(IC):
                        f = min(P, INTER - c * P)
                        dve.wait_ge(q["gsilu"], m * IC + c + 1)
                        dve.tensor_tensor(a[0:f, c, :], sg[0:f, c % 2, :], b[2 * (c % 2) + 1][0:f, :], ALU.mult)\
                           .then_inc(q["gated"], 1)
                    y = Y[:, bass.ds(g * GI, GI), :]
                    dve.wait_ge(q["down"], m + 2)
                    dve.tensor_tensor(y, b[5][:, :].rearrange("p (i d) -> p i d", i=GI), y, ALU.add).then_inc(q["Y_ready"], 1)
            dve.wait_ge(q["Y_ready"], NG + L3 * 2 * NG)
            dve.sem_inc(q["added"], 1)
            with dve.Fori(0, NG) as g:
                dve.wait_ge(q["added"], g + 1)
                nf.on_vector(dve, g, lambda i: Y[:, g * GI + i, :])
                x = X[:, bass.ds(g * GI, GI), :]
                dve.wait_ge(nf.ready, g + 2)
                dve.tensor_tensor(nf.xn[:, :, :], nf.xn[:, :, :], w["final"].unsqueeze(1).to_broadcast([P, GI, D]), ALU.mult)\
                   .then_inc(q["final_w"], 1)
                dve.wait_ge(q["final_w"], g + 1)
                dve.tensor_tensor(x, x, nf.xn[:, :, :], ALU.add).then_inc(q["added"], 1)


def pack_l3a(a):
    return {"final": np.broadcast_to(a["L3_attn_final_norm_w"][None], (P, D))}


def stream_l3a(a):
    wd = np.zeros((L3, IC * P, D), np.float32)
    wd[:, :INTER] = a["L3_attn_Wd"]
    onorm = np.concatenate([a["L3_attn_onorm_w"]] * EH, 1)
    return {"mix_l3a": np.concatenate([a["L3_attn_Wq"], a["L3_attn_Wk"], a["L3_attn_Wv"], a["L3_attn_Wb"], a["L3_attn_Wo"],
                                       a["L3_attn_norm1_w"][:, :, None], onorm[:, :, None]], 2),
            "ffn_l3a": np.concatenate([a["L3_attn_Wg"], wd.reshape(L3, IC, P, D).transpose(0, 2, 1, 3).reshape(L3, P, IC * D),
                                       a["L3_attn_norm2_w"][:, :, None]], 2)}



PACKS["l3x"] = Pack(("wq", D, D), ("wk", C + 1, D), ("wv", C + 1, D), ("bq", D, 1))


def sublayer_l3_xattn(k, s, n):
    nc, X, cT, ident = k.nc, k.X, k.cT, k.ident
    w, loaded, count = k.weights(n)
    SCALE = float(D) ** -0.5
    norm = Norm(k, s.sb, s.sem, "ln")
    cG = s.sb("cG", [C + 1, GI, T])
    xT = s.sb("xT", [D, GT])
    qT = s.sb("qT", [D, GT])
    kT = s.sb("kT", [D, GT])
    v = s.sb("v", [T, GI, D])
    nmax = s.sb("nmax", [T, GI])
    total = s.sb("total", [T, GI])
    inv = s.sb("inv", [T, GI])
    E = s.sb("E", [T, GI, T])
    ET = s.sb("ET", [T, GI, T])
    pX, pQ, pK, pV, pS, pT, pO = s.banks(7)
    cG_ready, xT_ready, kv_made, q_made = s.sem("cG_ready"), s.sem("xT_ready"), s.sem("kv_made"), s.sem("q_made")
    kv_ready, q_ready = s.sem("kv_ready"), s.sem("q_ready")
    scores, maxed, expd, turned, ET_ready = s.sem("scores"), s.sem("maxed"), s.sem("expd"), s.sem("turned"), s.sem("ET_ready")
    inverted, mixed, added = s.sem("inverted"), s.sem("mixed"), s.sem("added")

    with nc.Block() as block:
        @block.sync
        def _(sp):
            k.load(sp, n + 1)

        @block.gpsimd
        def _(pool):
            with pool.Fori(0, NG) as g:
                pool.wait_ge(kv_made, g + 1)
                pool.tensor_copy(cG[:, :, :], cT[:, bass.ds(g * GI, GI), :]).then_inc(cG_ready, 1)
                norm.on_pool(pool, g)

        @block.tensor
        def _(pe):
            pe.wait_ge(loaded, count)
            for free in (kv_made, mixed):
                pe.sem_inc(free, 1)
            with pe.Fori(0, NG) as g:
                pe.wait_ge(cG_ready, g + 1)
                pe.matmul(pK[:, :], w["wk"], cG[:, :, :], start=True, stop=True)
                for i in range(GI):
                    ins = pe.matmul(pV[:, i * D:(i + 1) * D], cG[:, i, :], w["wv"], start=True, stop=True)
                ins.then_inc(kv_made, 1)
                norm.on_tensor(pe, g, pX)
                pe.wait_ge(xT_ready, g + 1)
                pe.matmul(pQ[:, :], w["wq"], xT[:, :], start=True, stop=True).then_inc(q_made, 1)
                pe.wait_ge(kv_ready, g + 1)
                pe.wait_ge(q_ready, g + 1)
                for i in range(GI):
                    ins = pe.matmul(pS[:, i * T:(i + 1) * T], qT[:, i * T:(i + 1) * T], kT[:, i * T:(i + 1) * T],
                                    start=True, stop=True)
                ins.then_inc(scores, 1)
                pe.wait_ge(expd, g + 1)
                for i in range(GI):
                    ins = pe.transpose(pT[:, i * T:(i + 1) * T], E[:, i, :], ident[:, :])
                ins.then_inc(turned, 1)
                pe.wait_ge(ET_ready, g + 1)
                pe.wait_ge(added, g + 1)
                for i in range(GI):
                    ins = pe.matmul(pO[:, i * D:(i + 1) * D], ET[:, i, :], v[:, i, :], start=True, stop=True)
                ins.then_inc(mixed, 1)

        @block.scalar
        def _(act):
            with act.Fori(0, NG) as g:
                act.wait_ge(kv_made, g + 2)
                act.copy(kT[:, :], pK[:, :])
                act.wait_ge(mixed, g + 1)
                act.copy(v[:, :, :], pV[:, :]).then_inc(kv_ready, 1)
                act.wait_ge(norm.turned, g + 1)
                act.copy(xT[:, :], pX[:, :]).then_inc(xT_ready, 1)
                act.wait_ge(maxed, g + 1)
                act.wait_ge(inverted, g + 1)
                for i in range(GI):
                    ins = act.activation(E[:, i, :], pS[:, i * T:(i + 1) * T], ACT.Exp, bias=nmax[:, i:i + 1],
                                         accum_out=total[:, i:i + 1])
                ins.then_inc(expd, 1)

        @block.vector
        def _(dve):
            for free in (inverted, added):
                dve.sem_inc(free, 1)
            with dve.Fori(0, NG) as g:
                def src(i):
                    return X[:, g * GI + i, :]
                norm.on_vector_stats(dve, g, src)
                norm.on_vector_apply(dve, g, src)
                dve.wait_ge(q_made, g + 1)
                dve.tensor_scalar(qT[:, :], pQ[:, :], w["bq"], SCALE, ALU.add, ALU.mult).then_inc(q_ready, 1)
                dve.wait_ge(scores, g + 1)
                dve.tensor_reduce(nmax[:, :], pS[:, :].rearrange("p (i t) -> p i t", i=GI), AX.X, ALU.max,
                                  negate=True).then_inc(maxed, 1)
                dve.wait_ge(expd, g + 1)
                dve.reciprocal(inv[:, :], total[:, :]).then_inc(inverted, 1)
                dve.wait_ge(turned, g + 1)
                dve.tensor_copy(ET[:, :, :], pT[:, :]).then_inc(ET_ready, 1)
                dve.wait_ge(mixed, g + 2)
                dve.wait_ge(inverted, g + 2)
                for i in range(GI):
                    ins = dve.scalar_tensor_tensor(out=src(i), in0=pO[:, i * D:(i + 1) * D], scalar=inv[:, i:i + 1],
                                                   in1=src(i), op0=ALU.mult, op1=ALU.add)
                ins.then_inc(added, 1)
                dve.wait_ge(added, g + 2)


def pack_l3x(a):
    return {"wq": a["L3_xattn_Wq"], "bq": a["L3_xattn_bq"],
            "wk": np.concatenate([a["L3_xattn_Wk"], a["L3_xattn_bk"][None]], 0),
            "wv": np.concatenate([a["L3_xattn_Wv"], a["L3_xattn_bv"][None]], 0)}



SLOTS = 8 * 64
SC = SLOTS // P
HID = 4 * D
HC = HID // P
PACKS["l3f"] = Pack(("w1", D, HID), ("w2", P, HC * D), ("slots", P, SC * D), ("gx", D, 1), ("gs", D, 1))


def sublayer_l3_ffn(k, s, n):
    nc, X, ident = k.nc, k.X, k.ident
    w, loaded, count = k.weights(n)
    w1 = w["w1"]
    w2 = w["w2"].rearrange("p (c d) -> p c d", c=HC)
    slots = w["slots"].rearrange("p (c d) -> p c d", c=SC)
    ROOT = float(D) ** 0.5
    norm = Norm(k, s.sb, s.sem, "ln")
    seT = s.sb("seT", [D, SLOTS])
    se = s.sb("se", [P, SC, D])
    sq = s.sb("sq", [P, GI, D])
    ss = s.sb("ss", [P, GI])
    root = s.sb("root", [P, GI])
    safe = s.sb("safe", [P, GI])
    rn = s.sb("rn", [P, GI])
    xr = s.sb("xr", [T, GI, D])
    xT = s.sb("xT", [D, GT])
    cmax, csum, cinv = s.sb("cmax", [T, GI]), s.sb("csum", [T, GI]), s.sb("cinv", [T, GI])
    dmax, dsum, dinv = s.sb("dmax", [P, GI, SC]), s.sb("dsum", [P, GI, SC]), s.sb("dinv", [P, GI, SC])
    cx = s.sb("cx", [T, 2, SLOTS])
    dx = s.sb("dx", [P, 2, SC, T])
    dn = s.sb("dn", [P, 2, SC, T])
    cT = s.sb("cT", [P, GI, SC * T])
    dm = s.sb("dm", [T, 2, SLOTS])
    slT = s.sb("slT", [D, GI, SLOTS])
    hT = s.sb("hT", [P, 2, HC, SLOTS])
    pr = s.sb("pr", [P, 2, SC * D])
    bL, bLT, bC, bD, bH0, bH1, bP, bO = s.banks(8)
    bH = (bH0, bH1)
    names = ("se_squared se_root se_safe se_inv se_scaled se_turned se_ready squared rooted safed normed scaled "
             "xT_ready logits maxed expd dnormed cnormed turned cT_ready dm_ready slots_made slT_ready "
             "up gelud down pr_ready mixed added").split()
    q = {name: s.sem(name) for name in names}

    with nc.Block() as block:
        @block.sync
        def _(sp):
            k.load(sp, n + 1)

        @block.gpsimd
        def _(pool):
            pool.wait_ge(q["se_squared"], 1)
            pool.tensor_tensor(root[:, :], ss[:, :], k.plus[:, 0:GI], ALU.pow).then_inc(q["se_root"], 1)
            pool.wait_ge(q["se_root"], 1)
            pool.tensor_scalar(safe[:, :], root[:, :], 1e-12, None, ALU.max).then_inc(q["se_safe"], 1)
            with pool.Fori(0, NG) as g:
                norm.on_pool(pool, g)
                pool.wait_ge(q["squared"], g + 1)
                pool.tensor_tensor(root[:, :], ss[:, :], k.plus[:, 0:GI], ALU.pow).then_inc(q["rooted"], 1)
                k.wait_alone(pool, q["rooted"], g + 1)
                pool.tensor_scalar(safe[:, :], root[:, :], 1e-12, None, ALU.max).then_inc(q["safed"], 1)

        @block.tensor
        def _(pe):
            pe.wait_ge(loaded, count)
            pe.sem_inc(q["up"], 2)
            pe.wait_ge(q["se_scaled"], 1)
            for c in range(SC):
                ins = pe.transpose(bL[:, c * P:(c + 1) * P], se[:, c, :], ident[:, :])
            ins.then_inc(q["se_turned"], 1)
            pe.wait_ge(q["se_ready"], 1)
            with pe.Fori(0, NG) as g:
                pe.wait_ge(q["scaled"], g + 1)
                for i in range(GI):
                    ins = pe.transpose(bC[:, i * T:(i + 1) * T], xr[:, i, :], ident[:, :])
                ins.then_inc(norm.turned, 1)
                pe.wait_ge(q["xT_ready"], g + 1)
                for t in range(GI + 2):
                    if t < GI:
                        u = g * GI + t
                        if t:
                            pe.wait_ge(q["expd"], u)
                        x = xT[:, t * T:(t + 1) * T]
                        pe.matmul(bL[:, :], x, seT[:, :], start=True, stop=True)
                        for c in range(SC):
                            ins = pe.matmul(bLT[:, c * T:(c + 1) * T], seT[:, c * P:(c + 1) * P], x, start=True, stop=True)
                        ins.then_inc(q["logits"], 1)
                    if 0 <= t - 1 < GI:
                        u, b = g * GI + t - 1, (t - 1) % 2
                        if t - 1:
                            pe.wait_ge(q["cT_ready"], u)
                            pe.wait_ge(q["dm_ready"], u)
                        pe.wait_ge(q["dnormed"], u + 1)
                        for c in range(SC):
                            pe.transpose(bC[:, c * T:(c + 1) * T], cx[:, b, c * P:(c + 1) * P], ident[:, :])
                        for c in range(SC):
                            ins = pe.transpose(bD[:, c * P:(c + 1) * P], dn[:, b, c, :], ident[:, :])
                        ins.then_inc(q["turned"], 1)
                    if 0 <= t - 2 < GI:
                        u, b = g * GI + t - 2, (t - 2) % 2
                        if t - 2:
                            pe.wait_ge(q["slT_ready"], u)
                        pe.wait_ge(q["dm_ready"], u + 1)
                        pe.matmul(bO[:, :], xr[:, t - 2, :], dm[:, b, :], start=True, stop=True).then_inc(q["slots_made"], 1)
                for i in range(GI):
                    u, b = g * GI + i, i % 2
                    pe.wait_ge(q["slT_ready"], u + 1)
                    for c in range(HC):
                        pe.wait_ge(q["gelud"], u * HC + c + 1)
                        pe.matmul(bH[c % 2][:, :], w1[:, c * P:(c + 1) * P], slT[:, i, :], start=True, stop=True)\
                          .then_inc(q["up"], 1)
                    pe.wait_ge(q["gelud"], u * HC + HC + 2)
                    if i:
                        pe.wait_ge(q["pr_ready"], u)
                    for c in range(SC):
                        for f in range(HC):
                            ins = pe.matmul(bP[:, c * D:(c + 1) * D], hT[:, b, f, c * P:(c + 1) * P], w2[:, f, :],
                                            start=(f == 0), stop=(f == HC - 1))
                    ins.then_inc(q["down"], 1)
                    pe.wait_ge(q["pr_ready"], u + 1)
                    if i:
                        pe.wait_ge(q["added"], u)
                    for c in range(SC):
                        ins = pe.matmul(bO[:, 0:D], cT[:, i, c * T:(c + 1) * T], pr[:, b, c * D:(c + 1) * D],
                                        start=(c == 0), stop=(c == SC - 1))
                    ins.then_inc(q["mixed"], 1)

        @block.scalar
        def _(act):
            act.wait_ge(loaded, count)
            act.sem_inc(q["gelud"], 2)
            for c in range(SC):
                ins = act.activation(sq[:, c, :], slots[:, c, :], ACT.Square, accum_out=ss[:, c:c + 1])
            ins.then_inc(q["se_squared"], 1)
            act.wait_ge(q["se_turned"], 1)
            act.activation(seT[:, :], bL[:, :], ACT.Copy, scale=w["gs"]).then_inc(q["se_ready"], 1)
            with act.Fori(0, NG) as g:
                act.wait_ge(norm.ready, g + 1)
                for i in range(GI):
                    ins = act.activation(sq[:, i, :], norm.xn[:, i, :], ACT.Square, accum_out=ss[:, i:i + 1])
                ins.then_inc(q["squared"], 1)
                act.wait_ge(norm.turned, g + 1)
                act.activation(xT[:, :], bC[:, :], ACT.Copy, scale=w["gx"]).then_inc(q["xT_ready"], 1)
                for t in range(GI + 1):
                    if t < GI:
                        u, b = g * GI + t, t % 2
                        if t >= 2:
                            act.wait_ge(q["turned"], u - 1)
                        act.wait_ge(q["maxed"], u + 1)
                        act.activation(cx[:, b, :], bL[:, :], ACT.Exp, bias=cmax[:, t:t + 1], accum_out=csum[:, t:t + 1])
                        for c in range(SC):
                            ins = act.activation(dx[:, b, c, :], bLT[:, c * T:(c + 1) * T], ACT.Exp,
                                                 bias=dmax[:, t, c:c + 1], accum_out=dsum[:, t, c:c + 1])
                        ins.then_inc(q["expd"], 1)
                    if t >= 1:
                        u = g * GI + t - 1
                        act.wait_ge(q["turned"], u + 1)
                        act.copy(cT[:, t - 1, :], bC[:, :]).then_inc(q["cT_ready"], 1)
                for i in range(GI):
                    u, b = g * GI + i, i % 2
                    for c in range(HC):
                        act.wait_ge(q["up"], u * HC + c + 3)
                        act.activation(hT[:, b, c, :], bH[c % 2][:, :], ACT.Gelu).then_inc(q["gelud"], 1)

        @block.vector
        def _(dve):
            dve.wait_ge(loaded, count)
            dve.wait_ge(q["se_safe"], 1)
            dve.reciprocal(rn[:, :], safe[:, :]).then_inc(q["se_inv"], 1)
            dve.wait_ge(q["se_inv"], 1)
            for c in range(SC):
                ins = dve.tensor_scalar(se[:, c, :], slots[:, c, :], rn[:, c:c + 1], ROOT, ALU.mult, ALU.mult)
            ins.then_inc(q["se_scaled"], 1)
            with dve.Fori(0, NG) as g:
                def src(i):
                    return X[:, g * GI + i, :]
                norm.on_vector_stats(dve, g, src)
                norm.on_vector_apply(dve, g, src)
                k.wait_alone(dve, q["safed"], g + 1)
                dve.reciprocal(rn[:, :], safe[:, :]).then_inc(q["normed"], 1)
                k.wait_alone(dve, q["normed"], g + 1)
                for i in range(GI):
                    ins = dve.tensor_scalar(xr[:, i, :], norm.xn[:, i, :], rn[:, i:i + 1], ROOT, ALU.mult, ALU.mult)
                ins.then_inc(q["scaled"], 1)
                for t in range(GI + 2):
                    if t < GI:
                        dve.wait_ge(q["logits"], g * GI + t + 1)
                        dve.tensor_reduce(cmax[:, t:t + 1], bL[:, :], AX.X, ALU.max, negate=True)
                        dve.tensor_reduce(dmax[:, t, :], bLT[:, :].rearrange("p (c t) -> p c t", c=SC), AX.X, ALU.max,
                                          negate=True).then_inc(q["maxed"], 1)
                    if 0 <= t - 1 < GI:
                        i, u, b = t - 1, g * GI + t - 1, (t - 1) % 2
                        dve.wait_ge(q["expd"], u + 1)
                        dve.reciprocal(cinv[:, i:i + 1], csum[:, i:i + 1])
                        dve.reciprocal(dinv[:, i, :], dsum[:, i, :]).then_inc(q["cnormed"], 1)
                        dve.wait_ge(q["cnormed"], u + 1)
                        dve.tensor_tensor(dn[:, b, :, :], dx[:, b, :, :],
                                          dinv[:, i, :].unsqueeze(2).to_broadcast([P, SC, T]), ALU.mult)\
                           .then_inc(q["dnormed"], 1)
                        if t - 1 >= 2:
                            dve.wait_ge(q["slots_made"], u - 1)
                        dve.wait_ge(q["turned"], u + 1)
                        dve.tensor_copy(dm[:, b, :], bD[:, :]).then_inc(q["dm_ready"], 1)
                    if 0 <= t - 2 < GI:
                        i, u = t - 2, g * GI + t - 2
                        dve.wait_ge(q["slots_made"], u + 1)
                        dve.tensor_scalar(slT[:, i, :], bO[:, :], w["gx"], None, ALU.mult).then_inc(q["slT_ready"], 1)
                for i in range(GI):
                    u, b = g * GI + i, i % 2
                    dve.wait_ge(q["down"], u + 1)
                    dve.tensor_copy(pr[:, b, :], bP[:, :]).then_inc(q["pr_ready"], 1)
                    dve.wait_ge(q["mixed"], u + 1)
                    dve.scalar_tensor_tensor(out=src(i), in0=bO[:, 0:D], scalar=cinv[:, i:i + 1], in1=src(i),
                                             op0=ALU.mult, op1=ALU.add).then_inc(q["added"], 1)


def pack_l3f(a):
    return {"w1": a["L3_ffn_w1"], "gx": a["L3_ffn_gamma_x"], "gs": a["L3_ffn_gamma_slot"],
            "w2": a["L3_ffn_w2"].reshape(HC, P, D).transpose(1, 0, 2),
            "slots": a["L3_ffn_slot_embeds"].reshape(SC, P, D).transpose(1, 0, 2)}

BUILD = {
    "l0x": sublayer_soft_attention,
    "l1x": sublayer_soft_attention,
    "l2x": sublayer_soft_attention,
    "l0g": sublayer_soft_attention,
    "l0a": sublayer_retention,
    "l1a": sublayer_linear,
    "l2a": sublayer_over_sequences,
    "l0f": sublayer_moe,
    "l1f": sublayer_moe,
    "l2f": sublayer_moe,
    "l3a": sublayer_delta,
    "l3x": sublayer_l3_xattn,
    "l3f": sublayer_l3_ffn,
}
PACK_OF = {
    "l0x": pack_l0x,
    "l1x": pack_l1x,
    "l2x": pack_l2x,
    "l0g": pack_l0g,
    "l0a": pack_l0a,
    "l1a": pack_l1a,
    "l2a": pack_l2a,
    "l1f": pack_l1f,
    "l2f": pack_l2f,
    "l0f": pack_l0f,
    "l3a": pack_l3a,
    "l3x": pack_l3x,
    "l3f": pack_l3f,
}
STREAM_OF = {
    "l1a": stream_l1a,
    "l1f": stream_l1f,
    "l2f": stream_l2f,
    "l0f": stream_l0f,
    "l3a": stream_l3a,
}



NAMES = [["l0a"], ["l0x"], ["l0g", "l0f"], ["l1a"], ["l1x"], ["l1f"], ["l2a"], ["l2x"], ["l2f"], ["l3a"], ["l3x"], ["l3f"]]
UNITS = [name for ph in PHASES for name in NAMES[ph]]
ARENA = max(p.cols for p in PACKS.values())


def decoder_kernel(nc, dram, out):
    with ExitStack() as ctx:
        k = Shared(nc, ctx, dram)
        for n, name in enumerate(UNITS):
            with ExitStack() as mem:
                s = Scope(k, mem, name)
                if n == 0:
                    open_program(k)
                BUILD[name](k, s, n)
                nums = s.sems
                clear_semaphores(nc, nums)
        close_program(k, out)


def open_program(k):
    nc = k.nc
    with nc.Block() as block:
        @block.sync
        def _(sp):
            sp.dma_start(k.X[:, :, :], k.dram["x"][:, :, :]).then_inc(k.base_loaded, 16)
            sp.dma_start(k.cT[:, :, :], k.dram["cT"][:, :, :]).then_inc(k.base_loaded, 16)
            sp.dma_start(k.ident[:, :], k.dram["ident"][:, :]).then_inc(k.base_loaded, 16)
            sp.dma_start(k.iota[:, :], k.dram["iota"][:, :]).then_inc(k.base_loaded, 16)
            k.load(sp, 0)
            sp.wait_ge(k.base_loaded, BASE_LOADS)

        @block.gpsimd
        def _(pool):
            pool.memset(k.half[:, :], -0.5)
            pool.memset(k.plus[:, :], 0.5)


def clear_semaphores(nc, sems):
    with nc.Block() as block:
        @block.gpsimd
        def _(pool):
            for sem in sems:
                pool.sem_clear(sem)


def close_program(k, out):
    with k.nc.Block() as block, k.nc.semaphore("stored") as stored:
        @block.sync
        def _(sp):
            sp.dma_start(out[:, :, :], k.X[:, :, :]).then_inc(stored, 16)
            sp.wait_ge(stored, 16)



def kernel(**inputs):
    import concourse.bacc as _bacc
    from concourse.bass_utils import run_bass_kernel_spmd as _run

    a = {name: np.asarray(v) for name, v in inputs.items()}
    arrays = {
        "x": np.ascontiguousarray(a["x"].transpose(1, 0, 2)),
        "cT": np.concatenate([a["ctx_768"].transpose(2, 0, 1), np.ones((1, NB, T), np.float32)], 0),
        "iota": np.broadcast_to(np.arange(8, dtype=np.float32)[None], (P, 8)).copy(),
        "ident": np.eye(P, dtype=np.float32),
    }
    for name in UNITS:
        if PACKS[name].cols:
            arrays["w_" + name] = PACKS[name].fill(PACK_OF[name](a))
        if name in STREAM_OF:
            arrays.update(STREAM_OF[name](a))
    nc = _bacc.Bacc("TRN2", target_bir_lowering=False, num_devices=1)
    dram = {name: nc.dram_tensor(f"in_{name}", v.shape, mybir.dt.from_np(v.dtype), kind="ExternalInput").ap()
            for name, v in arrays.items()}
    out = nc.dram_tensor("out", (P, NB, D), F32, kind="ExternalOutput").ap()
    decoder_kernel(nc, dram, out)
    r = _run(nc, [{f"in_{name}": v for name, v in arrays.items()}], core_ids=[0])
    return r.results[0]["out"].transpose(1, 0, 2).copy()
```

```python
from contextlib import ExitStack

import numpy as np

import concourse.bass as bass
from concourse import mybir

F32 = mybir.dt.float32
BF16 = mybir.dt.bfloat16
U32 = mybir.dt.uint32
ALU = mybir.AluOpType
ACT = mybir.ActivationFunctionType
AX = mybir.AxisListType

P = 128
NB = 16
T = 128
D = 128
C = 96
GI = 4
NG = NB // GI
GT = GI * T
LN_EPS = 1e-5
BASE_LOADS = 64
PHASES = list(range(12))
ARENA = 0
NAMES = []
PACKS = {}



class Shared:

    def __init__(self, nc, ctx, dram):
        self.nc, self.dram = nc, dram
        self.X = ctx.enter_context(nc.sbuf_tensor("X", [P, NB, D], F32))
        self.cT = ctx.enter_context(nc.sbuf_tensor("cT", [C + 1, NB, T], F32))
        self.Z = ctx.enter_context(nc.sbuf_tensor("Z", [P, NB, D], F32))
        self.ident = ctx.enter_context(nc.sbuf_tensor("ident", [P, P], F32))
        self.half = ctx.enter_context(nc.sbuf_tensor("half", [P, 2 * GI], F32))
        self.plus = ctx.enter_context(nc.sbuf_tensor("plus", [P, 2 * GI], F32))
        self.iota = ctx.enter_context(nc.sbuf_tensor("iota", [P, 8], F32))
        self.arena = [ctx.enter_context(nc.sbuf_tensor(f"arena{i}", [P, ARENA], F32)) for i in range(2)]
        self.loaded = [ctx.enter_context(nc.semaphore(f"weights_loaded{i}")) for i in range(2)]
        self.base_loaded = ctx.enter_context(nc.semaphore("base_loaded"))
        self.loads = [0, 0]
        self.tick = ctx.enter_context(nc.semaphore("tick"))

    def wait_alone(self, eng, sem, value):
        eng.wait_ge(sem, value)
        eng.sem_inc(self.tick, 1)

    def load(self, eng, n):
        if n < len(UNITS):
            name = UNITS[n]
            cols = PACKS[name].cols
            if cols:
                eng.dma_start(self.arena[n % 2][:, 0:cols], self.dram["w_" + name][:, :]).then_inc(self.loaded[n % 2], 16)
                self.loads[n % 2] += 1

    def weights(self, n):
        pack = PACKS[UNITS[n]]
        return ({k: self.arena[n % 2][0:r, o:o + c] for k, (o, r, c) in pack.at.items()},
                self.loaded[n % 2], 16 * self.loads[n % 2])


class Pack:

    def __init__(self, *parts):
        self.at, self.cols = {}, 0
        for name, rows, cols in parts:
            self.at[name] = (self.cols, rows, cols)
            self.cols += cols

    def fill(self, parts):
        out = np.zeros((P, self.cols), np.float32)
        for name, (o, r, c) in self.at.items():
            out[0:r, o:o + c] = parts[name].reshape(r, c)
        return out


class Norm:

    def __init__(self, k, sb, sem, tag):
        self.k = k
        self.st = sb(f"{tag}_st", [P, GI, 6], F32)
        self.mv = sb(f"{tag}_mv", [P, GI, 2], F32)
        self.ve = sb(f"{tag}_ve", [P, GI], F32)
        self.rs = sb(f"{tag}_rs", [P, GI], F32)
        self.xn = sb(f"{tag}_xn", [P, GI, D], F32)
        self.bn = sem(f"{tag}_bn")
        self.stats = sem(f"{tag}_stats")
        self.eps = sem(f"{tag}_eps")
        self.rstd = sem(f"{tag}_rstd")
        self.ready = sem(f"{tag}_ready")
        self.turned = sem(f"{tag}_turned")

    def on_vector_stats(self, dve, g, src):
        for i in range(GI):
            ins = dve.bn_stats(self.st[:, i, :], src(i))
        ins.then_inc(self.bn, 1)
        self.k.wait_alone(dve, self.bn, g + 1)
        for i in range(GI):
            ins = dve.bn_aggr(self.mv[:, i, :], self.st[:, i, :])
        ins.then_inc(self.stats, 1)

    def on_pool(self, pool, g, eps=LN_EPS):
        self.k.wait_alone(pool, self.stats, g + 1)
        pool.tensor_scalar(self.ve[:, :], self.mv[:, :, 1], eps, None, ALU.add).then_inc(self.eps, 1)
        pool.wait_ge(self.eps, g + 1)
        pool.tensor_tensor(self.rs[:, :], self.ve[:, :], self.k.half[:, 0:GI], ALU.pow).then_inc(self.rstd, 1)

    def on_vector_apply(self, dve, g, src):
        dve.wait_ge(self.rstd, g + 1)
        for i in range(GI):
            ins = dve.tensor_scalar(self.xn[:, i, :], src(i), self.mv[:, i, 0:1], self.rs[:, i:i + 1],
                                    ALU.subtract, ALU.mult)
        ins.then_inc(self.ready, 1)

    def on_tensor(self, pe, g, bank):
        pe.wait_ge(self.ready, g + 1)
        for i in range(GI):
            ins = pe.transpose(bank[:, i * T:(i + 1) * T], self.xn[:, i, :], self.k.ident[:, :])
        ins.then_inc(self.turned, 1)


class Scope:

    def __init__(self, k, ctx, tag):
        self.k, self.ctx, self.tag, self.sems = k, ctx, tag, []

    def sb(self, name, shape, dt=F32):
        return self.ctx.enter_context(self.k.nc.sbuf_tensor(f"{self.tag}_{name}", shape, dt))

    def banks(self, n=8):
        return [self.ctx.enter_context(self.k.nc.psum_tensor(f"{self.tag}_bank{i}", [P, 512], F32)) for i in range(n)]

    def sem(self, name):
        s = self.ctx.enter_context(self.k.nc.semaphore(f"{self.tag}_{name}"))
        self.sems.append(s)
        return s



H = 16
DH = D // H
BANKS = 4
PLACES = H // BANKS
TILES = 8
HALF = 64
BLOCKS = 6
PARTS_Q = (0, 0, 1, 1, 0, 2)
PARTS_K = (0, 1, 0, 1, 2, 0)
PACKS["l0x"] = PACKS["l1x"] = PACKS["l2x"] = Pack(
    ("wq", D, D), ("bq", D, 1), ("wk", C + 1, D), ("wv", C + 1, D), ("wo", D, D), ("bo", 1, D), ("one", 1, T))
PACKS["l0g"] = Pack(
    ("wq", D, D), ("wqp", D, D), ("wk", D, D), ("wkp", D, D), ("wv", D, D), ("wo", D, D),
    ("ln1_w", D, 1), ("ln1_b", D, 1), ("conv", D, 3), ("cq", P, T), ("sq", P, T), ("ck", P, T), ("sk", P, T),
    ("mask", T, T), ("maskT", T, T))


def head_at(bank, slot):
    return 2 * (PLACES * (bank // 2) + slot) + bank % 2


def partners(w):
    order = [(d + DH // 2) % DH for d in range(DH)]
    return w.reshape(-1, H, DH)[:, :, order].reshape(-1, D)


def output_rows(wo):
    order = [head_at(bank, slot) for bank in range(BANKS) for slot in range(PLACES)]
    return wo.reshape(H, DH, D)[order].reshape(D, D)


class Selectors:

    def __init__(self, nc, ctx):
        sb = lambda name, shape, dt=BF16: ctx.enter_context(nc.sbuf_tensor(name, shape, dt))
        self.ident = sb("ident_b", [P, P])
        self.pick = [sb(f"pick{x}", [D, 3, TILES, P]) for x in range(2)]
        self.sel = sb("sel", [P, H, T])
        self.rowsum = sb("rowsum", [P, H], F32)
        self.cleared = ctx.enter_context(nc.semaphore("picks_cleared"))
        self.summed = ctx.enter_context(nc.semaphore("rows_summed"))

    def build(self, dve, ident):
        for x in range(2):
            dve.memset(self.pick[x][:, :, :, :], 0.0).then_inc(self.cleared, 1)
        dve.tensor_copy(self.ident[:, :], ident[:, :])
        dve.wait_ge(self.cleared, 2)
        heads = ident[:, :].rearrange("p (j r d) -> p j r d", r=2, d=DH)
        for x, parts in enumerate((PARTS_K, PARTS_Q)):
            for block, part in enumerate(parts):
                rows = self.pick[x][:, part, :, :].rearrange("p j (r c) -> p j r c", r=2)
                dve.tensor_copy(rows[:, :, :, block * DH:(block + 1) * DH], heads)
        dve.tensor_tensor(self.rowsum[:, :], ident[:, 0:H], ident[:, H:2 * H], ALU.add).then_inc(self.summed, 1)
        dve.wait_ge(self.summed, 1)
        dve.tensor_tensor(self.rowsum[:, :], self.rowsum[:, :], ident[:, 2 * H:3 * H], ALU.add).then_inc(self.summed, 1)
        dve.wait_ge(self.summed, 2)
        dve.tensor_copy(self.sel[:, :, :], self.rowsum[:, :].unsqueeze(2).to_broadcast([P, H, T]))


class SoftAttention:

    def __init__(self, k, s, n, kind):
        self.k, self.kind = k, kind
        self.w, self.loaded, self.count = k.weights(n)
        self.cross = kind != "l0g"
        self.SCALE = float(DH) ** -0.5
        sb = s.sb
        self.norm = Norm(k, sb, s.sem, "ln")
        self.xT = sb("xT", [D, GT])
        self.full = [sb("k_full", [D, GT]), sb("q_full", [D, GT])]
        self.parts = [[sb(f"part{x}{p}", [D, GT], BF16) for p in range(3)] for x in range(2)]
        self.rest = sb("rest", [D, GT])
        self.pick, self.sel, self.identb = k.selectors.pick, k.selectors.sel, k.selectors.ident
        self.stack = [sb("k_stack", [P, TILES, GT], BF16), sb("q_stack", [P, TILES, GT], BF16)]
        self.v = sb("v", [T, GI, H, 32])
        self.nm = sb("nm", [T, H])
        self.nr = sb("nr", [T, H])
        self.nparts = sb("nparts", [T, P // H, H], BF16)
        self.nT = sb("nT", [P, T], BF16)
        self.PT = [sb(f"PT{i}", [T, BANKS, PLACES * T]) for i in range(2)]
        self.o = sb("o", [P, BANKS * T])
        self.inverse = sb("inverse", [T, BANKS, PLACES])
        self.at = sb("at", [T, BANKS, PLACES, DH])
        self.aT = sb("aT", [D, T])
        if self.cross:
            self.cG = sb("cG", [C + 1, GI, T])
            self.bqs = sb("bqs", [D, 1])
            self.dst = k.X
        else:
            self.norm2 = Norm(k, sb, s.sem, "ln1")
            self.hT = sb("hT", [D, GT])
            self.t1, self.t2 = [sb(f"t1{i}", [P, GT]) for i in range(2)], [sb(f"t2{i}", [P, GT]) for i in range(2)]
            self.maskb = sb("maskb", [T, PLACES, T], BF16)
            self.maskTb = sb("maskTb", [T, PLACES, T], BF16)
            self.dst = k.Z
        self.b = s.banks(8)
        names = ("cG_ready k_made v_made v_ready xT_ready q_made full_ready split parts_ready spread even_taken odd_taken "
                 "zeroed bias_scaled scored maxed nsplit n_ready n_turned nT_ready "
                 "scored2 expd pv o_ready o_turned inverted at_ready at_turned aT_ready v_zeroed out_made added h_ready conv1 conv2 masks roped t_made")
        self.q = {x: s.sem(x) for x in names.split()}


    def constants_pool(self, pool):
        pool.memset(self.v[:, :, :, :], 0.0).then_inc(self.q["v_zeroed"], 1)
        pool.wait_ge(self.q["v_zeroed"], 1)
        pool.memset(self.v[:, :, :, DH:DH + 1], 1.0)
        pool.memset(self.nparts[:, :, :], 0.0).then_inc(self.q["zeroed"], 1)


    def project_tensor(self, pe, n, part):
        q, b, w = self.q, self.b, self.w
        if part == 0:
            pe.wait_ge(q["maxed"], n * GI * BANKS + 2)
            pe.wait_ge(q["cG_ready"], n + 1)
            pe.matmul(b[1][:, :], w["wk"], self.cG[:, :, :], start=True, stop=True).then_inc(q["k_made"], 1)
            self.norm.on_tensor(pe, n, b[0])
        else:
            pe.wait_ge(q["full_ready"], n * 2 + 1)
            pe.wait_ge(q["xT_ready"], n + 1)
            pe.matmul(b[1][:, :], w["wq"], self.xT[:, :], start=True, stop=True).then_inc(q["q_made"], 1)
            for i in range(GI):
                ins = pe.matmul(b[0][:, i * D:(i + 1) * D], self.cG[:, i, :], w["wv"], start=True, stop=True)
            ins.then_inc(q["v_made"], 1)

    def take_v(self, act, n):
        q, b = self.q, self.b
        act.wait_ge(q["pv"], n * GI + 2)
        act.wait_ge(q["v_made"], n + 2)
        act.copy(self.v[:, :, :, 0:DH], b[0][:, :].rearrange("p (i h d) -> p i h d", i=GI, h=H)).then_inc(q["v_ready"], 1)

    def project_scalar(self, act, n, part):
        q, b = self.q, self.b
        if part == 0:
            act.wait_ge(q["k_made"], n + 1)
            act.copy(self.full[0][:, :], b[1][:, :]).then_inc(q["full_ready"], 1)
            act.wait_ge(self.norm.turned, n + 1)
            act.copy(self.xT[:, :], b[0][:, :]).then_inc(q["xT_ready"], 1)
        else:
            act.wait_ge(q["q_made"], n + 1)
            act.activation(self.full[1][:, :], b[1][:, :], ACT.Identity, scale=self.SCALE, bias=self.bqs[:, :])\
               .then_inc(q["full_ready"], 1)

    def project_vector(self, dve, n):
        x_src = lambda i: self.k.X[:, n * GI + i, :]
        self.norm.on_vector_stats(dve, n, x_src)
        self.norm.on_vector_apply(dve, n, x_src)


    def own_tensor(self, pe, n, part):
        q, b, w = self.q, self.b, self.w
        if part == 0:
            pe.wait_ge(q["maxed"], n * GI * BANKS + 2)
            self.norm2.on_tensor(pe, n, b[0])
        else:
            pe.wait_ge(q["conv2"], n * 2 + 2)
            pe.wait_ge(q["expd"], n * GI * BANKS + 2)
            for m, name in enumerate(("k", "q")):
                pe.matmul(b[2 * m][:, :], w["w" + name], self.xT[:, :], start=True, stop=True)
                pe.matmul(b[2 * m + 1][:, :], w["w" + name + "p"], self.xT[:, :], start=True, stop=True)\
                  .then_inc(q["t_made"], 1)
            pe.wait_ge(q["roped"], n * 2 + 1)
            for i in range(GI):
                ins = pe.matmul(b[0][:, i * D:(i + 1) * D], self.xT[:, i * T:(i + 1) * T], w["wv"], start=True, stop=True)
            ins.then_inc(q["v_made"], 1)

    def own_scalar(self, act, n):
        act.wait_ge(self.norm2.turned, n + 1)
        act.activation(self.hT[:, :], self.b[0][:, :], ACT.Identity, scale=self.w["ln1_w"], bias=self.w["ln1_b"])\
           .then_inc(self.q["h_ready"], 1)

    def own_norms(self, dve, g):
        x_src = lambda i: self.k.X[:, g * GI + i, :]
        self.norm.on_vector_stats(dve, g, x_src)
        self.norm.on_vector_apply(dve, g, x_src)
        dve.wait_ge(self.norm.ready, g + 1)
        dve.tensor_copy(self.k.Z[:, bass.ds(g * GI, GI), :], self.norm.xn[:, :, :])
        y_src = lambda i: self.norm.xn[:, i, :]
        self.norm2.on_vector_stats(dve, g, y_src)
        self.norm2.on_vector_apply(dve, g, y_src)

    def convolve(self, dve, g):
        q, w = self.q, self.w
        h = self.hT[:, :].rearrange("p (i t) -> p i t", i=GI)
        x = self.xT[:, :].rearrange("p (i t) -> p i t", i=GI)
        dve.wait_ge(q["h_ready"], g + 1)
        dve.tensor_scalar(x, h, w["conv"][:, 2:3], None, ALU.mult).then_inc(q["conv1"], 1)
        dve.wait_ge(q["conv1"], g + 1)
        for shift in (1, 2):
            dve.scalar_tensor_tensor(out=x[:, :, shift:T], in0=h[:, :, 0:T - shift], scalar=w["conv"][:, 2 - shift:3 - shift],
                                     in1=x[:, :, shift:T], op0=ALU.mult, op1=ALU.add).then_inc(q["conv2"], 1)
            dve.wait_ge(q["conv2"], g * 2 + shift)

    def rotate(self, dve, g):
        q, b, w = self.q, self.b, self.w
        for m, name in enumerate(("k", "q")):
            dve.wait_ge(q["full_ready"], g * 2 + m + 1)
            dve.wait_ge(q["t_made"], g * 2 + m + 1)
            for t, bank, table in ((self.t1, b[2 * m], w["c" + name]), (self.t2, b[2 * m + 1], w["s" + name])):
                ins = dve.tensor_tensor(t[m][:, :].rearrange("p (i t) -> p i t", i=GI),
                                        bank[:, :].rearrange("p (i t) -> p i t", i=GI),
                                        table.unsqueeze(1).to_broadcast([P, GI, T]), ALU.mult)
            ins.then_inc(q["roped"], 1)

    def own_pool(self, pool, g):
        q = self.q
        self.norm.on_pool(pool, g)
        self.norm2.on_pool(pool, g)
        for m in range(2):
            pool.wait_ge(q["roped"], g * 2 + m + 1)
            pool.tensor_tensor(self.full[m][:, :], self.t1[m][:, :], self.t2[m][:, :], ALU.add).then_inc(q["full_ready"], 1)


    def split_vector(self, dve, g, x):
        q = self.q
        first = 0 if self.cross else 2
        high, mid, low = (p[:, :] for p in self.parts[x])
        full, rest = self.full[x][:, :], self.rest[:, :]
        done = (g * 2 + x) * 3
        dve.wait_ge(q["full_ready"], first + g * 2 + x + 1)
        dve.tensor_copy(high, full).then_inc(q["split"], 1)
        dve.wait_ge(q["split"], done + 1)
        dve.tensor_tensor(rest, full, high, ALU.subtract).then_inc(q["split"], 1)
        dve.wait_ge(q["split"], done + 2)
        dve.tensor_copy(mid, rest).then_inc(q["split"], 1)
        dve.wait_ge(q["split"], done + 3)
        dve.tensor_tensor(low, rest, mid, ALU.subtract).then_inc(q["parts_ready"], 1)
        dve.wait_ge(q["parts_ready"], g * 2 + x + 1)

    def spread_tensor(self, pe, g, x):
        q = self.q
        if x == 0:
            pe.wait_ge(q["full_ready"], g * 2 + (2 if self.cross else 4))
            pe.wait_ge(q["v_ready"], g + 1)
            pe.wait_ge(q["expd"], g * GI * BANKS + 2)
        pe.wait_ge(q["parts_ready"], g * 2 + x + 1)
        for m in range(x * TILES, x * TILES + TILES):
            pe.wait_ge(q["odd_taken" if m % 2 else "even_taken"], g * TILES + m // 2 + 1)
            for p in range(3):
                ins = pe.matmul(self.b[m % 4][:, :], self.pick[x][:, p, m % TILES, :], self.parts[x][p][:, :],
                                start=p == 0, stop=p == 2)
            ins.then_inc(q["spread"], 1)

    def take_stacks(self, eng, g, x, odd):
        q = self.q
        copy = eng.tensor_copy if odd else eng.copy
        for m in range(x * TILES + odd, x * TILES + TILES, 2):
            eng.wait_ge(q["spread"], g * 2 * TILES + m + 1)
            copy(self.stack[x][:, m % TILES, :], self.b[m % 4][:, :])\
                .then_inc(q["odd_taken" if odd else "even_taken"], 1)


    def stacked(self, x, i, bank, slot):
        r, j = bank % 2, PLACES * (bank // 2) + slot
        return self.stack[x][HALF * r:HALF * r + HALF, j, i * T:(i + 1) * T]

    def first_scores(self, pe, g, i, pair):
        q, u = self.q, g * GI + i
        banks = (2 * pair, 2 * pair + 1)
        pe.wait_ge(q["maxed"], u * BANKS + 2 * pair + 2)
        if not self.cross:
            for bank in banks:
                pe.matmul(self.b[bank % 2][:, :], self.identb[:, :], self.maskb[:, :, :], start=True, stop=False,
                          skip_group_check=True)
        for slot in range(PLACES):
            for bank in banks:
                ins = pe.matmul(self.b[bank % 2][:, slot * T:(slot + 1) * T], self.stacked(1, i, bank, slot),
                                self.stacked(0, i, bank, slot), start=self.cross, stop=True, skip_group_check=True)
        ins.then_inc(q["scored"], 1)

    def second_scores(self, pe, g, i, pair):
        q, u = self.q, g * GI + i
        banks = (2 * pair, 2 * pair + 1)
        pe.wait_ge(q["expd"], u * BANKS + 2 * pair + 2)
        if not self.cross:
            for bank in banks:
                pe.matmul(self.b[2 + bank % 2][:, :], self.identb[:, :], self.maskTb[:, :, :], start=True, stop=False,
                          skip_group_check=True)
        for slot in range(PLACES):
            for bank in banks:
                pe.matmul(self.b[2 + bank % 2][:, slot * T:(slot + 1) * T], self.stacked(0, i, bank, slot),
                          self.stacked(1, i, bank, slot), start=self.cross, stop=False, skip_group_check=True)
            for bank in banks:
                ins = pe.matmul(self.b[2 + bank % 2][:, slot * T:(slot + 1) * T], self.sel[:, bank * PLACES + slot, :],
                                self.nT[:, :], start=False, stop=True, skip_group_check=True)
        ins.then_inc(q["scored2"], 1)

    def values(self, pe, g, i):
        q, u = self.q, g * GI + i
        pe.wait_ge(q["expd"], u * BANKS + BANKS + 2)
        pe.wait_ge(q["o_ready"], u + 1)
        for bank in range(BANKS):
            for slot in range(PLACES):
                ins = pe.matmul(self.b[5][32 * slot:32 * slot + 32, bank * T:(bank + 1) * T],
                                self.v[:, i, head_at(bank, slot), :],
                                self.PT[i % 2][:, bank, slot * T:(slot + 1) * T], start=True, stop=True)
        ins.then_inc(q["pv"], 1)

    def attend_tensor(self, pe, g, after):
        q, b, w, ident = self.q, self.b, self.w, self.k.ident
        pe.wait_ge(q["even_taken"], g * TILES + TILES + 2)
        pe.wait_ge(q["odd_taken"], g * TILES + TILES + 2)
        for t in range(GI + 4):
            one, two, three, four = (0 <= t - lag < GI for lag in (1, 2, 3, 4))
            u = g * GI + t
            if one:
                pe.wait_ge(q["n_ready"], u)
                pe.matmul(b[4][:, 0:T], self.nparts[:, :, :].rearrange("p a h -> p (a h)"), self.identb[:, :],
                          start=True, stop=True).then_inc(q["n_turned"], 1)
            if t < GI:
                self.first_scores(pe, g, t, 0)
            if three:
                pe.wait_ge(q["o_ready"], u - 1)
                pe.wait_ge(q["at_ready"], u - 2)
                for bank in range(BANKS):
                    ins = pe.transpose(b[6][:, bank * T:(bank + 1) * T], self.o[:, bank * T:(bank + 1) * T], ident[:, :])
                ins.then_inc(q["o_turned"], 1)
            if one:
                pe.wait_ge(q["nT_ready"], u)
                self.second_scores(pe, g, t - 1, 0)
            if four:
                pe.wait_ge(q["aT_ready"], u - 3)
                ins = pe.matmul(b[7][:, 0:D], self.aT[:, :], w["wo"], start=True, stop=not self.cross)
                if self.cross:
                    ins = pe.matmul(b[7][:, 0:D], w["one"], w["bo"], start=False, stop=True)
                ins.then_inc(q["out_made"], 1)
            if t < GI:
                self.first_scores(pe, g, t, 1)
            if two:
                self.values(pe, g, t - 2)
            if one:
                self.second_scores(pe, g, t - 1, 1)
            if three:
                pe.wait_ge(q["at_ready"], u - 1)
                pe.wait_ge(q["added"], u - 2)
                pe.transpose(b[7][:, 0:T], self.at[:, :, :, :].rearrange("p b s d -> p (b s d)"), ident[:, :])\
                  .then_inc(q["at_turned"], 1)
            after(t)

    def exponentials(self, act, g, i, pair):
        q, u = self.q, g * GI + i
        act.wait_ge(q["scored2"], u * 2 + pair + 1)
        for bank in (2 * pair, 2 * pair + 1):
            act.activation(self.PT[i % 2][:, bank, :], self.b[2 + bank % 2][:, :], ACT.Exp).then_inc(q["expd"], 1)

    def attend_scalar(self, act, g, after):
        q, b = self.q, self.b
        for t in range(GI + 4):
            one, two, three = (0 <= t - lag < GI for lag in (1, 2, 3))
            u = g * GI + t
            if one:
                act.wait_ge(q["n_turned"], u + 1)
                act.copy(self.nT[:, :], b[4][:, 0:T]).then_inc(q["nT_ready"], 1)
                act.wait_ge(q["pv"], u)
                self.exponentials(act, g, t - 1, 0)
            if two:
                act.wait_ge(q["pv"], u + 1)
                act.wait_ge(q["o_turned"], u - 1)
                act.copy(self.o[:, :], b[5][:, :]).then_inc(q["o_ready"], 1)
            if one:
                self.exponentials(act, g, t - 1, 1)
            if three:
                act.wait_ge(q["at_turned"], u - 2)
                act.copy(self.aT[:, :], b[7][:, 0:T]).then_inc(q["aT_ready"], 1)
            after(t)

    def maxima(self, dve, g, i, pair):
        q, u = self.q, g * GI + i
        dve.wait_ge(q["scored"], u * 2 + pair + 1)
        for bank in (2 * pair, 2 * pair + 1):
            dve.tensor_reduce(self.nm[:, bank * PLACES:(bank + 1) * PLACES],
                              self.b[bank % 2][:, :].rearrange("p (s t) -> p s t", s=PLACES), AX.X, ALU.max, negate=True)\
               .then_inc(q["maxed"], 1)

    def attend_vector(self, dve, g, after):
        q, b = self.q, self.b
        for t in range(GI + 4):
            three, four = (0 <= t - lag < GI for lag in (3, 4))
            u = g * GI + t
            if t < GI:
                self.maxima(dve, g, t, 0)
            if three:
                o = b[6][:, :].rearrange("p (b s c) -> p b s c", b=BANKS, s=PLACES)
                self.k.wait_alone(dve, q["o_turned"], u - 1)
                dve.reciprocal(self.inverse[:, :, :], o[:, :, :, DH]).then_inc(q["inverted"], 1)
                dve.wait_ge(q["inverted"], u - 2)
                dve.tensor_tensor(self.at[:, :, :, :], o[:, :, :, 0:DH],
                                  self.inverse[:, :, :].unsqueeze(3).to_broadcast([T, BANKS, PLACES, DH]), ALU.mult)\
                   .then_inc(q["at_ready"], 1)
            if t < GI:
                self.maxima(dve, g, t, 1)
                high, mid, low = (self.nparts[:, a, :] for a in range(3))
                dve.wait_ge(q["maxed"], u * BANKS + BANKS + 2)
                dve.wait_ge(q["n_turned"], u + 1)
                dve.tensor_copy(high, self.nm[:, :]).then_inc(q["nsplit"], 1)
                dve.wait_ge(q["nsplit"], u * 3 + 1)
                dve.tensor_tensor(self.nr[:, :], self.nm[:, :], high, ALU.subtract).then_inc(q["nsplit"], 1)
                dve.wait_ge(q["nsplit"], u * 3 + 2)
                dve.tensor_copy(mid, self.nr[:, :]).then_inc(q["nsplit"], 1)
                dve.wait_ge(q["nsplit"], u * 3 + 3)
                dve.tensor_tensor(low, self.nr[:, :], mid, ALU.subtract).then_inc(q["n_ready"], 1)
                dve.wait_ge(q["n_ready"], u + 1)
            if four:
                x = self.dst[:, u - 4, :]
                dve.wait_ge(q["out_made"], u - 3)
                dve.tensor_tensor(x, b[7][:, 0:D], x, ALU.add).then_inc(q["added"], 1)
            after(t)


def over_groups(eng, prepare, attend):
    for _, work in prepare:
        work(eng, 0)

    def after(t, g):
        for step, work in prepare:
            if step == t:
                work(eng, g)

    with eng.Fori(0, NG - 1) as g:
        attend(eng, g, lambda t: after(t, g + 1))
    attend(eng, NG - 1, lambda t: None)


def sublayer_soft_attention(k, s, n):
    a = SoftAttention(k, s, n, UNITS[n])
    q, w = a.q, a.w
    with k.nc.Block() as block:
        @block.sync
        def _(sp):
            k.load(sp, n + 1)

        @block.gpsimd
        def _(pool):
            a.constants_pool(pool)
            if not a.cross:
                pool.sem_inc(q["full_ready"], 2)
            with pool.Fori(0, NG) as g:
                if a.cross:
                    k.wait_alone(pool, q["v_made"], g + 1)
                    pool.tensor_copy(a.cG[:, :, :], k.cT[:, bass.ds(g * GI, GI), :]).then_inc(q["cG_ready"], 1)
                    a.norm.on_pool(pool, g)
                else:
                    a.own_pool(pool, g)

        @block.tensor
        def _(pe):
            pe.wait_ge(a.loaded, a.count)
            pe.wait_ge(q["zeroed"], 1)
            if not a.cross:
                pe.wait_ge(q["masks"], 2)
            pe.sem_inc(q["pv"], 2)
            pe.sem_inc(q["v_made"], 1)
            pe.sem_inc(q["o_turned"], 1)
            pe.sem_inc(q["n_turned"], 1)
            make = a.project_tensor if a.cross else a.own_tensor
            over_groups(pe, [(3, lambda eng, g: make(eng, g, 0)), (4 if a.cross else 5, lambda eng, g: make(eng, g, 1)),
                             (5 if a.cross else 7, lambda eng, g: a.spread_tensor(eng, g, 0)),
                             (6 if a.cross else 7, lambda eng, g: a.spread_tensor(eng, g, 1))], a.attend_tensor)

        @block.scalar
        def _(act):
            act.wait_ge(a.loaded, a.count)
            act.wait_ge(q["zeroed"], 1)
            act.sem_inc(q["expd"], 2)
            act.sem_inc(q["o_ready"], 1)
            act.sem_inc(q["even_taken"], 2)
            if a.cross:
                act.activation(a.bqs[:, :], w["bq"], ACT.Identity, scale=a.SCALE).then_inc(q["bias_scaled"], 1)
                act.wait_ge(q["bias_scaled"], 1)
            else:
                act.copy(a.maskb[:, :, :], w["mask"].unsqueeze(1).to_broadcast([T, PLACES, T])).then_inc(q["masks"], 1)
                act.copy(a.maskTb[:, :, :], w["maskT"].unsqueeze(1).to_broadcast([T, PLACES, T])).then_inc(q["masks"], 1)
            if a.cross:
                make = [(3, lambda eng, g: a.project_scalar(eng, g, 0)), (4, lambda eng, g: a.project_scalar(eng, g, 1))]
            else:
                make = [(3, a.own_scalar)]
            over_groups(act, [*make, (5, a.take_v), (5 if a.cross else 7, lambda eng, g: a.take_stacks(eng, g, 0, 0)),
                              (6 if a.cross else 7, lambda eng, g: a.take_stacks(eng, g, 1, 0))], a.attend_scalar)

        @block.vector
        def _(dve):
            dve.wait_ge(q["zeroed"], 1)
            dve.wait_ge(a.loaded, a.count)
            dve.sem_inc(q["maxed"], 2)
            dve.sem_inc(q["added"], 1)
            dve.sem_inc(q["at_ready"], 1)
            dve.sem_inc(q["odd_taken"], 2)
            split = lambda x: lambda eng, g: a.split_vector(eng, g, x)
            take = lambda x: lambda eng, g: a.take_stacks(eng, g, x, 1)
            if a.cross:
                prepare = [(2, a.project_vector), (4, split(0)), (5, split(1)), (5, take(0)), (6, take(1))]
            else:
                prepare = [(2, a.own_norms), (4, a.convolve), (5, a.rotate), (6, split(0)), (6, split(1)), (7, take(0)),
                           (7, take(1))]
            over_groups(dve, prepare, a.attend_vector)


def cross_pack(wq, bq, wk, bk, wv, bv, wo, bo):
    return {"wq": wq, "bq": bq, "wk": np.concatenate([wk, bk[None]]), "wv": np.concatenate([wv, bv[None]]),
            "wo": output_rows(wo), "bo": bo, "one": np.ones((1, T), np.float32)}


def pack_l0x(a):
    wkv = a["L0_xattn_Wkv"].reshape(H, 2, DH, C)
    bkv = a["L0_xattn_bkv"].reshape(H, 2, DH)
    return cross_pack(a["L0_xattn_Wq"].T, a["L0_xattn_bq"], wkv[:, 0].reshape(D, C).T, bkv[:, 0].reshape(D),
                      wkv[:, 1].reshape(D, C).T, bkv[:, 1].reshape(D), a["L0_xattn_Wo"].T, a["L0_xattn_bo"])


def pack_l1x(a):
    z = np.zeros(D, np.float32)
    return cross_pack(a["L1_xattn_Wq"].T, z, a["L1_xattn_Wk"].T, z, a["L1_xattn_Wv"].T, z, a["L1_xattn_Wo"].T, z)


def pack_l2x(a):
    return cross_pack(*(a["L2_xattn_" + x].T for x in ("Wq", "bq", "Wk", "bk", "Wv", "bv", "Wo", "bo")))


def rotary(width, copies_at, scale):
    f = 1.0 / (10000.0 ** (np.arange(0, width, 2, dtype=np.float32) / np.float32(width)))
    angle = np.arange(T, dtype=np.float32)[:, None] * f.astype(np.float32)[None]
    cos, sin = np.zeros((P, T), np.float32), np.zeros((P, T), np.float32)
    for d in range(width):
        for row in copies_at(d):
            cos[row] = np.cos(angle[:, d % (width // 2)]) * scale
            sin[row] = np.sin(angle[:, d % (width // 2)]) * (-scale if d < width // 2 else scale)
    return cos, sin


def pack_l0g(a):
    wq, wk, wv = (a["L0_ffn_attn_w"][:, i * D:(i + 1) * D] for i in range(3))
    rows = lambda d: [h * DH + d for h in range(H)]
    cq, sq = rotary(DH, rows, float(DH) ** -0.5)
    ck, sk = rotary(DH, rows, 1.0)
    allowed = np.tril(np.ones((T, T), bool))
    mask = np.where(allowed, 0.0, -1e30).astype(np.float32)
    return {"wq": wq, "wqp": partners(wq), "wk": wk, "wkp": partners(wk), "wv": wv,
            "wo": output_rows(a["L0_ffn_proj_w"]), "ln1_w": a["L0_ffn_ln1_w"], "ln1_b": a["L0_ffn_ln1_b"],
            "conv": a["L0_ffn_conv_w"], "cq": cq, "sq": sq, "ck": ck, "sk": sk, "mask": mask, "maskT": mask.T}



RH, RK, RV = 4, 32, 64
PACKS["l0a"] = Pack(("wq", D, D), ("wqp", D, D), ("wk", D, D), ("wkp", D, D), ("wvg", D, 4 * D), ("wo", P, 2 * D),
                    ("gn", P, 1), ("cq", P, T), ("sq", P, T), ("ck", P, T), ("sk", P, T), ("decay", T, RH * T))


def sublayer_retention(k, s, n):
    nc, X, ident = k.nc, k.X, k.ident
    w, loaded, count = k.weights(n)
    norm = Norm(k, s.sb, s.sem, "ln")
    wo = s.sb("wo", [P, 2, D])
    xT = s.sb("xT", [D, GT])
    part = [s.sb(f"part{i}", [D, GT]) for i in range(4)]
    qT, kT = s.sb("qT", [D, GT]), s.sb("kT", [D, GT])
    vg = s.sb("vg", [T, GI, 2, RH * RV])
    PT = s.sb("PT", [T, RH, GT])
    osq = [s.sb(f"osq{i}", [T, RH, RV]) for i in range(2)]
    ss, sse, rr = s.sb("ss", [T, RH]), s.sb("sse", [T, RH]), s.sb("rr", [T, RH])
    on = s.sb("on", [T, RH, RV])
    og = [s.sb(f"og{i}", [T, RH * RV]) for i in range(2)]
    ogT = s.sb("ogT", [P, 2, T])
    b = s.banks(8)
    q = {x: s.sem(x) for x in ("gained xT_ready qk_made parts qk_ready vg_made vg_ready scored decayed o_made squared summed "
                               "meaned rooted on_ready og_ready og_turned ogT_ready out_made added").split()}

    with nc.Block() as block:
        @block.sync
        def _(sp):
            k.load(sp, n + 1)

        @block.gpsimd
        def _(pool):
            def group(g, more):
                pool.wait_ge(q["parts"], g + 1)
                pool.tensor_tensor(qT[:, :], part[0][:, :], part[1][:, :], ALU.add)
                pool.tensor_tensor(kT[:, :], part[2][:, :], part[3][:, :], ALU.add).then_inc(q["qk_ready"], 1)
                for i in range(GI):
                    u = g * GI + i
                    if i == 1 and more:
                        norm.on_pool(pool, g + 1)
                    k.wait_alone(pool, q["summed"], u + 1)
                    pool.tensor_scalar(sse[:, :], ss[:, :], 1.0 / RV, LN_EPS, ALU.mult, ALU.add).then_inc(q["meaned"], 1)
                    pool.wait_ge(q["meaned"], u + 1)
                    pool.tensor_tensor(rr[:, :], sse[:, :], k.half[:, 0:RH], ALU.pow).then_inc(q["rooted"], 1)

            norm.on_pool(pool, 0)
            with pool.Fori(0, NG - 1) as g:
                group(g, True)
            group(NG - 1, False)

        @block.tensor
        def _(pe):
            pe.wait_ge(loaded, count)
            with pe.Fori(0, NG) as g:
                norm.on_tensor(pe, g, b[6])
                pe.wait_ge(q["xT_ready"], g + 1)
                pe.wait_ge(q["added"], g * GI + 1)
                for j, name in enumerate(("wq", "wqp", "wk", "wkp")):
                    ins = pe.matmul(b[j][:, :], w[name], xT[:, :], start=True, stop=True)
                ins.then_inc(q["qk_made"], 1)
                for i in range(GI):
                    u = g * GI + i
                    pe.wait_ge(q["vg_ready"], u + 1)
                    pe.matmul(b[4 + i % 2][:, :], xT[:, i * T:(i + 1) * T], w["wvg"], start=True, stop=True)\
                      .then_inc(q["vg_made"], 1)
                pe.wait_ge(q["qk_ready"], g + 1)
                for h in range(RH):
                    for i in range(GI):
                        ins = pe.matmul(b[h][:, i * T:(i + 1) * T], kT[RK * h:RK * (h + 1), i * T:(i + 1) * T],
                                        qT[RK * h:RK * (h + 1), i * T:(i + 1) * T], start=True, stop=True)
                    ins.then_inc(q["scored"], 1)
                pe.wait_ge(q["decayed"], g * RH + RH)
                pe.wait_ge(q["vg_ready"], g * GI + GI + 2)
                for t in range(GI + 2):
                    if t < GI:
                        for h in range(RH):
                            ins = pe.matmul(b[6 + t % 2][:, h * RV:(h + 1) * RV], PT[:, h, t * T:(t + 1) * T],
                                            vg[:, t, 0, h * RV:(h + 1) * RV], start=True, stop=True)
                        ins.then_inc(q["o_made"], 1)
                    if 0 <= t - 2 < GI:
                        u = g * GI + t - 2
                        pe.wait_ge(q["ogT_ready"], u + 1)
                        pe.wait_ge(q["added"], u + 1)
                        for c in range(2):
                            ins = pe.matmul(b[0][:, 0:D], ogT[:, c, :], wo[:, c, :], start=(c == 0), stop=(c == 1))
                        ins.then_inc(q["out_made"], 1)
                    if 0 <= t - 1 < GI:
                        u = g * GI + t - 1
                        pe.wait_ge(q["og_ready"], u + 1)
                        for c in range(2):
                            ins = pe.transpose(b[4][:, c * T:(c + 1) * T], og[(t - 1) % 2][:, c * P:(c + 1) * P], ident[:, :])
                        ins.then_inc(q["og_turned"], 1)

        @block.scalar
        def _(act):
            act.sem_inc(q["vg_ready"], 2)
            with act.Fori(0, NG) as g:
                act.wait_ge(norm.turned, g + 1)
                act.copy(xT[:, :], b[6][:, :]).then_inc(q["xT_ready"], 1)
                for i in range(GI):
                    u = g * GI + i
                    act.wait_ge(q["vg_made"], u + 1)
                    act.copy(vg[:, i, :, :], b[4 + i % 2][:, :].rearrange("p (c x) -> p c x", c=2)).then_inc(q["vg_ready"], 1)
                for t in range(GI + 1):
                    if t < GI:
                        act.wait_ge(q["o_made"], g * GI + t + 1)
                        act.activation(osq[t % 2][:, :, :], b[6 + t % 2][:, 0:RH * RV].rearrange("p (h d) -> p h d", h=RH), ACT.Square)\
                           .then_inc(q["squared"], 1)
                    if t >= 1:
                        act.wait_ge(q["og_turned"], g * GI + t)
                        act.copy(ogT[:, :, :], b[4][:, 0:2 * T].rearrange("p (c t) -> p c t", c=2)).then_inc(q["ogT_ready"], 1)

        @block.vector
        def _(dve):
            dve.wait_ge(loaded, count)
            dve.tensor_scalar(wo[:, :, :], w["wo"].rearrange("p (c d) -> p c d", c=2), w["gn"], None, ALU.mult)\
               .then_inc(q["gained"], 1)
            dve.wait_ge(q["gained"], 1)
            dve.sem_inc(q["added"], 1)

            def rows_normed(m):
                def src(i):
                    return X[:, m * GI + i, :]
                norm.on_vector_stats(dve, m, src)
                norm.on_vector_apply(dve, m, src)

            def group(g, more):
                def src(i):
                    return X[:, g * GI + i, :]
                dve.wait_ge(q["qk_made"], g + 1)
                for j, name in enumerate(("cq", "sq", "ck", "sk")):
                    ins = dve.tensor_tensor(part[j][:, :].rearrange("p (i t) -> p i t", i=GI),
                                            b[j][:, :].rearrange("p (i t) -> p i t", i=GI),
                                            w[name].unsqueeze(1).to_broadcast([P, GI, T]), ALU.mult)
                ins.then_inc(q["parts"], 1)
                decay = w["decay"].rearrange("p (h t) -> p h t", h=RH)
                for h in range(RH):
                    dve.wait_ge(q["scored"], g * RH + h + 1)
                    dve.tensor_tensor(PT[:, h, :].rearrange("p (i t) -> p i t", i=GI),
                                      b[h][:, :].rearrange("p (i t) -> p i t", i=GI),
                                      decay[:, h, :].unsqueeze(1).to_broadcast([T, GI, T]), ALU.mult).then_inc(q["decayed"], 1)
                for t in range(GI + 2):
                    if t == 1 and more:
                        rows_normed(g + 1)
                    if 0 <= t - 2 < GI:
                        u = g * GI + t - 2
                        dve.wait_ge(q["out_made"], u + 1)
                        dve.tensor_tensor(src(t - 2), b[0][:, 0:D], src(t - 2), ALU.add).then_inc(q["added"], 1)
                    if t < GI:
                        u = g * GI + t
                        o = b[6 + t % 2][:, 0:RH * RV].rearrange("p (h d) -> p h d", h=RH)
                        dve.wait_ge(q["squared"], u + 1)
                        dve.tensor_reduce(ss[:, :], osq[t % 2][:, :, :], AX.X, ALU.add).then_inc(q["summed"], 1)
                        dve.wait_ge(q["rooted"], u + 1)
                        dve.tensor_tensor(on[:, :, :], o, rr[:, :].unsqueeze(2).to_broadcast([T, RH, RV]), ALU.mult)\
                           .then_inc(q["on_ready"], 1)
                        dve.wait_ge(q["on_ready"], u + 1)
                        dve.tensor_tensor(og[t % 2][:, :], on[:, :, :].rearrange("p h d -> p (h d)"), vg[:, t, 1, :], ALU.mult)\
                           .then_inc(q["og_ready"], 1)

            rows_normed(0)
            with dve.Fori(0, NG - 1) as g:
                group(g, True)
            group(NG - 1, False)


def pack_l0a(a):
    partner = [(c // RK) * RK + (c % RK + RK // 2) % RK for c in range(D)]
    rows = lambda d: [RK * h + d for h in range(RH)]
    cq, sq = rotary(RK, rows, float(RK) ** -0.5)
    ck, sk = rotary(RK, rows, 1.0)
    gamma = 1.0 - np.exp2(-5.0 - np.arange(RH, dtype=np.float32))
    steps = (np.arange(T)[None, :] - np.arange(T)[:, None]).astype(np.float32)
    decay = np.where(steps >= 0, gamma[:, None, None] ** np.maximum(steps, 0), 0.0).astype(np.float32)
    return {"wq": a["L0_attn_Wq"], "wqp": a["L0_attn_Wq"][:, partner], "wk": a["L0_attn_Wk"], "wkp": a["L0_attn_Wk"][:, partner],
            "wvg": np.concatenate([a["L0_attn_Wv"], a["L0_attn_Wg"]], 1),
            "wo": a["L0_attn_Wo"].reshape(2, P, D).transpose(1, 0, 2),
            "gn": np.concatenate([a["L0_attn_gn_weight"], a["L0_attn_gn_weight"]]),
            "cq": cq, "sq": sq, "ck": ck, "sk": sk, "decay": decay.transpose(1, 0, 2)}



LAYERS = 12
LAYER_COLS = D + 2 * D + D + 2 + 2 * D
PACKS["l1a"] = Pack(("blocks", D, D),)


def sublayer_linear(k, s, n):
    nc, X, ident = k.nc, k.X, k.ident
    w, loaded, count = k.weights(n)
    norm = Norm(k, s.sb, s.sem, "ln")
    RT = s.sb("RT", [D, NB * T])
    buf = [s.sb(f"layer{i}", [P, LAYER_COLS]) for i in range(2)]
    qT = [s.sb(f"qT{i}", [D, GT]) for i in range(4)]
    kv = [s.sb(f"kv{i}", [T, GI, 2 * D]) for i in range(2)]
    M = [s.sb(f"M{i}", [D, GT]) for i in range(2)]
    yT = [s.sb(f"yT{i}", [D, GT]) for i in range(2)]
    bQ, bK0, bK1, bM, bY, bR, bX0, bX1 = s.banks(8)
    bK = (bK0, bK1)
    q = {x: s.sem(x) for x in ("RT_set streamed0 streamed1 layer_done q_made q_ready kv_made kv_ready m_made m_ready y_made "
                               "y_ready r_made r_ready back added").split()}
    STEPS = 2 * NG

    with nc.Block() as block:
        @block.sync
        def _(sp):
            k.load(sp, n + 1)
            sp.sem_inc(q["layer_done"], 2)
            with sp.Fori(0, LAYERS // 2) as pair:
                for l in range(2):
                    sp.wait_ge(q["layer_done"], pair * 2 + l + 1)
                    sp.dma_start(buf[l][:, :], k.dram["layers_l1a"][bass.ds(pair * 2 + l, 1), :, :]
                                 .rearrange("o p c -> (o p) c")).then_inc(q[f"streamed{l}"], 16)

        @block.gpsimd
        def _(pool):
            with pool.Fori(0, NG) as g:
                norm.on_pool(pool, g)

        @block.tensor
        def _(pe):
            pe.wait_ge(loaded, count)
            pe.sem_inc(norm.turned, 1)
            with pe.Fori(0, NG) as g:
                pe.wait_ge(q["RT_set"], g + 1)
                norm.on_tensor(pe, g, bX0)
            pe.wait_ge(q["RT_set"], NG + 1)
            with pe.Fori(0, LAYERS // 2) as pair:
                for t in range(STEPS + 3):
                    if 0 <= t - 2 < STEPS:
                        x = t - 2
                        u = pair * STEPS + x
                        pe.wait_ge(q["m_ready"], u + 1)
                        pe.wait_ge(q["q_ready"], u + 2)
                        pe.wait_ge(q["y_ready"], u + 1)
                        for i in range(GI):
                            ins = pe.matmul(bY[:, i * T:(i + 1) * T], M[x % 2][:, i * D:(i + 1) * D],
                                            qT[x % 4][:, i * T:(i + 1) * T], start=True, stop=True)
                        ins.then_inc(q["y_made"], 1)
                    if 0 <= t - 3 < STEPS:
                        x = t - 3
                        u = pair * STEPS + x
                        pe.wait_ge(q["y_ready"], u + 2)
                        pe.wait_ge(q["r_ready"], u + 4)
                        pe.matmul(bR[:, :], buf[x // NG][:, 3 * D:4 * D], yT[x % 2][:, :], start=True, stop=True)\
                          .then_inc(q["r_made"], 1)
                    if 0 <= t - 1 < STEPS:
                        x = t - 1
                        u = pair * STEPS + x
                        pe.wait_ge(q["kv_ready"], u + 1)
                        for i in range(GI):
                            ins = pe.matmul(bM[:, i * D:(i + 1) * D], kv[x % 2][:, i, 0:D], kv[x % 2][:, i, D:2 * D],
                                            start=True, stop=True)
                        ins.then_inc(q["m_made"], 1)
                    if t < STEPS:
                        l, g = t // NG, t % NG
                        u = pair * STEPS + t
                        if g == 0:
                            pe.wait_ge(q[f"streamed{l}"], pair * 16 + 16)
                        pe.wait_ge(q["r_ready"], u + 1)
                        pe.wait_ge(q["q_ready"], u + 1)
                        pe.matmul(bQ[:, :], buf[l][:, 0:D], RT[:, g * GT:(g + 1) * GT], start=True, stop=True)\
                          .then_inc(q["q_made"], 1)
                        for i in range(GI):
                            ins = pe.matmul(bK[i // 2][:, (i % 2) * 2 * D:(i % 2 + 1) * 2 * D],
                                            RT[:, (g * GI + i) * T:(g * GI + i + 1) * T], buf[l][:, D:3 * D],
                                            start=True, stop=True)
                        ins.then_inc(q["kv_made"], 1)
            for g in range(NG):
                bank = (bX0, bX1)[g % 2]
                pe.wait_ge(q["r_ready"], LAYERS * NG + 4)
                if g >= 2:
                    pe.wait_ge(q["added"], g - 1)
                for i in range(GI):
                    ins = pe.transpose(bank[:, i * D:(i + 1) * D], RT[:, (g * GI + i) * T:(g * GI + i + 1) * T], ident[:, :])
                ins.then_inc(q["back"], 1)

        @block.scalar
        def _(act):
            act.sem_inc(q["RT_set"], 1)
            act.sem_inc(q["q_ready"], 1)
            act.sem_inc(q["y_ready"], 1)
            with act.Fori(0, NG) as g:
                act.wait_ge(norm.turned, g + 2)
                act.copy(RT[:, bass.ds(g * GT, GT)], bX0[:, :]).then_inc(q["RT_set"], 1)
            with act.Fori(0, LAYERS // 2) as pair:
                for t in range(STEPS + 2):
                    if 0 <= t - 2 < STEPS:
                        x = t - 2
                        act.wait_ge(q["y_made"], pair * STEPS + x + 1)
                        act.copy(yT[x % 2][:, :], bY[:, :]).then_inc(q["y_ready"], 1)
                    if t < STEPS:
                        if t % NG == 0:
                            act.wait_ge(q[f"streamed{t // NG}"], pair * 16 + 16)
                        act.wait_ge(q["q_made"], pair * STEPS + t + 1)
                        act.activation(qT[t % 4][:, :], bQ[:, :], ACT.Identity, bias=buf[t // NG][:, 4 * D:4 * D + 1])\
                           .then_inc(q["q_ready"], 1)

        @block.vector
        def _(dve):
            dve.wait_ge(loaded, count)
            dve.sem_inc(q["r_ready"], 4)
            with dve.Fori(0, NG) as g:
                def src(i):
                    return X[:, g * GI + i, :]
                norm.on_vector_stats(dve, g, src)
                dve.wait_ge(norm.turned, g + 1)
                norm.on_vector_apply(dve, g, src)
            dve.wait_ge(q["RT_set"], NG + 1)
            with dve.Fori(0, LAYERS // 2) as pair:
                for t in range(STEPS + 3):
                    if 0 <= t - 3 < STEPS:
                        x = t - 3
                        u = pair * STEPS + x
                        state = RT[:, (x % NG) * GT:(x % NG + 1) * GT]
                        dve.wait_ge(q["r_made"], u + 1)
                        dve.wait_ge(q["r_ready"], u + 1)
                        dve.scalar_tensor_tensor(out=state, in0=bR[:, :], scalar=buf[x // NG][:, 4 * D + 1:4 * D + 2],
                                                 in1=state, op0=ALU.add, op1=ALU.add).then_inc(q["r_ready"], 1)
                        if x % NG == NG - 1:
                            dve.wait_ge(q["r_ready"], u + 5)
                            dve.sem_inc(q["layer_done"], 1)
                    if 0 <= t - 1 < STEPS:
                        x = t - 1
                        dve.wait_ge(q["m_made"], pair * STEPS + x + 1)
                        dve.tensor_tensor(M[x % 2][:, :].rearrange("p (i d) -> p i d", i=GI),
                                          bM[:, :].rearrange("p (i d) -> p i d", i=GI),
                                          w["blocks"].unsqueeze(1).to_broadcast([D, GI, D]), ALU.mult).then_inc(q["m_ready"], 1)
                    if t < STEPS:
                        bias = buf[t // NG][:, 4 * D + 2:6 * D + 2].unsqueeze(1).to_broadcast([T, 2, 2 * D])
                        if t % NG == 0:
                            dve.wait_ge(q[f"streamed{t // NG}"], pair * 16 + 16)
                        dve.wait_ge(q["kv_made"], pair * STEPS + t + 1)
                        for c in range(2):
                            ins = dve.tensor_tensor(kv[t % 2][:, 2 * c:2 * c + 2, :],
                                                    bK[c][:, :].rearrange("p (i d) -> p i d", i=2), bias, ALU.add)
                        ins.then_inc(q["kv_ready"], 1)
            for g in range(NG):
                x = X[:, g * GI:(g + 1) * GI, :]
                dve.wait_ge(q["back"], g + 1)
                dve.tensor_tensor(x, (bX0, bX1)[g % 2][:, :].rearrange("p (i d) -> p i d", i=GI), x, ALU.add)\
                   .then_inc(q["added"], 1)


def pack_l1a(a):
    head = np.arange(D) // 8
    return {"blocks": (head[:, None] == head[None, :]).astype(np.float32) * np.float32(8.0 ** -0.5)}


def stream_l1a(a):
    wqkv, bqkv = a["L1_attn_Wqkv"].transpose(0, 2, 1), a["L1_attn_bqkv"]
    return {"layers_l1a": np.concatenate([
        wqkv, a["L1_attn_Wproj"].transpose(0, 2, 1), bqkv[:, 0:D, None], a["L1_attn_bproj"][:, :, None],
        np.broadcast_to(bqkv[:, None, D:], (LAYERS, P, 2 * D))], 2)}



PACKS["l2a"] = Pack(("wqkv", D, 3 * D), ("bias", P, 3 * D))


def sublayer_over_sequences(k, s, n):
    nc, X, ident = k.nc, k.X, k.ident
    w, loaded, count = k.weights(n)
    SCALE = float(DH) ** -0.5
    norm = Norm(k, s.sb, s.sem, "ln")
    xT = s.sb("xT", [D, GT])
    qkv = s.sb("qkv", [P, NB, 3 * D])
    S = s.sb("S", [P, NB, H, NB])
    prod = [s.sb(f"prod{i}", [P, NB * D]) for i in range(2)]
    nmax, den, inv = s.sb("nmax", [P, NB * H]), s.sb("den", [P, NB * H]), s.sb("inv", [P, NB * H])
    o = s.sb("o", [P, NB, D])
    b = s.banks(8)
    q = {x: s.sem(x) for x in ("xT_ready qkv_made qkv_ready filled mult reduced maxed shifted expd summed plus_one inverted "
                               "o_mult o_reduced o_scaled").split()}

    with nc.Block() as block:
        @block.sync
        def _(sp):
            k.load(sp, n + 1)

        @block.gpsimd
        def _(pool):
            pool.memset(S[:, :, :, :], -1e30).then_inc(q["filled"], 1)
            with pool.Fori(0, NG) as g:
                norm.on_pool(pool, g)

        @block.tensor
        def _(pe):
            pe.wait_ge(loaded, count)
            with pe.Fori(0, NG) as g:
                pe.wait_ge(q["xT_ready"], g + 1)
                norm.on_tensor(pe, g, b[4])
                pe.wait_ge(q["xT_ready"], g + 2)
                for i in range(GI):
                    pe.wait_ge(q["qkv_ready"], g * GI + i + 1)
                    pe.matmul(b[i][:, 0:3 * D], xT[:, i * T:(i + 1) * T], w["wqkv"], start=True, stop=True)\
                      .then_inc(q["qkv_made"], 1)

        @block.scalar
        def _(act):
            act.sem_inc(q["xT_ready"], 1)
            with act.Fori(0, NG) as g:
                act.wait_ge(norm.turned, g + 1)
                act.copy(xT[:, :], b[4][:, :]).then_inc(q["xT_ready"], 1)
            for i in range(NB):
                act.wait_ge(q["shifted"], i + 1)
                act.activation(S[:, i, :, :], S[:, i, :, :], ACT.Exp, scale=SCALE).then_inc(q["expd"], 1)

        @block.vector
        def _(dve):
            dve.wait_ge(loaded, count)
            dve.sem_inc(q["qkv_ready"], 4)
            with dve.Fori(0, NG) as g:
                def src(i):
                    return X[:, g * GI + i, :]
                norm.on_vector_stats(dve, g, src)
                norm.on_vector_apply(dve, g, src)
                for i in range(GI):
                    dve.wait_ge(q["qkv_made"], g * GI + i + 1)
                    dve.tensor_tensor(qkv[:, bass.ds(g * GI + i, 1), :].rearrange("p o c -> p (o c)"), b[i][:, 0:3 * D],
                                      w["bias"], ALU.add).then_inc(q["qkv_ready"], 1)
            dve.wait_ge(q["qkv_ready"], NB + 4)
            dve.wait_ge(q["filled"], 1)
            for i in range(NB + 1):
                if i < NB:
                    if i >= 2:
                        dve.wait_ge(q["reduced"], i - 1)
                    dve.tensor_tensor(prod[i % 2][:, 0:(i + 1) * D].rearrange("p (j c) -> p j c", c=D),
                                      qkv[:, 0:i + 1, D:2 * D],
                                      qkv[:, i:i + 1, 0:D].to_broadcast([P, i + 1, D]), ALU.mult).then_inc(q["mult"], 1)
                if i >= 1:
                    m = i - 1
                    dve.wait_ge(q["mult"], m + 1)
                    dve.tensor_reduce(S[:, m, :, 0:m + 1].rearrange("p h j -> p j h"),
                                      prod[m % 2][:, 0:(m + 1) * D].rearrange("p (j h d) -> p j h d", h=H, d=DH),
                                      AX.X, ALU.add).then_inc(q["reduced"], 1)
            dve.wait_ge(q["reduced"], NB)
            rows = S[:, :, :, :].rearrange("p i h j -> p (i h) j")
            dve.tensor_reduce(nmax[:, :], rows, AX.X, ALU.max).then_inc(q["maxed"], 1)
            dve.wait_ge(q["maxed"], 1)
            for i in range(NB):
                dve.tensor_tensor(S[:, i, :, :], S[:, i, :, :], nmax[:, i * H:(i + 1) * H].unsqueeze(2).to_broadcast([P, H, NB]),
                                  ALU.subtract).then_inc(q["shifted"], 1)
            dve.wait_ge(q["expd"], NB)
            dve.tensor_reduce(den[:, :], rows, AX.X, ALU.add).then_inc(q["summed"], 1)
            dve.wait_ge(q["summed"], 1)
            dve.tensor_scalar(inv[:, :], den[:, :], 1.0, None, ALU.add).then_inc(q["plus_one"], 1)
            dve.wait_ge(q["plus_one"], 1)
            dve.reciprocal(den[:, :], inv[:, :]).then_inc(q["inverted"], 1)
            dve.wait_ge(q["inverted"], 1)
            for i in range(NB + 1):
                if i < NB:
                    if i >= 2:
                        dve.wait_ge(q["o_reduced"], i - 1)
                    dve.tensor_tensor(prod[i % 2][:, 0:(i + 1) * D].rearrange("p (j h d) -> p j h d", h=H, d=DH),
                                      qkv[:, 0:i + 1, 2 * D:3 * D].rearrange("p j (h d) -> p j h d", h=H),
                                      S[:, i, :, 0:i + 1].rearrange("p h j -> p j h").unsqueeze(3)
                                      .to_broadcast([P, i + 1, H, DH]), ALU.mult).then_inc(q["o_mult"], 1)
                if i >= 1:
                    m = i - 1
                    dve.wait_ge(q["o_mult"], m + 1)
                    dve.tensor_reduce(o[:, m, :], prod[m % 2][:, 0:(m + 1) * D].rearrange("p (j c) -> p c j", c=D),
                                      AX.X, ALU.add).then_inc(q["o_reduced"], 1)
            dve.wait_ge(q["o_reduced"], NB)
            oh = o[:, :, :].rearrange("p i (h d) -> p (i h) d", h=H)
            dve.tensor_tensor(oh, oh, den[:, :].unsqueeze(2).to_broadcast([P, NB * H, DH]), ALU.mult).then_inc(q["o_scaled"], 1)
            dve.wait_ge(q["o_scaled"], 1)
            dve.tensor_tensor(X[:, :, :], X[:, :, :], o[:, :, :], ALU.add)


def pack_l2a(a):
    bias = np.concatenate([a["L2_attn_bq"], a["L2_attn_bk"], a["L2_attn_bv"]])
    return {"wqkv": np.concatenate([a["L2_attn_Wq"].T, a["L2_attn_Wk"].T, a["L2_attn_Wv"].T], 1),
            "bias": np.broadcast_to(bias[None], (P, 3 * D))}



FF = 4 * D
FC = FF // P
PACKS["l1f"] = Pack(("router", D, 8), ("b2", 8, D))
PACKS["l0f"] = Pack(("router", D, 4), ("ln2_w", D, 1), ("ln2_b", D, 1))
PACKS["l2f"] = Pack(("router", D, 8), ("b2", 9, D), ("gate_bias", P, 8))
EXPERT_COLS = {"l0f": 3 * FF, "l1f": 2 * FF + FC, "l2f": 2 * FF + FC}


class Moe:

    def __init__(self, k, s, n, kind):
        self.k, self.s, self.n, self.kind = k, s, n, kind
        self.w, self.loaded, self.count = k.weights(n)
        self.gated = kind == "l0f"
        self.shared = kind == "l2f"
        self.NR = 4 if self.gated else 8
        self.NE = self.NR + self.shared
        self.stream = k.dram["experts_" + kind]
        sb = s.sb
        self.xT = sb("xT", [D, NB * T])
        self.W = sb("W", [T, NB, self.NE])
        self.sc = sb("sc", [T, NB, 8])
        self.mx = sb("mx", [T, NB, 8])
        self.ix = sb("ix", [T, NB, 8], U32)
        self.idf = sb("idf", [T, NB, 2])
        self.den = sb("den", [T, NB])
        self.inv = sb("inv", [T, NB])
        self.w2top = sb("w2top", [T, NB, 2])
        self.oh = sb("oh", [T, NB * 2, 8])
        self.ohw = sb("ohw", [T, NB * 2, 8])
        self.wT = sb("wT", [self.NE, NB * T])
        self.buf = [sb(f"expert{i}", [P, EXPERT_COLS[kind]]) for i in range(2)]
        self.a = sb("a", [P, 2, FC, GT])
        self.sg = sb("sg", [P, 2, GT]) if self.gated else None
        self.banks = s.banks(8)
        names = ("logits_made lg_ready sc_ready best indexed idf_ready den_ready den2_ready inv_ready w_ready oh_ready "
                 "ohw_ready W_ready W_turned wT_ready bias_made xT_ready diff_ready e_ready X_set "
                 "streamed0 streamed1 expert_done up gated silud downed added moved")
        self.q = {x: s.sem(x) for x in names.split()}
        self.norm = Norm(k, sb, s.sem, "ln2")


    def setup_pool(self, pool):
        for g in range(NG):
            self.norm.on_pool(pool, g)

    def setup_tensor(self, pe):
        q, b = self.q, self.banks
        for g in range(NG + 1):
            if g < NG:
                self.norm.on_tensor(pe, g, b[4 + g])
            if g >= 1:
                pe.wait_ge(q["xT_ready"], g)
                for u in range((g - 1) * GI, g * GI):
                    ins = pe.matmul(b[0][:, u * 8:u * 8 + self.NR], self.xT[:, u * T:(u + 1) * T], self.w["router"],
                                    start=True, stop=True)
        ins.then_inc(q["logits_made"], 1)
        if self.gated:
            pe.wait_ge(q["lg_ready"], 1)
            return
        pe.wait_ge(q["W_ready"], 1)
        for u in range(NB):
            ins = pe.transpose(b[4 + u // GI][0:self.NE, (u % GI) * T:(u % GI + 1) * T], self.W[:, u, :], self.k.ident[:, :])
            if u % GI == GI - 1:
                ins.then_inc(q["W_turned"], 1)
        for u in range(NB):
            pe.wait_ge(q["wT_ready"], u // GI + 1)
            ins = pe.matmul(b[u // GI][:, (u % GI) * D:(u % GI + 1) * D], self.wT[:, u * T:(u + 1) * T], self.w["b2"],
                            start=True, stop=True)
            if u % GI == GI - 1:
                ins.then_inc(q["bias_made"], 1)
        pe.wait_ge(q["X_set"], NG)

    def setup_scalar(self, act):
        q, b = self.q, self.banks
        for g in range(NG):
            act.wait_ge(self.norm.turned, g + 1)
            xT = self.xT[:, g * GT:(g + 1) * GT]
            if self.gated:
                ins = act.activation(xT, b[4 + g][:, :], ACT.Identity, scale=self.w["ln2_w"], bias=self.w["ln2_b"])
            else:
                ins = act.copy(xT, b[4 + g][:, :])
            ins.then_inc(q["xT_ready"], 1)
        if self.gated:
            return
        if self.shared:
            act.wait_ge(q["lg_ready"], 1)
            act.activation(self.sc[:, :, :], self.oh[:, 0:NB, :], ACT.Sigmoid).then_inc(q["sc_ready"], 1)
        else:
            act.wait_ge(q["diff_ready"], 1)
            act.activation(self.inv[:, :], self.den[:, :], ACT.Exp).then_inc(q["e_ready"], 1)
        for g in range(NG):
            act.wait_ge(q["W_turned"], g + 1)
            act.copy(self.wT[:, g * GT:(g + 1) * GT], b[4 + g][0:self.NE, :]).then_inc(q["wT_ready"], 1)

    def norm_vector(self, dve):
        for g in range(NG):
            src = lambda i: (self.k.Z if self.gated else self.k.X)[:, g * GI + i, :]
            self.norm.on_vector_stats(dve, g, src)
            if g:
                dve.wait_ge(self.norm.turned, g)
            self.norm.on_vector_apply(dve, g, src)

    def route_vector(self, dve):
        q, k, b = self.q, self.k, self.banks
        lg = b[0][:, 0:NB * 8].rearrange("p (i e) -> p i e", i=NB)
        NR = self.NR
        dve.wait_ge(q["logits_made"], 1)
        if self.shared:
            dve.tensor_tensor(self.oh[:, 0:NB, :], lg, self.w["gate_bias"].unsqueeze(1).to_broadcast([P, NB, 8]), ALU.add)\
               .then_inc(q["lg_ready"], 1)
            k.wait_alone(dve, q["sc_ready"], 1)
        else:
            dve.tensor_copy(self.sc[:, :, 0:NR], lg[:, :, 0:NR]).then_inc(q["lg_ready"], 1)
            k.wait_alone(dve, q["lg_ready"], 1)
        for i in range(NB):
            ins = dve.max(self.mx[:, i, :], self.sc[:, i, :])
        ins.then_inc(q["best"], 1)
        k.wait_alone(dve, q["best"], 1)
        for i in range(NB):
            ins = dve.max_index(self.ix[:, i, :], self.mx[:, i, :], self.sc[:, i, :])
        ins.then_inc(q["indexed"], 1)
        k.wait_alone(dve, q["indexed"], 1)
        dve.tensor_copy(self.idf[:, :, :], self.ix[:, :, 0:2]).then_inc(q["idf_ready"], 1)
        iota8 = self.k.iota[:, 0:8]
        if self.gated:
            dve.wait_ge(q["idf_ready"], 1)
            dve.tensor_tensor(self.W[:, :, :], iota8[:, 0:NR].unsqueeze(1).to_broadcast([P, NB, NR]),
                              self.idf[:, :, 0:1].to_broadcast([P, NB, NR]), ALU.is_equal).then_inc(q["moved"], 1)
            X, Z = self.k.X[:, :, :], self.k.Z[:, :, :]
            dve.tensor_tensor(X, X, Z, ALU.add)\
               .then_inc(q["X_set"], 1)
            return
        best, second = self.mx[:, :, 0], self.mx[:, :, 1]
        if self.shared:
            dve.tensor_tensor(self.den[:, :], best, second, ALU.add).then_inc(q["den_ready"], 1)
            k.wait_alone(dve, q["den_ready"], 1)
            dve.tensor_scalar(self.den[:, :], self.den[:, :], 1e-6, None, ALU.add).then_inc(q["den2_ready"], 1)
            k.wait_alone(dve, q["den2_ready"], 1)
            dve.reciprocal(self.inv[:, :], self.den[:, :]).then_inc(q["inv_ready"], 1)
            dve.wait_ge(q["inv_ready"], 1)
            dve.tensor_tensor(self.w2top[:, :, :], self.mx[:, :, 0:2], self.inv[:, :].unsqueeze(2).to_broadcast([P, NB, 2]),
                              ALU.mult).then_inc(q["w_ready"], 1)
        else:
            dve.tensor_tensor(self.den[:, :], second, best, ALU.subtract).then_inc(q["diff_ready"], 1)
            k.wait_alone(dve, q["e_ready"], 1)
            dve.tensor_scalar(self.den[:, :], self.inv[:, :], 1.0, None, ALU.add).then_inc(q["den2_ready"], 1)
            k.wait_alone(dve, q["den2_ready"], 1)
            dve.reciprocal(self.w2top[:, :, 0], self.den[:, :]).then_inc(q["inv_ready"], 1)
            dve.wait_ge(q["inv_ready"], 1)
            dve.tensor_tensor(self.w2top[:, :, 1], self.w2top[:, :, 0], self.inv[:, :], ALU.mult).then_inc(q["w_ready"], 1)
        top = self.w2top[:, :, :].rearrange("p i r -> p (i r)").unsqueeze(2).to_broadcast([P, NB * 2, 8])
        idx = self.idf[:, :, :].rearrange("p i r -> p (i r)").unsqueeze(2).to_broadcast([P, NB * 2, 8])
        dve.wait_ge(q["idf_ready"], 1)
        if self.shared:
            dve.wait_ge(q["sc_ready"], 1)
        dve.tensor_tensor(self.oh[:, :, :], iota8.unsqueeze(1).to_broadcast([P, NB * 2, 8]), idx, ALU.is_equal)\
           .then_inc(q["oh_ready"], 1)
        dve.wait_ge(q["oh_ready"], 1)
        dve.wait_ge(q["w_ready"], 1)
        dve.tensor_tensor(self.ohw[:, :, :], self.oh[:, :, :], top, ALU.mult).then_inc(q["ohw_ready"], 1)
        dve.wait_ge(q["ohw_ready"], 1)
        pair = self.ohw[:, :, :].rearrange("p (i r) e -> p i r e", r=2)
        dve.tensor_tensor(self.W[:, :, 0:NR], pair[:, :, 0, :], pair[:, :, 1, :], ALU.add).then_inc(q["W_ready"], 1)
        for g in range(NG):
            x = self.k.X[:, g * GI:(g + 1) * GI, :]
            dve.wait_ge(q["bias_made"], g + 1)
            dve.tensor_tensor(x, b[g][:, :].rearrange("p (i d) -> p i d", i=GI), x, ALU.add).then_inc(q["X_set"], 1)

    def prime_vector(self, dve):
        q = self.q
        if self.gated:
            dve.memset(self.sc[:, :, :], -3e38).then_inc(q["moved"], 1)
        if self.shared:
            dve.memset(self.W[:, :, 8:9], 0.1).then_inc(q["moved"], 1)
        if self.gated or self.shared:
            dve.wait_ge(q["moved"], 1)


    def expert_sync(self, sp, e, b, pair):
        q = self.q
        sp.wait_ge(q["expert_done"], e + 1)
        sp.dma_start(self.buf[b][:, :], self.stream[bass.ds(e, 1), :, :].rearrange("o p c -> (o p) c"))\
          .then_inc(q[f"streamed{b}"], 16)

    def up_tensor(self, pe, u, g, b):
        q = self.q
        for c in range(FC):
            x = self.xT[:, g * GT:(g + 1) * GT]
            if self.gated:
                pe.wait_ge(q["gated"], u * FC + c + 1)
                j = 2 * (c % 2)
                pe.matmul(self.banks[j][:, :], self.buf[b][:, c * P:(c + 1) * P], x, start=True, stop=True)
                pe.matmul(self.banks[j + 1][:, :], self.buf[b][:, FF + c * P:FF + (c + 1) * P], x, start=True, stop=True)\
                  .then_inc(q["up"], 1)
            else:
                pe.wait_ge(q["gated"], u * FC + c + 1)
                pe.matmul(self.banks[c][:, :], self.buf[b][:, c * P:(c + 1) * P], x, start=True, stop=True)\
                  .then_inc(q["up"], 1)

    def down_tensor(self, pe, u, g, b, last):
        q, par = self.q, g % 2
        w2 = self.buf[b][:, (2 * FF if self.gated else FF):(3 * FF if self.gated else 2 * FF)].rearrange("p (c d) -> p c d", c=FC)
        out = self.banks[4 + par]
        pe.wait_ge(q["gated"], u * FC + FC + (2 if self.gated else 4))
        pe.wait_ge(q["added"], u + 3)
        for i in range(GI):
            for c in range(FC):
                ins = pe.matmul(out[:, i * D:(i + 1) * D], self.a[:, par, c, i * T:(i + 1) * T], w2[:, c, :],
                                start=(c == 0), stop=(c == FC - 1))
        ins.then_inc(q["downed"], 1)
        if last:
            pe.wait_ge(q["downed"], u + 3)
            pe.sem_inc(q["expert_done"], 1)

    def expert_tensor(self, pe, e, b, pair):
        pe.wait_ge(self.q[f"streamed{b}"], pair * 16 + 16)
        self.up_tensor(pe, e * NG, 0, b)
        for g in range(1, NG):
            self.up_tensor(pe, e * NG + g, g, b)
            self.down_tensor(pe, e * NG + g - 1, g - 1, b, False)
        self.down_tensor(pe, e * NG + NG - 1, NG - 1, b, True)

    def expert_scalar(self, act, e, b, pair):
        q = self.q
        for g in range(NG):
            u, par = e * NG + g, g % 2
            act.wait_ge(q["downed"], u + 1)
            for c in range(FC):
                act.wait_ge(q["up"], u * FC + c + 1)
                if self.gated:
                    act.wait_ge(q["gated"], u * FC + c + 1)
                    act.activation(self.sg[:, c % 2, :], self.banks[2 * (c % 2)][:, :], ACT.Silu).then_inc(q["silud"], 1)
                else:
                    act.activation(self.a[:, par, c, :], self.banks[c][:, :], ACT.Gelu,
                                   bias=self.buf[b][:, 2 * FF + c:2 * FF + c + 1]).then_inc(q["gated"], 1)

    def expert_vector(self, dve, e, b, pair):
        q, X = self.q, self.k.X
        for g in range(NG + 1):
            u = e * NG + g
            if g < NG and self.gated:
                dve.wait_ge(q["downed"], u + 1)
                for c in range(FC):
                    dve.wait_ge(q["silud"], u * FC + c + 1)
                    dve.tensor_tensor(self.a[:, g % 2, c, :], self.sg[:, c % 2, :], self.banks[2 * (c % 2) + 1][:, :],
                                      ALU.mult).then_inc(q["gated"], 1)
            if g >= 1:
                u, h = u - 1, g - 1
                dve.wait_ge(q["added"], u + 1)
                dve.wait_ge(q["downed"], u + 3)
                for i in range(GI):
                    x = X[:, h * GI + i, :]
                    ins = dve.scalar_tensor_tensor(out=x, in0=self.banks[4 + h % 2][:, i * D:(i + 1) * D],
                                                   scalar=self.W[:, h * GI + i, bass.ds(e, 1)], in1=x,
                                                   op0=ALU.mult, op1=ALU.add)
                ins.then_inc(q["added"], 1)


    def experts(self, eng, one):
        with eng.Fori(0, self.NR // 2) as pair:
            for b in range(2):
                one(eng, pair * 2 + b, b, pair)
        if self.shared:
            one(eng, self.NR, 0, self.NR // 2)


def sublayer_moe(k, s, n):
    m = Moe(k, s, n, UNITS[n])
    q, X = m.q, k.X
    with k.nc.Block() as block:
        @block.sync
        def _(sp):
            k.load(sp, n + 1)
            sp.sem_inc(q["expert_done"], 2)
            m.experts(sp, m.expert_sync)

        @block.gpsimd
        def _(pool):
            m.setup_pool(pool)

        @block.tensor
        def _(pe):
            pe.wait_ge(m.loaded, m.count)
            pe.sem_inc(q["downed"], 2)
            m.setup_tensor(pe)
            m.experts(pe, m.expert_tensor)

        @block.scalar
        def _(act):
            act.wait_ge(m.loaded, m.count)
            if not m.gated:
                act.sem_inc(q["gated"], 4)
            m.setup_scalar(act)
            m.experts(act, m.expert_scalar)

        @block.vector
        def _(dve):
            dve.wait_ge(m.loaded, m.count)
            m.prime_vector(dve)
            dve.sem_inc(q["added"], 4)
            if m.gated:
                dve.sem_inc(q["gated"], 2)
            m.norm_vector(dve)
            m.route_vector(dve)
            dve.wait_ge(q["X_set"], 1 if m.gated else NG)
            dve.wait_ge(q["moved"] if m.gated else q["W_ready"], 2 if m.gated else 1)
            m.experts(dve, m.expert_vector)


def expert_arrays(w1, b1, w2):
    e = w1.shape[0]
    return np.concatenate([w1.transpose(0, 2, 1), w2.transpose(0, 2, 1).reshape(e, FC, P, D).transpose(0, 2, 1, 3).reshape(e, P, FF),
                           b1.reshape(e, FC, P).transpose(0, 2, 1)], 2)


def pack_l1f(a):
    return {"router": a["L1_ffn_router_w"].T, "b2": a["L1_ffn_b2"]}


def stream_l1f(a):
    return {"experts_l1f": expert_arrays(a["L1_ffn_w1"], a["L1_ffn_b1"], a["L1_ffn_w2"])}


def pack_l2f(a):
    return {"router": a["L2_ffn_gate_w"].T, "b2": np.concatenate([a["L2_ffn_bd"], a["L2_ffn_sbd"][None]], 0),
            "gate_bias": np.broadcast_to(a["L2_ffn_gate_bias"][None], (P, 8))}


def stream_l2f(a):
    return {"experts_l2f": expert_arrays(np.concatenate([a["L2_ffn_Wu"], a["L2_ffn_sWu"][None]], 0),
                                         np.concatenate([a["L2_ffn_bu"], a["L2_ffn_sbu"][None]], 0),
                                         np.concatenate([a["L2_ffn_Wd"], a["L2_ffn_sWd"][None]], 0))}
def pack_l0f(a):
    return {"router": a["L0_ffn_router_w"], "ln2_w": a["L0_ffn_ln2_w"], "ln2_b": a["L0_ffn_ln2_b"]}


def stream_l0f(a):
    proj = a["L0_ffn_expert_proj"].reshape(4, FC, P, D).transpose(0, 2, 1, 3).reshape(4, P, FF)
    return {"experts_l0f": np.concatenate([a["L0_ffn_expert_wv"], proj], 2)}



L3 = 2
EH, ED = 8, 16
INTER = 352
IC = -(-INTER // P)
RMS_EPS = 1e-6
SPLIT = 8
QKVB = 3 * D + EH
MIX_COLS = QKVB + D + 2
FFN_COLS = 2 * INTER + IC * D + 1
PACKS["l3a"] = Pack(("final", P, D))


class RmsNorm:

    def __init__(self, k, sb, sem, tag):
        self.k = k
        self.ss, self.me, self.rs = (sb(f"{tag}_{x}", [P, NB]) for x in ("ss", "me", "rs"))
        self.xn = sb(f"{tag}_xn", [P, GI, D])
        self.squared, self.mean, self.root = sem(f"{tag}_squared"), sem(f"{tag}_mean"), sem(f"{tag}_root")
        self.ready, self.turned = sem(f"{tag}_ready"), sem(f"{tag}_turned")

    def on_scalar(self, act, src, squares):
        for i in range(NB):
            ins = act.activation(squares[:, i, 0:D], src[:, i, :], ACT.Square, accum_out=self.ss[:, i:i + 1])
        ins.then_inc(self.squared, 1)

    def on_pool(self, pool, n):
        self.k.wait_alone(pool, self.squared, n + 1)
        pool.tensor_scalar(self.me[:, :], self.ss[:, :], 1.0 / D, RMS_EPS, ALU.mult, ALU.add).then_inc(self.mean, 1)
        pool.wait_ge(self.mean, n + 1)
        pool.tensor_tensor(self.rs[:, :], self.me[:, :], self.k.half[:, 0:1].to_broadcast([P, NB]), ALU.pow)\
            .then_inc(self.root, 1)

    def on_vector(self, dve, n, g, src, read):
        dve.wait_ge(self.root, n + 1)
        dve.wait_ge(read, n * NG + g + 1)
        rows = src[:, bass.ds(g * GI, GI), :]
        factors = self.rs[:, bass.ds(g * GI, GI)].unsqueeze(2).to_broadcast([P, GI, D])
        dve.tensor_tensor(self.xn[:, :, :], rows, factors, ALU.mult).then_inc(self.ready, 1)

    def on_tensor(self, pe, m, bank):
        pe.wait_ge(self.ready, m + 1)
        for i in range(GI):
            ins = pe.transpose(bank[:, i * T:(i + 1) * T], self.xn[:, i, :], self.k.ident[:, :])
        ins.then_inc(self.turned, 1)


def sublayer_delta(k, s, n):
    nc, X, ident, Y = k.nc, k.X, k.ident, k.Z
    w, loaded, count = k.weights(n)
    sb = s.sb
    ln = Norm(k, sb, s.sem, "ln")
    n1, n2, nf = (RmsNorm(k, sb, s.sem, x) for x in ("n1", "n2", "nf"))
    mix, ffn = sb("mix", [P, MIX_COLS]), sb("ffn", [P, FFN_COLS])
    wqkvb, wo = mix[:, 0:QKVB], mix[:, QKVB:QKVB + D]
    gain1, gaino = mix[:, QKVB + D:QKVB + D + 1], mix[:, QKVB + D + 1:QKVB + D + 2]
    wd = ffn[:, 2 * INTER:2 * INTER + IC * D].rearrange("p (c d) -> p c d", c=IC)
    gain2 = ffn[:, FFN_COLS - 1:FFN_COLS]
    hT = sb("hT", [D, GT])
    qkv = sb("qkv", [P, NB, 3 * D])
    bl, beta = sb("bl", [P, NB, EH]), sb("beta", [P, NB, EH])
    sqk = sb("sqk", [P, NB, 2 * D])
    ss2, me2, rs2 = (sb(x, [P, NB * 2 * EH]) for x in ("ss2", "me2", "rs2"))
    kprod = [sb(f"kprod{i}", [P, NB * D]) for i in range(2)]
    qprod = [sb(f"qprod{i}", [P, NB * D]) for i in range(2)]
    GK, GQ = sb("GK", [P, NB, NB, EH]), sb("GQ", [P, NB, NB, EH])
    U, pred, o = sb("U", [P, NB, D]), sb("pred", [P, D]), sb("o", [P, NB, D])
    rt2, rto = sb("rt2", [P, NB * 2 * EH]), sb("rto", [P, NB * EH])
    sso, meo, rso = (sb(x, [P, NB * EH]) for x in ("sso", "meo", "rso"))
    on = sb("on", [P, GI, D])
    oT = sb("oT", [D, GT])
    sg = sb("sg", [P, 2, GT])
    a = sb("a", [P, IC, GT])
    b = s.banks(8)
    q = {x: s.sem(x) for x in (
        "Y_ready mix_loaded ffn_loaded mix_done ffn_done hT_ready qkv_made silud beta_half beta_ready sq_ready ss_ready me_ready "
        "length o_length qk_summed qk_copied o_summed rs_ready unit kk_mult kk_ready qk_mult qk_ready p_mult p_ready diff u_ready o_mult o_ready osq oss ome ors onormed "
        "o_turned oT_ready out_made hT2_ready up gsilu gated down final_w added").split()}

    def heads(x):
        return x.rearrange("p n (h d) -> p n h d", h=EH)

    with nc.Block() as block:
        @block.sync
        def _(sp):
            k.load(sp, n + 1)
            with sp.Fori(0, L3) as l:
                sp.wait_ge(q["mix_done"], l + 1)
                sp.dma_start(mix[:, :], k.dram["mix_l3a"][bass.ds(l, 1), :, :].rearrange("o p c -> (o p) c"))\
                  .then_inc(q["mix_loaded"], 16)
                sp.wait_ge(q["ffn_done"], l + 1)
                sp.dma_start(ffn[:, :], k.dram["ffn_l3a"][bass.ds(l, 1), :, :].rearrange("o p c -> (o p) c"))\
                  .then_inc(q["ffn_loaded"], 16)

        @block.gpsimd
        def _(pool):
            pool.sem_inc(q["qk_mult"], 1)
            pool.sem_inc(q["o_mult"], 1)
            with pool.Fori(0, NG) as g:
                ln.on_pool(pool, g)
            with pool.Fori(0, L3) as l:
                n1.on_pool(pool, l)
                k.wait_alone(pool, q["ss_ready"], l + 1)
                pool.tensor_scalar(me2[:, :], ss2[:, :], RMS_EPS, None, ALU.add).then_inc(q["me_ready"], 1)
                pool.wait_ge(q["unit"], l + 1)
                for i in range(NB):
                    if i < 2:
                        pool.wait_ge(q["o_summed"], l * NB + 2)
                    elif i - 2 < SPLIT:
                        pool.wait_ge(q["qk_ready"], l * SPLIT + i - 1)
                    else:
                        pool.wait_ge(q["qk_summed"], l * (NB - SPLIT) + i - 1 - SPLIT)
                    pool.tensor_tensor(qprod[i % 2][:, 0:(i + 1) * D].rearrange("p (j c) -> p j c", c=D),
                                       qkv[:, 0:i + 1, D:2 * D], qkv[:, i:i + 1, 0:D].to_broadcast([P, i + 1, D]), ALU.mult)\
                        .then_inc(q["qk_mult"], 1)
                for i in range(NB):
                    pool.wait_ge(q["o_summed"], l * NB + i + 1)
                    if i < 2:
                        pool.wait_ge(q["qk_copied"], l * (NB - SPLIT) + NB - SPLIT)
                    pool.wait_ge(q["u_ready"], l * NB + i + 1)
                    pool.tensor_tensor(heads(qprod[i % 2][:, 0:(i + 1) * D].rearrange("p (j c) -> p j c", c=D)),
                                       heads(U[:, 0:i + 1, :]),
                                       GQ[:, i, 0:i + 1, :].unsqueeze(3).to_broadcast([P, i + 1, EH, ED]), ALU.mult)\
                        .then_inc(q["o_mult"], 1)
                k.wait_alone(pool, q["oss"], l + 1)
                pool.tensor_scalar(meo[:, :], sso[:, :], 1.0 / ED, RMS_EPS, ALU.mult, ALU.add).then_inc(q["ome"], 1)
                n2.on_pool(pool, l)
            nf.on_pool(pool, 0)

        @block.tensor
        def _(pe):
            pe.sem_inc(q["mix_done"], 1)
            pe.sem_inc(q["ffn_done"], 1)
            pe.sem_inc(q["down"], 1)
            pe.sem_inc(q["o_turned"], 1)
            pe.sem_inc(q["o_summed"], 2)
            for norm in (n1, n2):
                pe.sem_inc(norm.turned, 1)
            with pe.Fori(0, L3) as l:
                k.wait_alone(pe, q["mix_loaded"], l * 16 + 16)
                with pe.Fori(0, NG) as g:
                    m = l * NG + g
                    n1.on_tensor(pe, m, b[4])
                    pe.wait_ge(q["hT_ready"], m + 1)
                    for i in range(GI):
                        pe.wait_ge(q["silud"], m * GI + i + 1)
                        pe.matmul(b[i][:, 0:QKVB], hT[:, i * T:(i + 1) * T], wqkvb, start=True, stop=True)\
                          .then_inc(q["qkv_made"], 1)
                for i in range(SPLIT, NB):
                    bank = b[6 + i % 2]
                    pe.wait_ge(q["qk_mult"], l * NB + i + 2)
                    if i < SPLIT + 2:
                        pe.wait_ge(q["o_ready"], l * NB + 2)
                    else:
                        pe.wait_ge(q["qk_copied"], l * (NB - SPLIT) + i - 1 - SPLIT)
                    products = qprod[i % 2][:, 0:(i + 1) * D].rearrange("p (m d) -> p m d", d=ED)
                    for d in range(ED):
                        ins = pe.matmul(bank[:, 0:(i + 1) * EH], ident[:, :], products[:, :, d], start=d == 0, stop=d == ED - 1)
                    ins.then_inc(q["qk_summed"], 1)
                for i in range(NB):
                    if i < 2:
                        pe.wait_ge(q["qk_copied"], l * (NB - SPLIT) + NB - SPLIT)
                    pe.wait_ge(q["o_ready"], l * NB + i + 1)
                    pe.wait_ge(q["o_mult"], l * NB + i + 2)
                    for j in range(i + 1):
                        ins = pe.matmul(b[6 + i % 2][:, 0:D], ident[:, :], qprod[i % 2][:, j * D:(j + 1) * D],
                                        start=j == 0, stop=j == i)
                    ins.then_inc(q["o_summed"], 1)
                with pe.Fori(0, NG) as g:
                    m = l * NG + g
                    pe.wait_ge(q["onormed"], m + 1)
                    pe.wait_ge(q["oT_ready"], m + 1)
                    for i in range(GI):
                        ins = pe.transpose(b[4][:, i * T:(i + 1) * T], on[:, i, :], ident[:, :])
                    ins.then_inc(q["o_turned"], 1)
                    pe.wait_ge(q["oT_ready"], m + 2)
                    pe.wait_ge(q["Y_ready"], NG + l * 2 * NG + g)
                    for i in range(GI):
                        ins = pe.matmul(b[5][:, i * D:(i + 1) * D], oT[:, i * T:(i + 1) * T], wo, start=True, stop=True)
                    ins.then_inc(q["out_made"], 1)
                pe.wait_ge(q["Y_ready"], NG + l * 2 * NG + NG)
                pe.sem_inc(q["mix_done"], 1)
                k.wait_alone(pe, q["ffn_loaded"], l * 16 + 16)
                with pe.Fori(0, NG) as g:
                    m = l * NG + g
                    n2.on_tensor(pe, m, b[4])
                    pe.wait_ge(q["hT2_ready"], m + 1)
                    for c in range(IC):
                        f = min(P, INTER - c * P)
                        pe.wait_ge(q["gated"], m * IC + c + 1)
                        pe.matmul(b[2 * (c % 2)][0:f, :], ffn[:, c * P:c * P + f], hT[:, :], start=True, stop=True)
                        pe.matmul(b[2 * (c % 2) + 1][0:f, :], ffn[:, INTER + c * P:INTER + c * P + f], hT[:, :],
                                  start=True, stop=True).then_inc(q["up"], 1)
                    pe.wait_ge(q["gated"], m * IC + IC + 2)
                    pe.wait_ge(q["Y_ready"], 2 * NG + l * 2 * NG + g)
                    for i in range(GI):
                        for c in range(IC):
                            f = min(P, INTER - c * P)
                            ins = pe.matmul(b[5][:, i * D:(i + 1) * D], a[0:f, c, i * T:(i + 1) * T], wd[0:f, c, :],
                                            start=(c == 0), stop=(c == IC - 1))
                    ins.then_inc(q["down"], 1)
                pe.wait_ge(q["Y_ready"], 3 * NG + l * 2 * NG)
                pe.sem_inc(q["ffn_done"], 1)

        @block.scalar
        def _(act):
            act.sem_inc(q["silud"], 4)
            act.sem_inc(q["oT_ready"], 1)
            act.sem_inc(q["o_ready"], 2)
            with act.Fori(0, L3) as l:
                act.wait_ge(q["Y_ready"], l * 2 * NG + NG)
                n1.on_scalar(act, Y, sqk)
                act.wait_ge(q["mix_loaded"], l * 16 + 16)
                with act.Fori(0, NG) as g:
                    m = l * NG + g
                    act.wait_ge(n1.turned, m + 2)
                    act.activation(hT[:, :], b[4][:, :], ACT.Copy, scale=gain1).then_inc(q["hT_ready"], 1)
                    for i in range(GI):
                        act.wait_ge(q["qkv_made"], m * GI + i + 1)
                        act.activation(qkv[:, bass.ds(g * GI + i, 1), :].rearrange("p o c -> p (o c)"), b[i][:, 0:3 * D], ACT.Silu)
                        act.copy(bl[:, bass.ds(g * GI + i, 1), :].rearrange("p o c -> p (o c)"), b[i][:, 3 * D:QKVB])\
                           .then_inc(q["silud"], 1)
                act.wait_ge(q["silud"], l * NB + NB + 4)
                act.activation(sqk[:, :, :], qkv[:, :, 0:2 * D], ACT.Square).then_inc(q["sq_ready"], 1)
                act.activation(beta[:, :, :], bl[:, :, :], ACT.Sigmoid).then_inc(q["beta_half"], 1)
                act.wait_ge(q["me_ready"], l + 1)
                act.activation(rt2[:, :], me2[:, :], ACT.Sqrt).then_inc(q["length"], 1)
                for i in range(SPLIT, NB):
                    act.wait_ge(q["qk_summed"], l * (NB - SPLIT) + i + 1 - SPLIT)
                    act.copy(GQ[:, i, 0:i + 1, :], b[6 + i % 2][:, 0:(i + 1) * EH].rearrange("p (j h) -> p j h", h=EH))\
                       .then_inc(q["qk_copied"], 1)
                for i in range(NB):
                    act.wait_ge(q["o_summed"], l * NB + i + 3)
                    act.copy(o[:, i, :], b[6 + i % 2][:, 0:D]).then_inc(q["o_ready"], 1)
                act.wait_ge(q["o_ready"], l * NB + NB + 2)
                act.activation(sqk[:, :, 0:D], o[:, :, :], ACT.Square).then_inc(q["osq"], 1)
                act.wait_ge(q["ome"], l + 1)
                act.activation(rto[:, :], meo[:, :], ACT.Sqrt).then_inc(q["o_length"], 1)
                with act.Fori(0, NG) as g:
                    m = l * NG + g
                    act.wait_ge(q["o_turned"], m + 2)
                    act.activation(oT[:, :], b[4][:, :], ACT.Copy, scale=gaino).then_inc(q["oT_ready"], 1)
                act.wait_ge(q["Y_ready"], NG + l * 2 * NG + NG)
                n2.on_scalar(act, Y, sqk)
                act.wait_ge(q["ffn_loaded"], l * 16 + 16)
                with act.Fori(0, NG) as g:
                    m = l * NG + g
                    act.wait_ge(n2.turned, m + 2)
                    act.activation(hT[:, :], b[4][:, :], ACT.Copy, scale=gain2).then_inc(q["hT2_ready"], 1)
                    for c in range(IC):
                        f = min(P, INTER - c * P)
                        act.wait_ge(q["up"], m * IC + c + 1)
                        act.wait_ge(q["gated"], m * IC + c + 1)
                        act.activation(sg[0:f, c % 2, :], b[2 * (c % 2)][0:f, :], ACT.Silu).then_inc(q["gsilu"], 1)
            act.wait_ge(q["Y_ready"], NG + L3 * 2 * NG)
            nf.on_scalar(act, Y, sqk)

        @block.vector
        def _(dve):
            dve.wait_ge(loaded, count)
            dve.sem_inc(q["gated"], 2)
            with dve.Fori(0, NG) as g:
                def src(i):
                    return X[:, g * GI + i, :]
                ln.on_vector_stats(dve, g, src)
                ln.on_vector_apply(dve, g, src)
                dve.wait_ge(ln.ready, g + 1)
                dve.tensor_copy(Y[:, bass.ds(g * GI, GI), :], ln.xn[:, :, :]).then_inc(q["Y_ready"], 1)
            with dve.Fori(0, L3) as l:
                with dve.Fori(0, NG) as g:
                    n1.on_vector(dve, l, g, Y, n1.turned)
                dve.wait_ge(q["sq_ready"], l + 1)
                dve.tensor_reduce(ss2[:, :], sqk[:, :, :].rearrange("p n (h d) -> p (n h) d", d=ED), AX.X, ALU.add)\
                   .then_inc(q["ss_ready"], 1)
                k.wait_alone(dve, q["beta_half"], l + 1)
                dve.tensor_scalar(beta[:, :, :], beta[:, :, :], 2.0, None, ALU.mult).then_inc(q["beta_ready"], 1)
                k.wait_alone(dve, q["length"], l + 1)
                dve.reciprocal(rs2[:, :], rt2[:, :]).then_inc(q["rs_ready"], 1)
                dve.wait_ge(q["rs_ready"], l + 1)
                qk = qkv[:, :, 0:2 * D].rearrange("p n (h d) -> p n h d", d=ED)
                dve.tensor_tensor(qk, qk, rs2[:, :].rearrange("p (n h) -> p n h", n=NB).unsqueeze(3)
                                  .to_broadcast([P, NB, 2 * EH, ED]), ALU.mult).then_inc(q["unit"], 1)
                dve.wait_ge(q["unit"], l + 1)
                for i in range(NB + 1):
                    if 1 <= i < NB:
                        if i >= 3:
                            dve.wait_ge(q["kk_ready"], l * (NB - 1) + i - 2)
                        dve.tensor_tensor(kprod[i % 2][:, 0:i * D].rearrange("p (j c) -> p j c", c=D),
                                          qkv[:, 0:i, D:2 * D], qkv[:, i:i + 1, D:2 * D].to_broadcast([P, i, D]), ALU.mult)\
                           .then_inc(q["kk_mult"], 1)
                    if i >= 2:
                        j = i - 1
                        dve.wait_ge(q["kk_mult"], l * (NB - 1) + j)
                        dve.tensor_reduce(GK[:, j, 0:j, :], kprod[j % 2][:, 0:j * D].rearrange("p (j h d) -> p j h d", h=EH, d=ED),
                                          AX.X, ALU.add).then_inc(q["kk_ready"], 1)
                    if 1 <= i <= SPLIT:
                        j = i - 1
                        dve.wait_ge(q["qk_mult"], l * NB + j + 2)
                        dve.tensor_reduce(GQ[:, j, 0:j + 1, :],
                                          qprod[j % 2][:, 0:(j + 1) * D].rearrange("p (j h d) -> p j h d", h=EH, d=ED),
                                          AX.X, ALU.add).then_inc(q["qk_ready"], 1)

                dve.wait_ge(q["kk_ready"], l * (NB - 1) + NB - 1)
                dve.wait_ge(q["beta_ready"], l + 1)
                for i in range(NB):
                    v, bi = qkv[:, i, 2 * D:3 * D], beta[:, i, :].unsqueeze(2).to_broadcast([P, EH, ED])
                    u = U[:, i, :].rearrange("p (h d) -> p h d", h=EH)
                    if i == 0:
                        dve.tensor_tensor(u, v.rearrange("p (h d) -> p h d", h=EH), bi, ALU.mult).then_inc(q["u_ready"], 1)
                        continue
                    dve.wait_ge(q["u_ready"], l * NB + i)
                    dve.tensor_tensor(heads(kprod[0][:, 0:i * D].rearrange("p (j c) -> p j c", c=D)), heads(U[:, 0:i, :]),
                                      GK[:, i, 0:i, :].unsqueeze(3).to_broadcast([P, i, EH, ED]), ALU.mult).then_inc(q["p_mult"], 1)
                    dve.wait_ge(q["p_mult"], l * (NB - 1) + i)
                    dve.tensor_reduce(pred[:, :], kprod[0][:, 0:i * D].rearrange("p (j c) -> p c j", c=D), AX.X, ALU.add)\
                       .then_inc(q["p_ready"], 1)
                    dve.wait_ge(q["p_ready"], l * (NB - 1) + i)
                    dve.tensor_tensor(pred[:, :], v, pred[:, :], ALU.subtract).then_inc(q["diff"], 1)
                    dve.wait_ge(q["diff"], l * (NB - 1) + i)
                    dve.tensor_tensor(u, pred[:, :].rearrange("p (h d) -> p h d", h=EH), bi, ALU.mult).then_inc(q["u_ready"], 1)
                dve.wait_ge(q["osq"], l + 1)
                dve.tensor_reduce(sso[:, :], sqk[:, :, 0:D].rearrange("p n (h d) -> p n h d", h=EH), AX.X, ALU.add)\
                   .then_inc(q["oss"], 1)
                k.wait_alone(dve, q["o_length"], l + 1)
                dve.reciprocal(rso[:, :], rto[:, :]).then_inc(q["ors"], 1)
                k.wait_alone(dve, q["ors"], l + 1)
                with dve.Fori(0, NG) as g:
                    m = l * NG + g
                    dve.wait_ge(q["o_turned"], m + 1)
                    dve.tensor_tensor(on[:, :, :].rearrange("p i (h d) -> p (i h) d", h=EH),
                                      o[:, bass.ds(g * GI, GI), :].rearrange("p i (h d) -> p (i h) d", h=EH),
                                      rso[:, bass.ds(g * GI * EH, GI * EH)].unsqueeze(2).to_broadcast([P, GI * EH, ED]),
                                      ALU.mult).then_inc(q["onormed"], 1)
                    y = Y[:, bass.ds(g * GI, GI), :]
                    dve.wait_ge(q["Y_ready"], l * 2 * NG + g + 1)
                    dve.wait_ge(q["out_made"], m + 1)
                    dve.tensor_tensor(y, b[5][:, :].rearrange("p (i d) -> p i d", i=GI), y, ALU.add).then_inc(q["Y_ready"], 1)

                def feed_forward(g, more):
                    m = l * NG + g
                    for c in range(IC):
                        f = min(P, INTER - c * P)
                        dve.wait_ge(q["gsilu"], m * IC + c + 1)
                        dve.tensor_tensor(a[0:f, c, :], sg[0:f, c % 2, :], b[2 * (c % 2) + 1][0:f, :], ALU.mult)\
                           .then_inc(q["gated"], 1)
                    if more:
                        n2.on_vector(dve, l, g + 1, Y, n2.turned)
                    y = Y[:, bass.ds(g * GI, GI), :]
                    dve.wait_ge(q["down"], m + 2)
                    dve.tensor_tensor(y, b[5][:, :].rearrange("p (i d) -> p i d", i=GI), y, ALU.add).then_inc(q["Y_ready"], 1)

                dve.wait_ge(q["Y_ready"], NG + l * 2 * NG + NG)
                n2.on_vector(dve, l, 0, Y, n2.turned)
                with dve.Fori(0, NG - 1) as g:
                    feed_forward(g, True)
                feed_forward(NG - 1, False)
            dve.wait_ge(q["Y_ready"], NG + L3 * 2 * NG)
            dve.sem_inc(q["added"], 1)
            with dve.Fori(0, NG) as g:
                nf.on_vector(dve, 0, g, Y, q["added"])
                x = X[:, bass.ds(g * GI, GI), :]
                dve.wait_ge(nf.ready, g + 1)
                dve.tensor_tensor(nf.xn[:, :, :], nf.xn[:, :, :], w["final"].unsqueeze(1).to_broadcast([P, GI, D]), ALU.mult)\
                   .then_inc(q["final_w"], 1)
                dve.wait_ge(q["final_w"], g + 1)
                dve.tensor_tensor(x, x, nf.xn[:, :, :], ALU.add).then_inc(q["added"], 1)


def pack_l3a(a):
    return {"final": np.broadcast_to(a["L3_attn_final_norm_w"][None], (P, D))}


def stream_l3a(a):
    wd = np.zeros((L3, IC * P, D), np.float32)
    wd[:, :INTER] = a["L3_attn_Wd"]
    onorm = np.concatenate([a["L3_attn_onorm_w"]] * EH, 1)
    return {"mix_l3a": np.concatenate([a["L3_attn_Wq"], a["L3_attn_Wk"], a["L3_attn_Wv"], a["L3_attn_Wb"], a["L3_attn_Wo"],
                                       a["L3_attn_norm1_w"][:, :, None], onorm[:, :, None]], 2),
            "ffn_l3a": np.concatenate([a["L3_attn_Wg"], wd.reshape(L3, IC, P, D).transpose(0, 2, 1, 3).reshape(L3, P, IC * D),
                                       a["L3_attn_norm2_w"][:, :, None]], 2)}



PACKS["l3x"] = Pack(("wq", D, D), ("wk", C + 1, D), ("wv", C + 1, D), ("bq", D, 1))


def sublayer_l3_xattn(k, s, n):
    nc, X, cT, ident = k.nc, k.X, k.cT, k.ident
    w, loaded, count = k.weights(n)
    SCALE = float(D) ** -0.5
    norm = Norm(k, s.sb, s.sem, "ln")
    cG = s.sb("cG", [C + 1, GI, T])
    xT = s.sb("xT", [D, GT])
    qT = s.sb("qT", [D, GT])
    kT = s.sb("kT", [D, GT])
    v = s.sb("v", [T, GI, D])
    nmax = s.sb("nmax", [T, GI])
    total = s.sb("total", [T, GI])
    inv = s.sb("inv", [T, GI])
    E = s.sb("E", [T, GI, T])
    ET = s.sb("ET", [T, GI, T])
    pX, pQ, pK, pV, pS, pT, pO = s.banks(7)
    cG_ready, xT_ready, kv_made, q_made = s.sem("cG_ready"), s.sem("xT_ready"), s.sem("kv_made"), s.sem("q_made")
    kv_ready, q_ready = s.sem("kv_ready"), s.sem("q_ready")
    scores, maxed, expd, turned, ET_ready = s.sem("scores"), s.sem("maxed"), s.sem("expd"), s.sem("turned"), s.sem("ET_ready")
    inverted, mixed, added = s.sem("inverted"), s.sem("mixed"), s.sem("added")

    with nc.Block() as block:
        @block.sync
        def _(sp):
            k.load(sp, n + 1)

        @block.gpsimd
        def _(pool):
            with pool.Fori(0, NG) as g:
                pool.wait_ge(kv_made, g + 1)
                pool.tensor_copy(cG[:, :, :], cT[:, bass.ds(g * GI, GI), :]).then_inc(cG_ready, 1)
                norm.on_pool(pool, g)

        @block.tensor
        def _(pe):
            pe.wait_ge(loaded, count)
            for free in (kv_made, mixed):
                pe.sem_inc(free, 1)
            with pe.Fori(0, NG) as g:
                pe.wait_ge(cG_ready, g + 1)
                pe.matmul(pK[:, :], w["wk"], cG[:, :, :], start=True, stop=True)
                for i in range(GI):
                    ins = pe.matmul(pV[:, i * D:(i + 1) * D], cG[:, i, :], w["wv"], start=True, stop=True)
                ins.then_inc(kv_made, 1)
                norm.on_tensor(pe, g, pX)
                pe.wait_ge(xT_ready, g + 1)
                pe.matmul(pQ[:, :], w["wq"], xT[:, :], start=True, stop=True).then_inc(q_made, 1)
                pe.wait_ge(kv_ready, g + 1)
                pe.wait_ge(q_ready, g + 1)
                for i in range(GI):
                    ins = pe.matmul(pS[:, i * T:(i + 1) * T], qT[:, i * T:(i + 1) * T], kT[:, i * T:(i + 1) * T],
                                    start=True, stop=True)
                ins.then_inc(scores, 1)
                pe.wait_ge(expd, g + 1)
                for i in range(GI):
                    ins = pe.transpose(pT[:, i * T:(i + 1) * T], E[:, i, :], ident[:, :])
                ins.then_inc(turned, 1)
                pe.wait_ge(ET_ready, g + 1)
                pe.wait_ge(added, g + 1)
                for i in range(GI):
                    ins = pe.matmul(pO[:, i * D:(i + 1) * D], ET[:, i, :], v[:, i, :], start=True, stop=True)
                ins.then_inc(mixed, 1)

        @block.scalar
        def _(act):
            with act.Fori(0, NG) as g:
                act.wait_ge(kv_made, g + 2)
                act.copy(kT[:, :], pK[:, :])
                act.wait_ge(mixed, g + 1)
                act.copy(v[:, :, :], pV[:, :]).then_inc(kv_ready, 1)
                act.wait_ge(norm.turned, g + 1)
                act.copy(xT[:, :], pX[:, :]).then_inc(xT_ready, 1)
                act.wait_ge(maxed, g + 1)
                act.wait_ge(inverted, g + 1)
                for i in range(GI):
                    ins = act.activation(E[:, i, :], pS[:, i * T:(i + 1) * T], ACT.Exp, bias=nmax[:, i:i + 1],
                                         accum_out=total[:, i:i + 1])
                ins.then_inc(expd, 1)

        @block.vector
        def _(dve):
            for free in (inverted, added):
                dve.sem_inc(free, 1)
            with dve.Fori(0, NG) as g:
                def src(i):
                    return X[:, g * GI + i, :]
                norm.on_vector_stats(dve, g, src)
                norm.on_vector_apply(dve, g, src)
                dve.wait_ge(q_made, g + 1)
                dve.tensor_scalar(qT[:, :], pQ[:, :], w["bq"], SCALE, ALU.add, ALU.mult).then_inc(q_ready, 1)
                dve.wait_ge(scores, g + 1)
                dve.tensor_reduce(nmax[:, :], pS[:, :].rearrange("p (i t) -> p i t", i=GI), AX.X, ALU.max,
                                  negate=True).then_inc(maxed, 1)
                dve.wait_ge(expd, g + 1)
                dve.reciprocal(inv[:, :], total[:, :]).then_inc(inverted, 1)
                dve.wait_ge(turned, g + 1)
                dve.tensor_copy(ET[:, :, :], pT[:, :]).then_inc(ET_ready, 1)
                dve.wait_ge(mixed, g + 2)
                dve.wait_ge(inverted, g + 2)
                for i in range(GI):
                    ins = dve.scalar_tensor_tensor(out=src(i), in0=pO[:, i * D:(i + 1) * D], scalar=inv[:, i:i + 1],
                                                   in1=src(i), op0=ALU.mult, op1=ALU.add)
                ins.then_inc(added, 1)
                dve.wait_ge(added, g + 2)


def pack_l3x(a):
    return {"wq": a["L3_xattn_Wq"], "bq": a["L3_xattn_bq"],
            "wk": np.concatenate([a["L3_xattn_Wk"], a["L3_xattn_bk"][None]], 0),
            "wv": np.concatenate([a["L3_xattn_Wv"], a["L3_xattn_bv"][None]], 0)}



SLOTS = 8 * 64
SC = SLOTS // P
HID = 4 * D
HC = HID // P
PACKS["l3f"] = Pack(("w1", D, HID), ("w2", P, HC * D), ("slots", P, SC * D), ("gx", D, 1), ("gs", D, 1))


def sublayer_l3_ffn(k, s, n):
    nc, X, ident = k.nc, k.X, k.ident
    w, loaded, count = k.weights(n)
    w1 = w["w1"]
    w2 = w["w2"].rearrange("p (c d) -> p c d", c=HC)
    slots = w["slots"].rearrange("p (c d) -> p c d", c=SC)
    ROOT = float(D) ** 0.5
    norm = Norm(k, s.sb, s.sem, "ln")
    seT = s.sb("seT", [D, SLOTS])
    se = s.sb("se", [P, SC, D])
    xa = s.sb("xa", [P, NB, D])
    sq = s.sb("sq", [P, NB, D])
    ss, root, safe, rn = (s.sb(x, [P, NB]) for x in ("ss", "root", "safe", "rn"))
    xr = s.sb("xr", [T, GI, D])
    xT = s.sb("xT", [D, GT])
    cmax, csum, cinv = s.sb("cmax", [T, GI]), s.sb("csum", [T, GI]), s.sb("cinv", [T, GI])
    dmax, dsum, dinv = s.sb("dmax", [P, GI, SC]), s.sb("dsum", [P, GI, SC]), s.sb("dinv", [P, GI, SC])
    cx = s.sb("cx", [T, 2, SLOTS])
    dx = s.sb("dx", [P, 2, SC, T])
    dn = s.sb("dn", [P, 2, SC, T])
    cT = s.sb("cT", [P, GI, SC * T])
    dm = s.sb("dm", [T, 2, SLOTS])
    slT = s.sb("slT", [D, GI, SLOTS])
    hT = s.sb("hT", [P, 2, HC, SLOTS])
    pr = s.sb("pr", [P, 2, SC * D])
    bL, bLT, bC, bD, bH0, bH1, bP, bO = s.banks(8)
    bH = (bH0, bH1)
    logit_banks = ((bL, bLT), bH)
    names = ("se_squared se_root se_safe se_inv se_scaled se_turned se_ready kept squared rooted safed normed scaled "
             "xT_ready logits maxed expd dnormed cnormed turned cT_ready dm_ready slots_made slT_ready "
             "up gelud down pr_ready mixed added").split()
    q = {name: s.sem(name) for name in names}

    with nc.Block() as block:
        @block.sync
        def _(sp):
            k.load(sp, n + 1)

        @block.gpsimd
        def _(pool):
            pool.wait_ge(q["se_squared"], 1)
            pool.tensor_tensor(root[:, 0:SC], ss[:, 0:SC], k.plus[:, 0:SC], ALU.pow).then_inc(q["se_root"], 1)
            pool.wait_ge(q["se_root"], 1)
            pool.tensor_scalar(safe[:, 0:SC], root[:, 0:SC], 1e-12, None, ALU.max).then_inc(q["se_safe"], 1)
            with pool.Fori(0, NG) as g:
                norm.on_pool(pool, g)
            pool.wait_ge(q["squared"], 1)
            pool.tensor_tensor(root[:, :], ss[:, :], k.plus[:, 0:1].to_broadcast([P, NB]), ALU.pow).then_inc(q["rooted"], 1)
            pool.wait_ge(q["rooted"], 1)
            pool.wait_ge(q["se_inv"], 1)
            pool.tensor_scalar(safe[:, :], root[:, :], 1e-12, None, ALU.max).then_inc(q["safed"], 1)

        @block.tensor
        def _(pe):
            pe.wait_ge(loaded, count)
            pe.sem_inc(q["up"], 2)
            pe.wait_ge(q["se_scaled"], 1)
            for c in range(SC):
                ins = pe.transpose(bL[:, c * P:(c + 1) * P], se[:, c, :], ident[:, :])
            ins.then_inc(q["se_turned"], 1)
            pe.wait_ge(q["se_ready"], 1)

            def rows_turned(m):
                pe.wait_ge(q["scaled"], m + 1)
                for i in range(GI):
                    ins = pe.transpose(bC[:, i * T:(i + 1) * T], xr[:, i, :], ident[:, :])
                ins.then_inc(norm.turned, 1)

            def group(g, more):
                pe.wait_ge(q["xT_ready"], g + 1)
                for t in range(GI + 3):
                    if t < GI:
                        u = g * GI + t
                        if t >= 2:
                            pe.wait_ge(q["expd"], u - 1)
                        x = xT[:, t * T:(t + 1) * T]
                        forth, back = logit_banks[t % 2]
                        pe.matmul(forth[:, :], x, seT[:, :], start=True, stop=True)
                        for c in range(SC):
                            ins = pe.matmul(back[:, c * T:(c + 1) * T], seT[:, c * P:(c + 1) * P], x, start=True, stop=True)
                        ins.then_inc(q["logits"], 1)
                    if 0 <= t - 2 < GI:
                        i, u, b = t - 2, g * GI + t - 2, t % 2
                        if i:
                            pe.wait_ge(q["cT_ready"], u)
                            pe.wait_ge(q["dm_ready"], u)
                        pe.wait_ge(q["dnormed"], u + 1)
                        for c in range(SC):
                            pe.transpose(bC[:, c * T:(c + 1) * T], cx[:, b, c * P:(c + 1) * P], ident[:, :])
                        for c in range(SC):
                            ins = pe.transpose(bD[:, c * P:(c + 1) * P], dn[:, b, c, :], ident[:, :])
                        ins.then_inc(q["turned"], 1)
                    if 0 <= t - 3 < GI:
                        i, u, b = t - 3, g * GI + t - 3, (t - 3) % 2
                        if i:
                            pe.wait_ge(q["slT_ready"], u)
                        pe.wait_ge(q["dm_ready"], u + 1)
                        pe.matmul(bO[:, :], xr[:, i, :], dm[:, b, :], start=True, stop=True).then_inc(q["slots_made"], 1)
                for i in range(GI):
                    u, b = g * GI + i, i % 2
                    pe.wait_ge(q["slT_ready"], u + 1)
                    if i == 1 and more:
                        pe.wait_ge(q["cT_ready"], g * GI + GI)
                        rows_turned(g + 1)
                    for c in range(HC):
                        pe.wait_ge(q["gelud"], u * HC + c + 1)
                        pe.matmul(bH[c % 2][:, :], w1[:, c * P:(c + 1) * P], slT[:, i, :], start=True, stop=True)\
                          .then_inc(q["up"], 1)
                    pe.wait_ge(q["gelud"], u * HC + HC + 2)
                    if i:
                        pe.wait_ge(q["pr_ready"], u)
                    for c in range(SC):
                        for f in range(HC):
                            ins = pe.matmul(bP[:, c * D:(c + 1) * D], hT[:, b, f, c * P:(c + 1) * P], w2[:, f, :],
                                            start=(f == 0), stop=(f == HC - 1))
                    ins.then_inc(q["down"], 1)
                    pe.wait_ge(q["pr_ready"], u + 1)
                    if i:
                        pe.wait_ge(q["added"], u)
                    for c in range(SC):
                        ins = pe.matmul(bO[:, 0:D], cT[:, i, c * T:(c + 1) * T], pr[:, b, c * D:(c + 1) * D],
                                        start=(c == 0), stop=(c == SC - 1))
                    ins.then_inc(q["mixed"], 1)

            rows_turned(0)
            with pe.Fori(0, NG - 1) as g:
                group(g, True)
            group(NG - 1, False)

        @block.scalar
        def _(act):
            act.wait_ge(loaded, count)
            act.sem_inc(q["gelud"], 2)
            for c in range(SC):
                ins = act.activation(sq[:, c, :], slots[:, c, :], ACT.Square, accum_out=ss[:, c:c + 1])
            ins.then_inc(q["se_squared"], 1)
            act.wait_ge(q["se_turned"], 1)
            act.activation(seT[:, :], bL[:, :], ACT.Copy, scale=w["gs"]).then_inc(q["se_ready"], 1)
            act.wait_ge(q["kept"], NG)
            act.wait_ge(q["se_safe"], 1)
            for i in range(NB):
                ins = act.activation(sq[:, i, :], xa[:, i, :], ACT.Square, accum_out=ss[:, i:i + 1])
            ins.then_inc(q["squared"], 1)

            def take_rows(m):
                act.wait_ge(norm.turned, m + 1)
                act.activation(xT[:, :], bC[:, :], ACT.Copy, scale=w["gx"]).then_inc(q["xT_ready"], 1)

            def group(g, more):
                for t in range(GI + 1):
                    if t < GI:
                        u, b = g * GI + t, t % 2
                        if t >= 2:
                            act.wait_ge(q["turned"], u - 1)
                        act.wait_ge(q["maxed"], u + 1)
                        forth, back = logit_banks[b]
                        act.activation(cx[:, b, :], forth[:, :], ACT.Exp, bias=cmax[:, t:t + 1], accum_out=csum[:, t:t + 1])
                        for c in range(SC):
                            ins = act.activation(dx[:, b, c, :], back[:, c * T:(c + 1) * T], ACT.Exp,
                                                 bias=dmax[:, t, c:c + 1], accum_out=dsum[:, t, c:c + 1])
                        ins.then_inc(q["expd"], 1)
                    if t >= 1:
                        u = g * GI + t - 1
                        act.wait_ge(q["turned"], u + 1)
                        act.copy(cT[:, t - 1, :], bC[:, :]).then_inc(q["cT_ready"], 1)
                for i in range(GI):
                    u, b = g * GI + i, i % 2
                    for c in range(HC):
                        act.wait_ge(q["up"], u * HC + c + 3)
                        act.activation(hT[:, b, c, :], bH[c % 2][:, :], ACT.Gelu).then_inc(q["gelud"], 1)
                    if i == 1 and more:
                        take_rows(g + 1)

            take_rows(0)
            with act.Fori(0, NG - 1) as g:
                group(g, True)
            group(NG - 1, False)

        @block.vector
        def _(dve):
            dve.wait_ge(loaded, count)
            dve.wait_ge(q["se_safe"], 1)
            dve.reciprocal(rn[:, 0:SC], safe[:, 0:SC]).then_inc(q["se_inv"], 1)
            dve.wait_ge(q["se_inv"], 1)
            for c in range(SC):
                ins = dve.tensor_scalar(se[:, c, :], slots[:, c, :], rn[:, c:c + 1], ROOT, ALU.mult, ALU.mult)
            ins.then_inc(q["se_scaled"], 1)
            with dve.Fori(0, NG) as g:
                def src(i):
                    return X[:, g * GI + i, :]
                norm.on_vector_stats(dve, g, src)
                norm.on_vector_apply(dve, g, src)
                dve.wait_ge(norm.ready, g + 1)
                dve.tensor_copy(xa[:, bass.ds(g * GI, GI), :], norm.xn[:, :, :]).then_inc(q["kept"], 1)
            dve.wait_ge(q["safed"], 1)
            dve.wait_ge(q["se_scaled"], 1)
            dve.reciprocal(rn[:, :], safe[:, :]).then_inc(q["normed"], 1)
            dve.wait_ge(q["normed"], 1)
            dve.tensor_scalar(root[:, :], rn[:, :], ROOT, None, ALU.mult).then_inc(q["normed"], 1)
            dve.wait_ge(q["normed"], 2)

            def scale_rows(m):
                dve.tensor_tensor(xr[:, :, :], xa[:, bass.ds(m * GI, GI), :],
                                  root[:, bass.ds(m * GI, GI)].unsqueeze(2).to_broadcast([P, GI, D]), ALU.mult)\
                   .then_inc(q["scaled"], 1)

            def group(g, more):
                def src(i):
                    return X[:, g * GI + i, :]
                for t in range(GI + 2):
                    if t < GI:
                        dve.wait_ge(q["logits"], g * GI + t + 1)
                        forth, back = logit_banks[t % 2]
                        dve.tensor_reduce(cmax[:, t:t + 1], forth[:, :], AX.X, ALU.max, negate=True)
                        dve.tensor_reduce(dmax[:, t, :], back[:, :].rearrange("p (c t) -> p c t", c=SC), AX.X, ALU.max,
                                          negate=True).then_inc(q["maxed"], 1)
                    if 0 <= t - 1 < GI:
                        i, u, b = t - 1, g * GI + t - 1, (t - 1) % 2
                        dve.wait_ge(q["expd"], u + 1)
                        dve.reciprocal(cinv[:, i:i + 1], csum[:, i:i + 1])
                        dve.reciprocal(dinv[:, i, :], dsum[:, i, :]).then_inc(q["cnormed"], 1)
                        dve.wait_ge(q["cnormed"], u + 1)
                        dve.tensor_tensor(dn[:, b, :, :], dx[:, b, :, :],
                                          dinv[:, i, :].unsqueeze(2).to_broadcast([P, SC, T]), ALU.mult)\
                           .then_inc(q["dnormed"], 1)
                        if t - 1 >= 2:
                            dve.wait_ge(q["slots_made"], u - 1)
                        dve.wait_ge(q["turned"], u + 1)
                        dve.tensor_copy(dm[:, b, :], bD[:, :]).then_inc(q["dm_ready"], 1)
                    if 0 <= t - 2 < GI:
                        i, u = t - 2, g * GI + t - 2
                        dve.wait_ge(q["slots_made"], u + 1)
                        dve.tensor_scalar(slT[:, i, :], bO[:, :], w["gx"], None, ALU.mult).then_inc(q["slT_ready"], 1)
                if more:
                    scale_rows(g + 1)
                for i in range(GI):
                    u, b = g * GI + i, i % 2
                    dve.wait_ge(q["down"], u + 1)
                    dve.tensor_copy(pr[:, b, :], bP[:, :]).then_inc(q["pr_ready"], 1)
                    dve.wait_ge(q["mixed"], u + 1)
                    dve.scalar_tensor_tensor(out=src(i), in0=bO[:, 0:D], scalar=cinv[:, i:i + 1], in1=src(i),
                                             op0=ALU.mult, op1=ALU.add).then_inc(q["added"], 1)

            scale_rows(0)
            with dve.Fori(0, NG - 1) as g:
                group(g, True)
            group(NG - 1, False)


def pack_l3f(a):
    return {"w1": a["L3_ffn_w1"], "gx": a["L3_ffn_gamma_x"], "gs": a["L3_ffn_gamma_slot"],
            "w2": a["L3_ffn_w2"].reshape(HC, P, D).transpose(1, 0, 2),
            "slots": a["L3_ffn_slot_embeds"].reshape(SC, P, D).transpose(1, 0, 2)}

BUILD = {
    "l0x": sublayer_soft_attention,
    "l1x": sublayer_soft_attention,
    "l2x": sublayer_soft_attention,
    "l0g": sublayer_soft_attention,
    "l0a": sublayer_retention,
    "l1a": sublayer_linear,
    "l2a": sublayer_over_sequences,
    "l0f": sublayer_moe,
    "l1f": sublayer_moe,
    "l2f": sublayer_moe,
    "l3a": sublayer_delta,
    "l3x": sublayer_l3_xattn,
    "l3f": sublayer_l3_ffn,
}
PACK_OF = {
    "l0x": pack_l0x,
    "l1x": pack_l1x,
    "l2x": pack_l2x,
    "l0g": pack_l0g,
    "l0a": pack_l0a,
    "l1a": pack_l1a,
    "l2a": pack_l2a,
    "l1f": pack_l1f,
    "l2f": pack_l2f,
    "l0f": pack_l0f,
    "l3a": pack_l3a,
    "l3x": pack_l3x,
    "l3f": pack_l3f,
}
STREAM_OF = {
    "l1a": stream_l1a,
    "l1f": stream_l1f,
    "l2f": stream_l2f,
    "l0f": stream_l0f,
    "l3a": stream_l3a,
}



NAMES = [["l0a"], ["l0x"], ["l0g", "l0f"], ["l1a"], ["l1x"], ["l1f"], ["l2a"], ["l2x"], ["l2f"], ["l3a"], ["l3x"], ["l3f"]]
UNITS = [name for ph in PHASES for name in NAMES[ph]]
ARENA = max(p.cols for p in PACKS.values())


def decoder_kernel(nc, dram, out):
    with ExitStack() as ctx:
        k = Shared(nc, ctx, dram)
        k.selectors = Selectors(nc, ctx)
        for n, name in enumerate(UNITS):
            with ExitStack() as mem:
                s = Scope(k, mem, name)
                if n == 0:
                    open_program(k)
                BUILD[name](k, s, n)
                nums = s.sems
                clear_semaphores(nc, nums)
        close_program(k, out)


def open_program(k):
    nc = k.nc
    with nc.Block() as block:
        @block.sync
        def _(sp):
            sp.dma_start(k.X[:, :, :], k.dram["x"][:, :, :]).then_inc(k.base_loaded, 16)
            sp.dma_start(k.cT[:, :, :], k.dram["cT"][:, :, :]).then_inc(k.base_loaded, 16)
            sp.dma_start(k.ident[:, :], k.dram["ident"][:, :]).then_inc(k.base_loaded, 16)
            sp.dma_start(k.iota[:, :], k.dram["iota"][:, :]).then_inc(k.base_loaded, 16)
            k.load(sp, 0)
            sp.wait_ge(k.base_loaded, BASE_LOADS)

        @block.vector
        def _(dve):
            dve.wait_ge(k.base_loaded, BASE_LOADS)
            k.selectors.build(dve, k.ident)

        @block.gpsimd
        def _(pool):
            pool.memset(k.half[:, :], -0.5)
            pool.memset(k.plus[:, :], 0.5)


def clear_semaphores(nc, sems):
    def clear(eng, part):
        for sem in sems[part::5]:
            eng.sem_clear(sem)

    with nc.Block() as block:
        @block.sync
        def _(sp):
            clear(sp, 0)

        @block.gpsimd
        def _(pool):
            clear(pool, 1)

        @block.tensor
        def _(pe):
            clear(pe, 2)

        @block.scalar
        def _(act):
            clear(act, 3)

        @block.vector
        def _(dve):
            clear(dve, 4)


def close_program(k, out):
    with k.nc.Block() as block, k.nc.semaphore("stored") as stored:
        @block.sync
        def _(sp):
            sp.dma_start(out[:, :, :], k.X[:, :, :]).then_inc(stored, 16)
            sp.wait_ge(stored, 16)



def kernel(**inputs):
    import concourse.bacc as _bacc
    from concourse.bass_utils import run_bass_kernel_spmd as _run

    a = {name: np.asarray(v) for name, v in inputs.items()}
    arrays = {
        "x": np.ascontiguousarray(a["x"].transpose(1, 0, 2)),
        "cT": np.concatenate([a["ctx_768"].transpose(2, 0, 1), np.ones((1, NB, T), np.float32)], 0),
        "iota": np.broadcast_to(np.arange(8, dtype=np.float32)[None], (P, 8)).copy(),
        "ident": np.eye(P, dtype=np.float32),
    }
    for name in UNITS:
        if PACKS[name].cols:
            arrays["w_" + name] = PACKS[name].fill(PACK_OF[name](a))
        if name in STREAM_OF:
            arrays.update(STREAM_OF[name](a))
    nc = _bacc.Bacc("TRN2", target_bir_lowering=False, num_devices=1)
    dram = {name: nc.dram_tensor(f"in_{name}", v.shape, mybir.dt.from_np(v.dtype), kind="ExternalInput").ap()
            for name, v in arrays.items()}
    out = nc.dram_tensor("out", (P, NB, D), F32, kind="ExternalOutput").ap()
    decoder_kernel(nc, dram, out)
    r = _run(nc, [{f"in_{name}": v for name, v in arrays.items()}], core_ids=[0])
    return r.results[0]["out"].transpose(1, 0, 2).copy()
```
